# Optimizing a Trainium2 kernel written in Bass

```python
import numpy as np
import jax
import jax.numpy as jnp

def _softmax(x, axis=-1):
    return jax.nn.softmax(x, axis=axis)

def _gelu(x):
    return jax.nn.gelu(x, approximate=True)

def _silu(x):
    return jax.nn.silu(x)

def _sigmoid(x):
    return jax.nn.sigmoid(x)

def _layernorm(x, axis=-1, eps=1e-05):
    m = jnp.mean(x, axis=axis, keepdims=True)
    v = jnp.var(x, axis=axis, keepdims=True)
    return (x - m) / jnp.sqrt(v + eps)

def _scatter_add(tgt, idx, src, axis=0):
    return tgt.at[idx].add(src)

def _segment_sum(src, seg, n):
    return jax.ops.segment_sum(src, seg, n)
kernel_name = 'mk_gnn_resnorm_d4_gnn_r8_581206'

def setup_inputs(seed: int=0):
    np.random.seed(seed)
    _w = jnp.asarray

    def _rec_inputs():
        import jax
        import jax.numpy as jnp
        _gk = jax.random.key(seed)
        x = -0.0002117 + 1 * jax.random.normal(jax.random.fold_in(_gk, 1), (1250, 512), jnp.float32)
        src = jax.random.randint(jax.random.fold_in(_gk, 2), (40000,), 0, 1250, jnp.int32)
        dst = jnp.minimum((1250 * jax.random.uniform(jax.random.fold_in(_gk, 3), (40000,)) ** 2.0).astype(jnp.int32), 9999)
        _o = jnp.argsort(dst, stable=True)
        src = src[_o]
        dst = dst[_o]
        edge_attr_128 = -5.16925e-05 + 1.00005 * jax.random.normal(jax.random.fold_in(_gk, 11), (40000, 128), jnp.float32)
        edge_weight = jax.random.uniform(jax.random.fold_in(_gk, 13), (40000,), jnp.float32, 0.0, 0.999996)
        return (x, src, dst, edge_attr_128, edge_weight)
    x, src, dst, edge_attr_128, edge_weight = _rec_inputs()

    def _L0_gnn_setup():
        import jax, jax.numpy as jnp
        import numpy as np
        N = 6250
        IN_CH = 512
        OUT_CH = 512
        DEG = 32
        E = N * DEG
        key = jax.random.key(seed)
        kx, kwc, kwn, kb, ke = jax.random.split(key, 5)
        x = jax.random.normal(kx, (N, IN_CH), dtype=jnp.float32)
        bound = 1.0 / np.sqrt(IN_CH)
        wc = jax.random.uniform(kwc, (IN_CH, OUT_CH), minval=-bound, maxval=bound, dtype=jnp.float32)
        wn = jax.random.uniform(kwn, (IN_CH, OUT_CH), minval=-bound, maxval=bound, dtype=jnp.float32)
        bias = jax.random.uniform(kb, (OUT_CH,), minval=-bound, maxval=bound, dtype=jnp.float32)
        src = jnp.repeat(jnp.arange(N, dtype=jnp.int64), DEG)
        dst = jax.random.randint(ke, (E,), 0, N, dtype=jnp.int64)
        edge_index = jnp.stack([src, dst], axis=0)
        return {'x': x, 'wc': wc, 'wn': wn, 'bias': bias, 'edge_index': edge_index}
    _L0_gnn_all = _L0_gnn_setup()
    _L0_gnn_in = {k: v for k, v in _L0_gnn_all.items() if k in ('wc', 'wn', 'bias')}
    del _L0_gnn_all

    def _L1_gnn_setup():
        import jax, jax.numpy as jnp
        import numpy as np
        D = 512
        H = 8
        DH = D // H
        F = 256
        L = 2
        N = 2500
        E = 40000
        EPS = 1e-05

        def _xavier(key, shape):
            fan_out, fan_in = (shape[-2], shape[-1])
            lim = float(np.sqrt(6.0 / (fan_in + fan_out)))
            return jax.random.uniform(key, shape, jnp.float32, -lim, lim)

        def _batchnorm(x, g, b):
            mu = jnp.mean(x, axis=0)
            var = jnp.mean(jnp.square(x - mu), axis=0)
            return (x - mu) * jax.lax.rsqrt(var + EPS) * g + b

        def _layernorm(x, g, b):
            mu = jnp.mean(x, axis=-1, keepdims=True)
            var = jnp.mean(jnp.square(x - mu), axis=-1, keepdims=True)
            return (x - mu) * jax.lax.rsqrt(var + EPS) * g + b
        key = jax.random.key(seed)
        ks = jax.random.split(key, 12)
        src = jax.random.normal(ks[0], (N, D), jnp.float32)
        edge_index = jax.random.randint(ks[1], (2, E), 0, N)
        return {'src': src, 'edge_index': edge_index, 'Wq': _xavier(ks[2], (L, D, D)), 'bq': jnp.zeros((L, D), jnp.float32), 'Wk': _xavier(ks[3], (L, D, D)), 'Wv': _xavier(ks[4], (L, D, D)), 'Wo': _xavier(ks[5], (L, D, D)), 'bo': jnp.zeros((L, D), jnp.float32), 'W1': _xavier(ks[6], (L, F, D)), 'b1': jnp.zeros((L, F), jnp.float32), 'W2': _xavier(ks[7], (L, D, F)), 'b2': jnp.zeros((L, D), jnp.float32), 'g1': jnp.ones((L, D), jnp.float32), 'beta1': jnp.zeros((L, D), jnp.float32), 'g2': jnp.ones((L, D), jnp.float32), 'beta2': jnp.zeros((L, D), jnp.float32), 'ln_g': jnp.ones((D,), jnp.float32), 'ln_b': jnp.zeros((D,), jnp.float32)}
    _L1_gnn_all = _L1_gnn_setup()
    _L1_gnn_in = {k: v for k, v in _L1_gnn_all.items() if k in ('Wq', 'bq', 'Wk', 'Wv', 'Wo', 'bo', 'W1', 'b1', 'W2', 'b2', 'g1', 'beta1', 'g2', 'beta2', 'ln_g', 'ln_b')}
    del _L1_gnn_all

    def _L2_gnn_setup():
        import jax, jax.numpy as jnp
        import numpy as np
        N = 1250
        E = 20000
        D_IN = 512
        D_OUT = 512
        key = jax.random.key(seed)
        k1, k2, k3, k4, k5 = jax.random.split(key, 5)
        x = jax.random.normal(k1, (N, D_IN), dtype=jnp.float32)
        edge_index = jax.random.randint(k2, (2, E), 0, N, dtype=jnp.int64)
        edge_attr = jax.random.uniform(k3, (E,), dtype=jnp.float32)
        W = jax.random.normal(k4, (D_IN, D_OUT), dtype=jnp.float32) * 0.05
        b = jax.random.normal(k5, (D_OUT,), dtype=jnp.float32) * 0.05
        return {'x': x, 'edge_index': edge_index, 'edge_attr': edge_attr, 'W': W, 'b': b}
    _L2_gnn_all = _L2_gnn_setup()
    _L2_gnn_in = {k: v for k, v in _L2_gnn_all.items() if k in ('W', 'b')}
    del _L2_gnn_all

    def _L3_gnn_setup():
        import jax, jax.numpy as jnp
        import numpy as np
        LN_EPS = 1e-05

        def layer_norm(x, g, b):
            m = jnp.mean(x, axis=-1, keepdims=True)
            v = jnp.mean(jnp.square(x - m), axis=-1, keepdims=True)
            return (x - m) * jax.lax.rsqrt(v + LN_EPS) * g + b
        key = jax.random.key(seed)
        ks = jax.random.split(key, 16)
        N, E, D, ED = (6250, 100000, 512, 128)
        s = lambda k, shape, fan: (jax.random.normal(k, shape, jnp.float32) * (1.0 / np.sqrt(fan))).astype(jnp.float32)
        return {'node_feats': jax.random.normal(ks[0], (N, D), jnp.float32), 'edge_index': jax.random.randint(ks[1], (2, E), 0, N, jnp.int64), 'edge_attr': jax.random.normal(ks[2], (E, ED), jnp.float32), 'W_edge': s(ks[3], (ED, D), ED), 'b_edge': jnp.zeros((D,), jnp.float32), 'eps': jnp.zeros((), jnp.float32), 'W1': s(ks[4], (D, 2 * D), D), 'b1': jnp.zeros((2 * D,), jnp.float32), 'g1': jnp.ones((2 * D,), jnp.float32), 'be1': jnp.zeros((2 * D,), jnp.float32), 'W2': s(ks[5], (2 * D, D), 2 * D), 'b2': jnp.zeros((D,), jnp.float32), 'g2': jnp.ones((D,), jnp.float32), 'be2': jnp.zeros((D,), jnp.float32), 'gA': jnp.ones((D,), jnp.float32), 'bA': jnp.zeros((D,), jnp.float32), 'M1': s(ks[6], (D, 2 * D), D), 'M2': s(ks[7], (2 * D, D), 2 * D), 'gB': jnp.ones((D,), jnp.float32), 'bB': jnp.zeros((D,), jnp.float32)}
    _L3_gnn_all = _L3_gnn_setup()
    _L3_gnn_in = {k: v for k, v in _L3_gnn_all.items() if k in ('W_edge', 'b_edge', 'eps', 'W1', 'b1', 'g1', 'be1', 'W2', 'b2', 'g2', 'be2', 'gA', 'bA', 'M1', 'M2', 'gB', 'bB')}
    del _L3_gnn_all
    return {'x': x, 'src': src, 'dst': dst, 'edge_attr_128': edge_attr_128, 'edge_weight': edge_weight, 'L0_gnn_wc': _L0_gnn_in['wc'], 'L0_gnn_wn': _L0_gnn_in['wn'], 'L0_gnn_bias': _L0_gnn_in['bias'], 'L1_gnn_Wq': _L1_gnn_in['Wq'], 'L1_gnn_bq': _L1_gnn_in['bq'], 'L1_gnn_Wk': _L1_gnn_in['Wk'], 'L1_gnn_Wv': _L1_gnn_in['Wv'], 'L1_gnn_Wo': _L1_gnn_in['Wo'], 'L1_gnn_bo': _L1_gnn_in['bo'], 'L1_gnn_W1': _L1_gnn_in['W1'], 'L1_gnn_b1': _L1_gnn_in['b1'], 'L1_gnn_W2': _L1_gnn_in['W2'], 'L1_gnn_b2': _L1_gnn_in['b2'], 'L1_gnn_g1': _L1_gnn_in['g1'], 'L1_gnn_beta1': _L1_gnn_in['beta1'], 'L1_gnn_g2': _L1_gnn_in['g2'], 'L1_gnn_beta2': _L1_gnn_in['beta2'], 'L1_gnn_ln_g': _L1_gnn_in['ln_g'], 'L1_gnn_ln_b': _L1_gnn_in['ln_b'], 'L2_gnn_W': _L2_gnn_in['W'], 'L2_gnn_b': _L2_gnn_in['b'], 'L3_gnn_W_edge': _L3_gnn_in['W_edge'], 'L3_gnn_b_edge': _L3_gnn_in['b_edge'], 'L3_gnn_eps': _L3_gnn_in['eps'], 'L3_gnn_W1': _L3_gnn_in['W1'], 'L3_gnn_b1': _L3_gnn_in['b1'], 'L3_gnn_g1': _L3_gnn_in['g1'], 'L3_gnn_be1': _L3_gnn_in['be1'], 'L3_gnn_W2': _L3_gnn_in['W2'], 'L3_gnn_b2': _L3_gnn_in['b2'], 'L3_gnn_g2': _L3_gnn_in['g2'], 'L3_gnn_be2': _L3_gnn_in['be2'], 'L3_gnn_gA': _L3_gnn_in['gA'], 'L3_gnn_bA': _L3_gnn_in['bA'], 'L3_gnn_M1': _L3_gnn_in['M1'], 'L3_gnn_M2': _L3_gnn_in['M2'], 'L3_gnn_gB': _L3_gnn_in['gB'], 'L3_gnn_bB': _L3_gnn_in['bB']}

def reference(x, src, dst, edge_attr_128, edge_weight, L0_gnn_wc, L0_gnn_wn, L0_gnn_bias, L1_gnn_Wq, L1_gnn_bq, L1_gnn_Wk, L1_gnn_Wv, L1_gnn_Wo, L1_gnn_bo, L1_gnn_W1, L1_gnn_b1, L1_gnn_W2, L1_gnn_b2, L1_gnn_g1, L1_gnn_beta1, L1_gnn_g2, L1_gnn_beta2, L1_gnn_ln_g, L1_gnn_ln_b, L2_gnn_W, L2_gnn_b, L3_gnn_W_edge, L3_gnn_b_edge, L3_gnn_eps, L3_gnn_W1, L3_gnn_b1, L3_gnn_g1, L3_gnn_be1, L3_gnn_W2, L3_gnn_b2, L3_gnn_g2, L3_gnn_be2, L3_gnn_gA, L3_gnn_bA, L3_gnn_M1, L3_gnn_M2, L3_gnn_gB, L3_gnn_bB):
    import jax
    import jax.numpy as jnp

    def _L0_gnn_ref(x, wc, wn, bias, edge_index):
        import jax, jax.numpy as jnp
        import numpy as np
        N = 6250
        IN_CH = 512
        OUT_CH = 512
        DEG = 32
        E = N * DEG
        alpha = x @ wc
        beta = x @ wn
        src, dst = (edge_index[0], edge_index[1])
        sums = jax.ops.segment_sum(beta[dst], src, num_segments=x.shape[0])
        counts = jax.ops.segment_sum(jnp.ones_like(src, dtype=beta.dtype), src, num_segments=x.shape[0])
        gamma = sums / counts[:, None]
        return alpha + gamma + bias

    def _L1_gnn_ref(src, edge_index, Wq, bq, Wk, Wv, Wo, bo, W1, b1, W2, b2, g1, beta1, g2, beta2, ln_g, ln_b):
        import jax, jax.numpy as jnp
        import numpy as np
        D = 512
        H = 8
        DH = D // H
        F = 256
        L = 2
        N = 2500
        E = 40000
        EPS = 1e-05

        def _xavier(key, shape):
            fan_out, fan_in = (shape[-2], shape[-1])
            lim = float(np.sqrt(6.0 / (fan_in + fan_out)))
            return jax.random.uniform(key, shape, jnp.float32, -lim, lim)

        def _batchnorm(x, g, b):
            mu = jnp.mean(x, axis=0)
            var = jnp.mean(jnp.square(x - mu), axis=0)
            return (x - mu) * jax.lax.rsqrt(var + EPS) * g + b

        def _layernorm(x, g, b):
            mu = jnp.mean(x, axis=-1, keepdims=True)
            var = jnp.mean(jnp.square(x - mu), axis=-1, keepdims=True)
            return (x - mu) * jax.lax.rsqrt(var + EPS) * g + b
        n = src.shape[0]
        scaling = float(DH) ** (-0.5)
        tgt = edge_index[1]
        srcidx = edge_index[0]
        x = src
        for l in range(L):
            q = ((x @ Wq[l].T + bq[l]) * scaling).reshape(n, H, DH)
            k = (x @ Wk[l].T).reshape(n, H, DH)
            v = (x @ Wv[l].T).reshape(n, H, DH)
            scores = jnp.einsum('ehd,ehd->eh', q[tgt], k[srcidx])
            m = jax.ops.segment_max(scores, tgt, num_segments=n)
            p = jnp.exp(scores - m[tgt])
            s = jax.ops.segment_sum(p, tgt, num_segments=n)
            w = p / (s[tgt] + 1e-16)
            agg = jax.ops.segment_sum(w[:, :, None] * v[srcidx], tgt, num_segments=n)
            attn = agg.reshape(n, D) @ Wo[l].T + bo[l]
            x = _batchnorm(x + attn, g1[l], beta1[l])
            ff = jax.nn.relu(x @ W1[l].T + b1[l]) @ W2[l].T + b2[l]
            x = _batchnorm(x + ff, g2[l], beta2[l])
        return _layernorm(x, ln_g, ln_b)

    def _L2_gnn_ref(x, edge_index, edge_attr, W, b):
        import jax, jax.numpy as jnp
        import numpy as np
        N = 1250
        E = 20000
        D_IN = 512
        D_OUT = 512
        n = x.shape[0]
        row, col = (edge_index[0], edge_index[1])
        loop = jnp.arange(n, dtype=edge_index.dtype)
        row_f = jnp.concatenate([row, loop])
        col_f = jnp.concatenate([col, loop])
        ew = jnp.concatenate([edge_attr, jnp.ones((n,), dtype=edge_attr.dtype)])
        deg = jax.ops.segment_sum(ew, col_f, num_segments=n)
        dinv = jnp.where(deg > 0, jax.lax.rsqrt(deg), 0.0)
        norm = dinv[row_f] * ew * dinv[col_f]
        h = x @ W
        msg = h[row_f] * norm[:, None]
        out = jax.ops.segment_sum(msg, col_f, num_segments=n)
        return out + b

    def _L3_gnn_ref(node_feats, edge_index, edge_attr, W_edge, b_edge, eps, W1, b1, g1, be1, W2, b2, g2, be2, gA, bA, M1, M2, gB, bB):
        import jax, jax.numpy as jnp
        import numpy as np
        LN_EPS = 1e-05

        def layer_norm(x, g, b):
            m = jnp.mean(x, axis=-1, keepdims=True)
            v = jnp.mean(jnp.square(x - m), axis=-1, keepdims=True)
            return (x - m) * jax.lax.rsqrt(v + LN_EPS) * g + b
        N = node_feats.shape[0]
        src, dst = (edge_index[0], edge_index[1])
        edge_emb = edge_attr @ W_edge + b_edge
        msg = jax.nn.relu(node_feats[src] + edge_emb)
        aggr = jax.ops.segment_sum(msg, dst, num_segments=N)
        h = (1.0 + eps) * node_feats + aggr
        h = jax.nn.gelu(layer_norm(h @ W1 + b1, g1, be1), approximate=False)
        h = jax.nn.gelu(layer_norm(h @ W2 + b2, g2, be2), approximate=False)
        h = layer_norm(node_feats + h, gA, bA)
        m = jax.nn.gelu(h @ M1, approximate=False) @ M2
        return layer_norm(h + m, gB, bB)
    edge_index = jnp.stack([src, dst])
    x = _layernorm(x + _L0_gnn_ref(x, L0_gnn_wc, L0_gnn_wn, L0_gnn_bias, edge_index), axis=-1)
    x = _layernorm(x + _L1_gnn_ref(x, edge_index, L1_gnn_Wq, L1_gnn_bq, L1_gnn_Wk, L1_gnn_Wv, L1_gnn_Wo, L1_gnn_bo, L1_gnn_W1, L1_gnn_b1, L1_gnn_W2, L1_gnn_b2, L1_gnn_g1, L1_gnn_beta1, L1_gnn_g2, L1_gnn_beta2, L1_gnn_ln_g, L1_gnn_ln_b), axis=-1)
    x = _layernorm(x + _L2_gnn_ref(x, edge_index, edge_weight, L2_gnn_W, L2_gnn_b), axis=-1)
    x = _layernorm(x + _L3_gnn_ref(x, edge_index, edge_attr_128, L3_gnn_W_edge, L3_gnn_b_edge, L3_gnn_eps, L3_gnn_W1, L3_gnn_b1, L3_gnn_g1, L3_gnn_be1, L3_gnn_W2, L3_gnn_b2, L3_gnn_g2, L3_gnn_be2, L3_gnn_gA, L3_gnn_bA, L3_gnn_M1, L3_gnn_M2, L3_gnn_gB, L3_gnn_bB), axis=-1)
    return x

_drawn_inputs = setup_inputs


def setup_inputs(seed=0):
    import zlib

    import numpy as np

    out = dict(_drawn_inputs(seed))
    spreads = {'L1_gnn_bq': (0.0, 0.344),
     'L1_gnn_bo': (0.0, 2.0),
     'L1_gnn_b1': (0.0, 0.276),
     'L1_gnn_b2': (0.0, 2.0),
     'L1_gnn_g1': (1.0, 0.2),
     'L1_gnn_beta1': (0.0, 0.1),
     'L1_gnn_g2': (1.0, 0.2),
     'L1_gnn_beta2': (0.0, 0.1),
     'L1_gnn_ln_g': (1.0, 0.2),
     'L1_gnn_ln_b': (0.0, 0.1),
     'L3_gnn_b_edge': (0.0, 0.275),
     'L3_gnn_b1': (0.0, 2.0),
     'L3_gnn_g1': (1.0, 0.2),
     'L3_gnn_be1': (0.0, 0.1),
     'L3_gnn_b2': (0.0, 0.1),
     'L3_gnn_g2': (1.0, 0.2),
     'L3_gnn_be2': (0.0, 0.1),
     'L3_gnn_gA': (1.0, 0.2),
     'L3_gnn_bA': (0.0, 0.1),
     'L3_gnn_gB': (1.0, 0.2),
     'L3_gnn_bB': (0.0, 0.1)}
    factors = {'L0_gnn_bias': 3.191}
    for name, (base, spread) in spreads.items():
        noise = np.random.default_rng([zlib.crc32(name.encode()), seed]).standard_normal(out[name].shape)
        drawn = base * np.exp(spread * noise) if base else spread * noise
        out[name] = jnp.asarray(drawn.astype(out[name].dtype))
    for name, factor in factors.items():
        out[name] = (out[name] * factor).astype(out[name].dtype)
    return out
```

```python
import concourse.bass as bass
from concourse import mybir

F32 = mybir.dt.float32
F16 = mybir.dt.float16
BF16 = mybir.dt.bfloat16
I32 = mybir.dt.int32
U32 = mybir.dt.uint32
U16 = mybir.dt.uint16
ALU = mybir.AluOpType
ACT = mybir.ActivationFunctionType
AX = mybir.AxisListType.X

P = 128
N = 1250
D = 512
E = 40000
NB = -(-N // P)
NP = NB * P
KC = D // P
EC = 320
EP = E // EC
assert EP * EC == E and EP <= P
GT = 4
GE = GT * P
REC = 4
C3 = 417
C4 = 313
W3 = 3 * C3
NK3 = 3 * NB
NG = -(-(E // GE + NB) // 2) * 2
NG3 = -(-(E // GE + NK3) // 2) * 2
NT, NT3 = NG * GT, NG3 * GT
W4 = 4 * C4
HALF = NP // 2
H = 8
DH = D // H
HP = H // 2
FF = 256
LAYERS = 2
ED = 128
D2 = 2 * D
EPS = 1e-5
ARENA, ARENA_END = 16512, 229344
NEVER = -2.0 ** 100


class Steps:

    def __init__(self, nc, eng, sem):
        self.sem, self.eng, self.n = nc.alloc_semaphore(sem) if isinstance(sem, str) else sem, eng, 0

    def mark(self, ins):
        ins.then_inc(self.sem, 1)
        self.n += 1
        return self.n

    def then(self, ins):
        self.eng.wait_ge(self.sem, self.mark(ins))


class Region:

    def __init__(self, nc, start, end):
        self.nc, self.at, self.end = nc, start, end

    def take(self, name, shape, dt):
        size = {F32: 4, I32: 4, U32: 4, F16: 2, BF16: 2, U16: 2}[dt]
        for n in shape[1:]:
            size *= n
        t = self.nc.alloc_sbuf_tensor_at(name, shape, dt, offset=self.at)
        self.at += -(-size // 32) * 32
        assert self.at <= self.end, (name, self.at, self.end)
        return t


class Norm:

    PIECES = 3

    def __init__(self, nc, r, name, n):
        self.n = n
        self.pieces = r.take(name + "_pieces", [P, n, self.PIECES, 6], F32)
        self.mean_var = r.take(name + "_mean_var", [P, n, 2], F32)
        self.var, self.dev = r.take(name + "_var", [P, n], F32), r.take(name + "_dev", [P, n], F32)

    def stats(self, dve, me, b, *rows):
        for j, piece in enumerate(rows):
            me.mark(dve.bn_stats(self.pieces[:, b, j, :], piece))
        dve.wait_ge(me.sem, me.n)
        me.mark(dve.bn_aggr(self.mean_var[:, b, :], self.pieces[:, b, 0:len(rows), :]))

    def variance(self, dve, me, ready):
        dve.wait_ge(me.sem, me.n)
        dve.tensor_scalar(self.var[:], self.mean_var[:, :, 1], EPS, None, ALU.add).then_inc(ready, 1)

    def invert(self, dve, me):
        me.then(dve.reciprocal(self.dev[:], self.dev[:]))

    def affine(self, dve, me, b, rows, gain, shift):
        me.then(dve.scalar_tensor_tensor(rows, rows, self.mean_var[:, b, 0:1], gain, ALU.subtract, ALU.mult))
        return dve.scalar_tensor_tensor(rows, rows, self.dev[:, b:b + 1], shift, ALU.mult, ALU.add)

    def apply(self, dve, b, rows):
        return dve.tensor_scalar(rows, rows, self.mean_var[:, b, 0:1], self.dev[:, b:b + 1], ALU.subtract, ALU.mult)


def gate(eng, sem, value, passed):
    eng.wait_ge(sem, value)
    eng.sem_inc(passed, 1)


def last_rows(b):
    return min(P, N - b * P)


def row_of(vector):
    return vector.rearrange("(o n) -> o n", o=1).to_broadcast([P, vector.shape[0]])


def constants(nc, k):
    made = nc.alloc_semaphore("const_made")
    with nc.Block() as block:
        @block.gpsimd
        def _(pool):
            pool.memset(k.ident[:], 0.0).then_inc(made, 1)
            pool.memset(k.before[:], 1.0).then_inc(made, 1)
            pool.memset(k.ones[:], 1.0).then_inc(made, 1)
            pool.wait_ge(made, 3)
            pool.affine_select(out=k.ident[:], in_=k.ident[:], compare_op=ALU.not_equal, fill=1.0,
                               base=0, pattern=[[-1, P]], channel_multiplier=1).then_inc(made, 1)
            pool.affine_select(out=k.before[:], in_=k.before[:], compare_op=ALU.is_gt, fill=0.0,
                               base=0, pattern=[[1, P]], channel_multiplier=-1).then_inc(made, 1)
            pool.iota(k.node_row[:], pattern=[[1, NP]], base=0, channel_multiplier=0,
                      allow_small_or_imprecise_dtypes=True).then_inc(made, 1)
            pool.iota(k.row128[:], pattern=[[1, P]], base=0, channel_multiplier=0,
                      allow_small_or_imprecise_dtypes=True).then_inc(made, 1)
            pool.iota(k.row128f[:], pattern=[[1, P]], base=0, channel_multiplier=0,
                      allow_small_or_imprecise_dtypes=True).then_inc(made, 1)
            pool.iota(k.groups_row[:], pattern=[[1, NG3]], base=0, channel_multiplier=0,
                      allow_small_or_imprecise_dtypes=True).then_inc(made, 1)
            pool.iota(k.pad_rows[:], pattern=[[0, 1]], base=0, channel_multiplier=1,
                      allow_small_or_imprecise_dtypes=True).then_inc(made, 1)
            pool.memset(k.sel[:], 1.0).then_inc(made, 1)
            pool.wait_ge(made, 11)
            pool.tensor_copy(k.ident16[:], k.ident[:]).then_inc(made, 1)
            pool.tensor_scalar(k.pad_rows[:], k.pad_rows[:], float(last_rows(NB - 1)), 1.0, ALU.is_ge, ALU.mult).then_inc(made, 1)
            pool.affine_select(out=k.sel[:], in_=k.sel[:], compare_op=ALU.is_ge, fill=0.0,
                               base=0, pattern=[[-3, H], [0, P]], channel_multiplier=1).then_inc(made, 1)
            pool.wait_ge(made, 14)
            pool.affine_select(out=k.sel[:], in_=k.sel[:], compare_op=ALU.is_ge, fill=0.0,
                               base=2, pattern=[[3, H], [0, P]], channel_multiplier=-1).then_inc(made, 1)
            pool.wait_ge(made, 15)


def scatter_edges(pool, S, name, edge_pos, rec, stage, slots_dram, slots, scattered, prefilled):
    st_pos, st_rec = stage
    staged, passed = S(name + "_staged"), S(name + "_passed")
    pool.wait_ge(prefilled, 16)
    with pool.Fori(0, EC // 16) as i:
        for u in range(2):
            pool.tensor_copy(st_pos[:, u, :], edge_pos[:, bass.ds(i * 16 + 8 * u, 8)]).then_inc(staged, 1)
            pool.tensor_copy(st_rec[:, u, :], rec[:].rearrange("p c w -> p (c w)")[:, bass.ds(i * 64 + 32 * u, 32)]).then_inc(staged, 1)
            gate(pool, staged, i * 4 + 2 * u + 2, passed)
            for c in range(8):
                pool.indirect_dma_start(
                    out=slots_dram, out_offset=bass.IndirectOffsetOnAxis(ap=st_pos[:, u, c:c + 1], axis=0),
                    in_=st_rec[:, u, REC * c:REC * (c + 1)], in_offset=None,
                    bounds_check=slots - 1, oob_is_err=False).then_inc(scattered, 16)
        gate(pool, scattered, i * 256 + 256, passed)


def sort_edges(nc, k, a):
    S = nc.alloc_semaphore
    cleared, loaded, prefilled = S("edges_cleared"), S("edges_loaded"), S("slots_prefilled")
    pads_made, totals_ready, offsets_ready, pos_ready = S("pads_made"), S("totals_ready"), S("offsets_ready"), S("pos_ready")
    scattered, read_back = S("scattered3"), S("read_back3")
    x_loaded, w_loaded, x_transposed, xt_copied = S("x_loaded"), S("w0_loaded"), S("x_transposed"), S("xt_copied")
    dense_done, dense_copied, id_made = S("dense0_done"), S("beta_copied"), S("id_made")
    alpha_done, bias_loaded = S("alpha_done"), S("bias0_loaded")
    r = Region(nc, k.beta_end, ARENA_END)
    xt = r.take("xt_in", [P, KC, NP], F32)
    src_i, dst_i = r.take("src_i", [P, EC], I32), r.take("dst_i", [P, EC], I32)
    bidx, dloc = r.take("bidx", [P, EC], I32), r.take("dloc", [P, EC], I32)
    ew_s, bidx_f = r.take("ew_s", [P, EC], F32), r.take("bidx_f", [P, EC], F32)
    third, bucket3 = r.take("third", [P, EC], F32), r.take("bucket3", [P, EC], F32)
    is_in, one_row = r.take("is_in", [P, NK3, EC], BF16), r.take("one_row", [P, EC], BF16)
    prefix = r.take("prefix", [P, NK3, EC], F32)
    small, small_i = r.take("small", [P, 6, NK3], F32), r.take("small_i", [P, 2, NK3], I32)
    lin, lin_i = r.take("lin", [P, 4, EC], F32), r.take("lin_i", [P, 3, EC], I32)
    pos3 = r.take("pos3", [P, EC], U32)
    stage = r.take("st_pos3", [P, 2, 8], U32), r.take("st_rec3", [P, 2, 8 * REC], F32)
    pads = r.take("pads", [P, NT3, REC], F32)
    slots = r.take("slots3", [P, NT3, REC], F32)
    slot_wb = r.take("slot_wb", [P, NT3], BF16)
    key_f, key_i = r.take("key_f", [P, 3, NG3], F32), r.take("key_i", [P, 2, NG3], I32)
    wc = r.take("wc", [P, KC, D], F32)
    wn = r.take("wn", [P, KC, D], F32)
    bias = r.take("bias0", [P, D], F32)
    ps_off, ps_tot, ps_d = k.bank[:, 4, :], k.bank[:, 5, :], k.bank
    with nc.Block() as block:
        T, OFF, TOT, GRP, GS, M = range(6)

        @block.sync
        def _(sp):
            sp.wait_ge(cleared, 4)
            sp.dma_start(dst_i[0:EP, :], a.dst.rearrange("(p c) -> p c", c=EC)).then_inc(loaded, 16)
            sp.dma_start(src_i[0:EP, :], a.src.rearrange("(p c) -> p c", c=EC)).then_inc(loaded, 16)
            sp.dma_start(ew_s[0:EP, :], a.edge_weight.rearrange("(p c) -> p c", c=EC)).then_inc(loaded, 16)
            whole = (N // P) * P
            sp.dma_start(k.alpha[:, 0:N // P, :], a.x[0:whole, :].rearrange("(b p) f -> p b f", p=P)).then_inc(x_loaded, 16)
            sp.dma_start(k.alpha[0:N - whole, N // P, :], a.x[whole:N, :]).then_inc(x_loaded, 16)
            sp.dma_start(wc[:], a.L0_gnn_wc.rearrange("(c p) n -> p c n", p=P)).then_inc(w_loaded, 16)
            sp.dma_start(wn[:], a.L0_gnn_wn.rearrange("(c p) n -> p c n", p=P)).then_inc(w_loaded, 16)
            sp.dma_start(bias[:], row_of(a.L0_gnn_bias)).then_inc(bias_loaded, 16)
            sp.wait_ge(pads_made, 1)
            sp.dma_start(k.slots3_dram.rearrange("(p t) w -> p (t w)", p=P),
                         pads[:].rearrange("p t w -> p (t w)")).then_inc(prefilled, 16)
            sp.dma_start(k.slots_dram.rearrange("(p t) w -> p (t w)", p=P),
                         pads[:, 0:NT, :].rearrange("p t w -> p (t w)")).then_inc(k.prefilled1, 16)
            sp.wait_ge(scattered, 16 * EC)
            sp.dma_start(slots[:].rearrange("p t w -> p (t w)"),
                         k.slots3_dram.rearrange("(p t) w -> p (t w)", p=P)).then_inc(read_back, 16)
            sp.wait_ge(read_back, 16)
            sp.wait_ge(k.prefilled1, 16)

        @block.gpsimd
        def _(pool):
            pool.iota(k.rec[:, :, 3], pattern=[[1, EC]], base=0, channel_multiplier=EC,
                      allow_small_or_imprecise_dtypes=True).then_inc(id_made, 1)
            pool.wait_ge(id_made, 1)
            pool.wait_ge(pos_ready, 1)
            scatter_edges(pool, S, "scatter3", pos3, k.rec, stage, k.slots3_dram, P * NT3, scattered, prefilled)

        @block.vector
        def _(dve):
            me = Steps(nc, dve, "sort_dve")

            def place(bucket, nk, tiles, turn, to):
                def row(j):
                    return small[:, j, 0:nk]

                for b in range(nk):
                    me.mark(dve.tensor_scalar(is_in[:, b, :], bucket[:], float(b), None, ALU.is_equal))
                dve.wait_ge(me.sem, me.n)
                counts = prefix[:, 0:nk, :]
                for b in range(nk):
                    me.mark(dve.tensor_tensor_scan(counts[:, b, :], one_row[:], is_in[:, b, :], 0.0, ALU.mult, ALU.add))
                dve.wait_ge(me.sem, me.n)
                dve.tensor_copy(row(T), counts[:, :, EC - 1]).then_inc(totals_ready, 1)
                dve.wait_ge(offsets_ready, 2 * turn)
                me.mark(dve.tensor_copy(row(OFF), ps_off[:, 0:nk]))
                me.then(dve.tensor_scalar(row(TOT), ps_tot[:, 0:nk], float(GE - 1), None, ALU.add))
                me.then(dve.tensor_copy(small_i[:, 0, 0:nk], row(TOT)))
                me.then(dve.tensor_scalar(small_i[:, 1, 0:nk], small_i[:, 0, 0:nk], GE.bit_length() - 1, None, ALU.arith_shift_right))
                me.then(dve.tensor_copy(row(GRP), small_i[:, 1, 0:nk]))
                me.then(dve.tensor_tensor_scan(row(GS), k.ones[:, 0:nk], row(GRP), 0.0, ALU.mult, ALU.add))
                me.then(dve.tensor_tensor(row(GS), row(GS), row(GRP), ALU.subtract))
                me.then(dve.tensor_scalar(row(M), row(GS), float(GE), -1.0, ALU.mult, ALU.add))
                me.then(dve.tensor_tensor(row(M), row(M), row(OFF), ALU.add))
                me.then(dve.tensor_tensor(counts, counts, row(M).unsqueeze(2).to_broadcast([P, nk, EC]), ALU.add))
                me.then(dve.tensor_tensor(counts, counts, is_in[:, 0:nk, :], ALU.mult))
                me.then(dve.tensor_reduce(lin[:, 0, :], counts.rearrange("p b c -> p c b"), axis=AX, op=ALU.add))
                me.then(dve.tensor_copy(lin_i[:, 0, :], lin[:, 0, :]))
                me.mark(dve.tensor_scalar(lin_i[:, 1, :], lin_i[:, 0, :], P - 1, None, ALU.bitwise_and))
                me.then(dve.tensor_scalar(lin_i[:, 2, :], lin_i[:, 0, :], 7, None, ALU.arith_shift_right))
                me.mark(dve.tensor_copy(lin[:, 1, :], lin_i[:, 1, :]))
                me.then(dve.tensor_copy(lin[:, 2, :], lin_i[:, 2, :]))
                me.mark(dve.scalar_tensor_tensor(lin[:, 3, :], lin[:, 1, :], float(tiles), lin[:, 2, :], ALU.mult, ALU.add))
                me.then(dve.tensor_scalar(lin[:, 0, :], bidx_f[:], float(NB), float(16 * P * NT3), ALU.is_ge, ALU.mult))
                me.then(dve.tensor_tensor(lin[:, 3, :], lin[:, 3, :], lin[:, 0, :], ALU.add))
                return dve.tensor_copy(to[:], lin[:, 3, :])

            dve.memset(dst_i[:], NP).then_inc(cleared, 1)
            dve.memset(src_i[:], 0).then_inc(cleared, 1)
            dve.memset(ew_s[:], 0.0).then_inc(cleared, 1)
            dve.memset(k.alpha[:, NB - 1, :], 0.0).then_inc(cleared, 1)
            me.then(dve.memset(pads[:], 0.0))
            dve.memset(pads[:, :, 1], -1.0).then_inc(pads_made, 1)
            me.mark(dve.memset(one_row[:], 1.0))
            dve.wait_ge(loaded, 48)
            me.mark(dve.tensor_scalar(bidx[:], dst_i[:], 7, None, ALU.arith_shift_right))
            me.mark(dve.tensor_scalar(dloc[:], dst_i[:], P - 1, None, ALU.bitwise_and))
            me.mark(dve.tensor_copy(k.rec[:, :, 0], src_i[:]))
            me.then(dve.tensor_copy(k.rec[:, :, 2], ew_s[:]))
            me.mark(dve.tensor_copy(k.rec[:, :, 1], dloc[:]))
            me.mark(dve.tensor_copy(bidx_f[:], bidx[:]))
            me.then(dve.tensor_scalar(third[:], k.rec[:, :, 0], float(C3), None, ALU.is_ge))
            me.then(dve.scalar_tensor_tensor(third[:], k.rec[:, :, 0], float(2 * C3), third[:], ALU.is_ge, ALU.add))
            me.then(dve.scalar_tensor_tensor(bucket3[:], bidx_f[:], 3.0, third[:], ALU.mult, ALU.add))
            place(bucket3, NK3, NT3, 1, pos3).then_inc(pos_ready, 1)
            key, div, col = key_f[:, 0, :], key_f[:, 1, :], key_f[:, 2, :]
            me.then(dve.tensor_scalar(key, k.groups_row[:], small[:, GS, 1:2], None, ALU.is_ge))
            for b in range(2, NK3):
                me.then(dve.scalar_tensor_tensor(key, k.groups_row[:], small[:, GS, b:b + 1], key, ALU.is_ge, ALU.add))
            me.then(dve.tensor_scalar(div, key, 171.0, None, ALU.mult))
            me.then(dve.tensor_copy(key_i[:, 0, :], div))
            me.then(dve.tensor_scalar(key_i[:, 1, :], key_i[:, 0, :], 9, None, ALU.arith_shift_right))
            me.then(dve.tensor_copy(div, key_i[:, 1, :]))
            me.then(dve.scalar_tensor_tensor(col, div, -3.0, key, ALU.mult, ALU.add))
            me.then(dve.tensor_scalar(col, col, float(C3), None, ALU.mult))
            me.then(dve.scalar_tensor_tensor(key, div, float(NP), col, ALU.mult, ALU.add))
            me.then(dve.tensor_copy(k.place3[:], key[0:1, :]))
            dve.wait_ge(bias_loaded, 16)
            for b in range(NB):
                dve.wait_ge(dense_done, 2 * b + 1)
                me.then(dve.tensor_tensor(k.alpha[:, b, :], ps_d[:, 2 * b % 4, :], k.alpha[:, b, :], ALU.add))
                dve.tensor_tensor(k.alpha[:, b, :], k.alpha[:, b, :], bias[:], ALU.add).then_inc(alpha_done, 1)
            me.then(place(bidx_f, NB, NT, 2, k.pos))
            me.then(dve.tensor_scalar(k.blk_f[:], k.groups_row[0:1, 0:NG], small[0:1, GS, 1:2], None, ALU.is_ge))
            for b in range(2, NB):
                me.then(dve.scalar_tensor_tensor(k.blk_f[:], k.groups_row[0:1, 0:NG], small[0:1, GS, b:b + 1], k.blk_f[:], ALU.is_ge, ALU.add))
            me.then(dve.tensor_copy(k.blk[:], k.blk_f[:]))
            dve.wait_ge(read_back, 16)
            me.mark(dve.tensor_copy(k.slot3_dst[:], slots[:, :, 1]))
            me.mark(dve.tensor_tensor(k.slot3_src[:].rearrange("p (g j) -> p g j", j=GT), slots[:, :, 0].rearrange("p (g j) -> p g j", j=GT),
                                      col.unsqueeze(2).to_broadcast([P, NG3, GT]), ALU.subtract))
            ew = slots[:, :, 2]
            me.then(dve.tensor_copy(slot_wb[:], ew))
            me.then(dve.tensor_copy(k.slot_w[:, 0, :], slot_wb[:]))
            me.then(dve.tensor_tensor(k.slot_w[:, 1, :], ew, k.slot_w[:, 0, :], ALU.subtract))
            me.then(dve.tensor_copy(slot_wb[:], k.slot_w[:, 1, :]))
            me.then(dve.tensor_copy(k.slot_w[:, 3, :], slot_wb[:]))
            me.then(dve.tensor_tensor(k.slot_w[:, 2, :], k.slot_w[:, 1, :], k.slot_w[:, 3, :], ALU.subtract))
            me.then(dve.tensor_copy(k.slot_w[:, 1, :], k.slot_w[:, 3, :]))

        @block.tensor
        def _(pe):
            def offsets(turn, nk):
                pe.wait_ge(totals_ready, turn)
                pe.matmul(ps_off[:, 0:nk], k.before[:], small[:, T, 0:nk], start=True, stop=True).then_inc(offsets_ready, 1)
                pe.matmul(ps_tot[:, 0:nk], k.ones[:, 0:P], small[:, T, 0:nk], start=True, stop=True).then_inc(offsets_ready, 1)

            pe.wait_ge(x_loaded, 32)
            for b in range(NB):
                if b >= 4:
                    pe.wait_ge(xt_copied, b - 3)
                for c in range(KC):
                    t = pe.transpose(ps_d[:, b % 4, c * P:(c + 1) * P], k.alpha[:, b, c * P:(c + 1) * P], k.ident[:])
                t.then_inc(x_transposed, 1)
            offsets(1, NK3)
            pe.wait_ge(w_loaded, 32)
            pe.wait_ge(xt_copied, NB)
            for n in range(2 * NB):
                b, w = n // 2, (wc, wn)[n % 2]
                if n >= 4:
                    pe.wait_ge((alpha_done, dense_copied)[n % 2], (n - 4) // 2 + 1)
                for c in range(KC):
                    m = pe.matmul(ps_d[:, n % 4, :], xt[:, c, b * P:(b + 1) * P], w[:, c, :], start=(c == 0), stop=(c == KC - 1))
                m.then_inc(dense_done, 1)
            offsets(2, NB)

        @block.scalar
        def _(act):
            for b in range(NB):
                act.wait_ge(x_transposed, b + 1)
                act.copy(xt[:, :, b * P:(b + 1) * P], ps_d[:, b % 4, :].rearrange("p (c n) -> p c n", c=KC)).then_inc(xt_copied, 1)
            for b in range(NB):
                act.wait_ge(dense_done, 2 * b + 2)
                act.copy(k.beta[:, b, :], ps_d[:, (2 * b + 1) % 4, :]).then_inc(dense_copied, 1)


def edge_matrices(nc, k):
    S = nc.alloc_semaphore
    acc_cleared, hots_built, chunk_done, added = S("acc_cleared"), S("hots_built"), S("chunk_done"), S("chunk_added")
    weighted, scattered = S("hots_weighted"), S("scattered1")
    slots_back, passed = S("slots_back"), S("slots_passed")
    r = Region(nc, k.acc_end, ARENA_END)
    hot_src = r.take("hot_src", [P, 2, GT, C3 + 1], BF16)
    hot_dst = r.take("hot_dst", [P, 2, GT, 4, P], BF16)
    stage = r.take("st_pos", [P, 2, 8], U32), r.take("st_rec", [P, 2, 8 * REC], F32)
    slots = r.take("slots1", [P, NT, REC], F32)
    acc_c, acc_a = (m[:].rearrange("p b n -> p (b n)") for m in (k.acc_c, k.acc_a))
    with nc.Block() as block:
        @block.gpsimd
        def _(pool):
            pool.memset(acc_a, 0.0).then_inc(acc_cleared, 1)
            scatter_edges(pool, S, "scatter1", k.pos, k.rec, stage, k.slots_dram, P * NT, scattered, k.prefilled1)

        @block.sync
        def _(sp):
            sp.wait_ge(scattered, 16 * EC)
            sp.dma_start(slots[:].rearrange("p t w -> p (t w)"), k.slots_dram.rearrange("(p t) w -> p (t w)", p=P)).then_inc(slots_back, 16)
            sp.wait_ge(slots_back, 16)

        @block.vector
        def _(dve):
            def build(g, u):
                for j in range(GT):
                    t = g * GT + j
                    dve.tensor_scalar(hot_dst[:, u, j, 0, :], k.row128[:], k.slot3_dst[:, bass.ds(t, 1)], None, ALU.is_equal).then_inc(hots_built, 1)
                for j in range(GT):
                    t = g * GT + j
                    at = k.slot3_dst[:, bass.ds(t, 1)]
                    dve.tensor_scalar(hot_dst[:, u, j, 1, :], k.row128[:], at, k.slot_w[:, 0, bass.ds(t, 1)], ALU.is_equal, ALU.mult)
                    last = dve.tensor_scalar(hot_src[:, u, j, 0:C3], k.node_row[:, 0:C3], k.slot3_src[:, bass.ds(t, 1)], None, ALU.is_equal)
                last.then_inc(hots_built, 1)

            def add(g, u):
                to = dve.value_load(k.place3[0:1, bass.ds(g, 1)], min_val=0, max_val=(NB - 1) * NP + 2 * C3)
                dve.wait_ge(added, g * 2 + 4)
                for c, acc in enumerate((acc_c, acc_a)):
                    dve.wait_ge(chunk_done, g * 2 + c + 5)
                    rows = acc[:, bass.ds(to, C3)]
                    dve.tensor_tensor(rows, k.bank[:, 2 * u + c, 0:C3], rows, ALU.add).then_inc(added, 1)

            dve.memset(acc_c, 0.0).then_inc(added, 4)
            dve.wait_ge(acc_cleared, 1)
            build(0, 0)
            with dve.Fori(0, NG3 // 2 - 1) as i:
                for u in range(2):
                    build(i * 2 + u + 1, 1 - u)
                    add(i * 2 + u, u)
            build(NG3 - 1, 1)
            add(NG3 - 2, 0)
            add(NG3 - 1, 1)
            dve.wait_ge(slots_back, 16)
            dve.tensor_copy(k.slot_dst[:], slots[:, :, 1])
            dve.tensor_copy(k.src_idx[:], slots[:, :, 0])
            dve.tensor_copy(k.id_idx[:], slots[:, :, 3])

        @block.scalar
        def _(act):
            with act.Fori(0, NG3 // 2) as i:
                for u in range(2):
                    g = i * 2 + u
                    act.wait_ge(chunk_done, g * 2 + 2)
                    for j in range(GT):
                        act.wait_ge(hots_built, g * (GT + 1) + j + 1)
                        for q in (1, 2):
                            last = act.activation(hot_dst[:, u, j, 1 + q, :], hot_dst[:, u, j, 0, :], ACT.Copy,
                                                  scale=k.slot_w[:, q, bass.ds(g * GT + j, 1)])
                    last.then_inc(weighted, 1)

        @block.tensor
        def _(pe):
            pe.sem_inc(chunk_done, 4)
            with pe.Fori(0, NG3 // 2) as i:
                for u in range(2):
                    g = i * 2 + u
                    pe.wait_ge(hots_built, g * (GT + 1) + GT + 1)
                    for c, parts in enumerate(((0,), (1, 2, 3))):
                        pe.wait_ge(added, g * 2 + c + 1)
                        if c:
                            pe.wait_ge(weighted, g + 1)
                        for j in range(GT):
                            for q in parts:
                                m = pe.matmul(k.bank[:, 2 * u + c, 0:C3], hot_dst[:, u, j, q, :], hot_src[:, u, j, 0:C3],
                                              start=(j == 0 and q == parts[0]), stop=(j == GT - 1 and q == parts[-1]))
                        m.then_inc(chunk_done, 1)


def transpose_weights_of_edges(nc, k):
    S = nc.alloc_semaphore
    transposed, copied, stored, summed = S("at_transposed"), S("at_copied"), S("at_stored"), S("deg_summed")
    r = Region(nc, k.acc_end, ARENA_END)
    rows = r.take("at_rows", [P, 2, NP], F32)
    with nc.Block() as block:
        @block.tensor
        def _(pe):
            for s in range(NB):
                if s >= 2:
                    pe.wait_ge(copied, s - 1)
                for b in range(NB):
                    t = pe.transpose(k.bank[:, 4 * (s % 2) + b // 4, b % 4 * P:(b % 4 + 1) * P], k.acc_a[:, b, s * P:(s + 1) * P], k.ident[:])
                t.then_inc(transposed, 1)

        @block.scalar
        def _(act):
            for s in range(NB):
                act.wait_ge(transposed, s + 1)
                if s >= 2:
                    act.wait_ge(stored, 16 * (s - 1))
                act.copy(rows[:, s % 2, 0:2 * 512].rearrange("p (b n) -> p b n", n=512), k.bank[:, 4 * (s % 2):4 * (s % 2) + 2, :])
                act.copy(rows[:, s % 2, 2 * 512:NP], k.bank[:, 4 * (s % 2) + 2, 0:NP - 2 * 512]).then_inc(copied, 1)

        @block.sync
        def _(sp):
            for s in range(NB):
                sp.wait_ge(copied, s + 1)
                sp.dma_start(k.at_dram[s * P:(s + 1) * P, :], rows[:, s % 2, :]).then_inc(stored, 16)
                sp.wait_ge(stored, 16 * (s + 1))

        @block.vector
        def _(dve):
            dve.tensor_reduce(k.deg[:], k.acc_a[:], axis=AX, op=ALU.add).then_inc(summed, 1)
            dve.wait_ge(summed, 1)


def layer0(nc, k):
    S = nc.alloc_semaphore
    ct_transposed, ct_copied, gamma_done, y_done = S("ct_transposed"), S("ct_copied"), S("gamma_done"), S("y0_done")
    inv_ready, var_ready, dev_ready, x1_ready, x1_stored = S("inv0_ready"), S("var0_ready"), S("dev0_ready"), S("x1_ready"), S("x1_stored")
    x1t_done, x1t_copied = S("x1t_transposed"), S("x1t_copied")
    r = Region(nc, k.acc_end - 4 * NB * NP, k.tail - 4 * KC * NP)
    inv = r.take("inv0", [P, NB], F32)
    norm = Norm(nc, r, "norm0", NB)
    y = k.alpha
    with nc.Block() as block:
        @block.tensor
        def _(pe):
            for s in range(NB):
                if s >= 2:
                    pe.wait_ge(ct_copied, s - 1)
                for b in range(NB):
                    t = pe.transpose(k.bank[:, 3 * (s % 2) + b // 4, b % 4 * P:(b % 4 + 1) * P], k.acc_c[:, b, s * P:(s + 1) * P], k.ident[:])
                t.then_inc(ct_transposed, 1)
            for s in range(NB):
                if s >= 2:
                    pe.wait_ge(y_done, s - 1)
                for b in range(NB):
                    m = pe.matmul(k.bank[:, 6 + s % 2, :], k.acc_c[:, b, s * P:(s + 1) * P], k.beta[:, b, :], start=(b == 0), stop=(b == NB - 1))
                m.then_inc(gamma_done, 1)
            pe.wait_ge(ct_copied, NB)
            for b in range(NB):
                pe.wait_ge(x1_ready, b + 1)
                if b >= 4:
                    pe.wait_ge(x1t_copied, b - 3)
                for c in range(KC):
                    t = pe.transpose(k.bank[:, b % 4, c * P:(c + 1) * P], y[:, b, c * P:(c + 1) * P], k.ident[:])
                t.then_inc(x1t_done, 1)

        @block.scalar
        def _(act):
            for s in range(NB):
                act.wait_ge(ct_transposed, s + 1)
                act.copy(k.ct[:, s, 0:2 * 512].rearrange("p (b n) -> p b n", n=512), k.bank[:, 3 * (s % 2):3 * (s % 2) + 2, :])
                act.copy(k.ct[:, s, 2 * 512:NP], k.bank[:, 3 * (s % 2) + 2, 0:NP - 2 * 512]).then_inc(ct_copied, 1)
            act.wait_ge(var_ready, 1)
            act.sqrt(norm.dev[:], norm.var[:]).then_inc(dev_ready, 1)
            for b in range(NB):
                act.wait_ge(x1t_done, b + 1)
                act.copy(k.x1t[:, :, b * P:(b + 1) * P], k.bank[:, b % 4, :].rearrange("p (c n) -> p c n", c=KC)).then_inc(x1t_copied, 1)

        @block.vector
        def _(dve):
            me = Steps(nc, dve, "layer0_dve")
            for b in range(NB):
                me.mark(dve.tensor_scalar(k.mask[:, b, :], k.acc_c[:, b, :], 0.5, NEVER, ALU.is_lt, ALU.mult))
            for s in range(NB):
                dve.wait_ge(ct_copied, s + 1)
                me.mark(dve.tensor_reduce(k.counts[:, s:s + 1], k.ct[:, s, :], axis=AX, op=ALU.add))
            dve.wait_ge(me.sem, me.n)
            me.mark(dve.tensor_copy(inv[:, 0:NB - 1], k.counts[:, 0:NB - 1]))
            me.then(dve.tensor_tensor(inv[:, NB - 1:NB], k.counts[:, NB - 1:NB], k.pad_rows[:], ALU.add))
            me.then(dve.reciprocal(inv[:], inv[:]))
            for s in range(NB):
                dve.wait_ge(gamma_done, s + 1)
                dve.scalar_tensor_tensor(y[:, s, :], k.bank[:, 6 + s % 2, :], inv[:, s:s + 1], y[:, s, :], ALU.mult, ALU.add).then_inc(y_done, 1)
                dve.wait_ge(y_done, s + 1)
                norm.stats(dve, me, s, y[:, s, :])
            norm.variance(dve, me, var_ready)
            dve.wait_ge(dev_ready, 1)
            norm.invert(dve, me)
            for b in range(NB):
                norm.apply(dve, b, y[:, b, :]).then_inc(x1_ready, 1)

        @block.sync
        def _(sp):
            for b in range(NB):
                sp.wait_ge(x1_ready, b + 1)
                sp.dma_start(k.x1_dram[b * P:(b + 1) * P, :], y[:, b, :]).then_inc(x1_stored, 16)
            sp.wait_ge(x1_stored, 16 * NB)


WIDE = (0, C3, 2 * C3)


def turned(pe, k, bank, rows, j, n):
    for o in range(n):
        t = pe.transpose(k.bank[:, bank, o * P:(o + 1) * P], rows[:, o, j * P:(j + 1) * P], k.ident[:])
    return t


def project(nc, k, a, l, at):
    S = at.sem
    w_loaded, w_turned, w_copied = [S(f"wqkv_loaded{j}") for j in range(3)], S("wqkv_turned"), S("wqkv_copied")
    v_loaded, v_turned, v_ready = S("vectors_loaded"), S("vectors_turned"), S("vectors_ready")
    q_done, k_done, val_done = S("q_done"), S("k_done"), S("v_done")
    q_copied, k_copied, val_copied, ones_set = S("q_copied"), S("k_copied"), S("v_copied"), S("v_ones_set")
    cols_done, bq_scaled = S("cols_done"), S("bq_scaled")
    r = Region(nc, at.temps, k.tail - 4 * KC * NP)
    w_rows = r.take("wqkv_rows", [P, 2, KC, D], F32)
    w_in = r.take("wqkv_in", [P, 2, KC, D], F32)
    weights = (a.L1_gnn_Wq, a.L1_gnn_Wk, a.L1_gnn_Wv)
    with nc.Block() as block:
        @block.sync
        def _(sp):
            row = 0
            for v, n in ((a.L1_gnn_bq, KC), (a.L1_gnn_bo, KC), (a.L1_gnn_g1, KC), (a.L1_gnn_beta1, KC), (a.L1_gnn_b1, FF // P),
                         (a.L1_gnn_b2, KC), (a.L1_gnn_g2, KC), (a.L1_gnn_beta2, KC)):
                sp.dma_start(at.vec_rows[row:row + n, :], v[bass.ds(l, 1), :].rearrange("l (c p) -> (l c) p", p=P)).then_inc(v_loaded, 16)
                row += n
            for j in range(3):
                if j >= 2:
                    sp.wait_ge(w_turned, (j - 1) * KC)
                sp.dma_start(w_rows[:, j % 2, :, :], weights[j][bass.ds(l, 1), :, :].rearrange("l (o p) i -> p (l o) i", p=P)).then_inc(w_loaded[j], 16)

        @block.tensor
        def _(pe):
            pe.wait_ge(v_loaded, 16 * 8)
            pe.transpose(k.bank[:, 7, 0:at.NV], at.vec_rows[0:at.NV, :], k.ident[0:at.NV, 0:at.NV]).then_inc(v_turned, 1)

            def turn(j):
                pe.wait_ge(w_loaded[j], 16)
                for c in range(KC):
                    n = j * KC + c
                    if n >= 2:
                        pe.wait_ge(w_copied, n - 1)
                    turned(pe, k, n % 2, w_rows[:, j % 2], c, KC).then_inc(w_turned, 1)

            n = 0
            turn(0)
            for j, done, copied in ((0, q_done, q_copied), (1, k_done, k_copied)):
                turn(j + 1)
                pe.wait_ge(w_copied, (j + 1) * KC)
                for o in range(KC):
                    for c in range(3):
                        if n >= 4:
                            m4 = n - 4
                            pe.wait_ge(q_copied if m4 < 12 else k_copied, m4 % 12 + 1)
                        for i in range(KC):
                            m = pe.matmul(k.bank[:, 2 + n % 4, 0:C3], w_in[:, j % 2, i, o * P:(o + 1) * P],
                                          k.x1t[:, i, WIDE[c]:WIDE[c] + C3], start=(i == 0), stop=(i == KC - 1))
                        m.then_inc(done, 1)
                        n += 1
            pe.wait_ge(w_copied, 3 * KC)
            pe.wait_ge(k_copied, 12)
            for b in range(NB):
                if b >= 4:
                    pe.wait_ge(val_copied, b - 3)
                for i in range(KC):
                    m = pe.matmul(k.bank[:, 2 + b % 4, :], k.x1t[:, i, b * P:(b + 1) * P], w_in[:, 0, i, :], start=(i == 0), stop=(i == KC - 1))
                m.then_inc(val_done, 1)

        @block.scalar
        def _(act):
            def copy_weights(j):
                for c in range(KC):
                    act.wait_ge(w_turned, j * KC + c + 1)
                    if j == 2 and c == 0:
                        act.wait_ge(q_done, 12)
                    act.copy(w_in[:, j % 2, c, :], k.bank[:, (j * KC + c) % 2, :]).then_inc(w_copied, 1)

            copy_weights(0)
            copy_weights(1)
            act.wait_ge(bq_scaled, 1)
            for n in range(12):
                act.wait_ge(q_done, n + 1)
                act.activation(at.q[:, n // 3, WIDE[n % 3]:WIDE[n % 3] + C3], k.bank[:, 2 + n % 4, 0:C3], ACT.Identity,
                               bias=at.bq[:, n // 3:n // 3 + 1], scale=DH ** -0.5).then_inc(q_copied, 1)
            copy_weights(2)

        @block.vector
        def _(dve):
            dve.memset(at.val[:, :, :, DH:2 * DH], 1.0).then_inc(ones_set, 1)
            dve.memset(at.q[:, :, W3:NP], 0.0)
            dve.memset(at.k[:, :, W3:NP], 0.0)
            dve.wait_ge(v_turned, 1)
            dve.tensor_copy(at.vec[:], k.bank[:, 7, 0:at.NV]).then_inc(v_ready, 1)
            dve.wait_ge(v_ready, 1)
            dve.tensor_scalar(at.bq[:], at.vec[:, 0:KC], DH ** -0.5, None, ALU.mult).then_inc(bq_scaled, 1)
            for n in range(12):
                dve.wait_ge(k_done, n + 1)
                dve.tensor_copy(at.k[:, n // 3, WIDE[n % 3]:WIDE[n % 3] + C3], k.bank[:, 2 + n % 4, 0:C3]).then_inc(k_copied, 1)
            for b in range(NB):
                dve.wait_ge(val_done, b + 1)
                heads = k.bank[:, 2 + b % 4, :].rearrange("p (h u d) -> p h u d", u=2, d=DH)
                dve.tensor_copy(at.val[:, b, :, 0:DH], heads[:, :, 0, :])
                dve.tensor_copy(at.val[:, b, :, 2 * DH:3 * DH], heads[:, :, 1, :]).then_inc(val_copied, 1)


def attend(nc, k, at):
    S = at.sem
    scored, maxed, max_ready, max_turned, max_copied = S("scored"), S("maxed"), S("max_ready"), S("max_turned"), S("max_copied")
    st_done, exp_done, p_ready, pv_done, pv_copied = S("st_done"), S("exp_done"), S("p_ready"), S("pv_done"), S("pv_copied")
    head_done, pair_max = S("head_done"), S("pair_max")
    NPT = 3
    r = Region(nc, at.temps, k.tail - 4 * KC * NP)
    junk = r.take("junk", [P, 2, 2, 2, C4], BF16)
    maxes = r.take("maxes", [P, NB, H, 2], F32)
    m1, m2 = r.take("m1", [P, NB, H], F32), r.take("m2", [P, NB, H], F32)
    parts = r.take("m_parts", [P, NB, H, 3], BF16)
    mt = r.take("mt", [3 * H, NP], BF16)
    pt = r.take("pt", [P, NPT, NP], F32)
    raw = r.take("raw", [P, W3], F32)
    inv = r.take("inv_s", [P, W3], F32)
    order = [(p, b, hf) for p in range(HP) for b in range(NB) for hf in range(2)]
    units = [(p, u, j) for p in range(HP) for u in range(2) for j in range(NB)]
    with nc.Block() as block:
        @block.tensor
        def _(pe):
            for n, (p, b, hf) in enumerate(order):
                if n >= 2:
                    pe.wait_ge(maxed, 2 * (n - 1))
                for c in range(2):
                    for u in range(2):
                        at0 = (2 * hf + c) * C4
                        m = pe.matmul(k.bank[:, 4 * (n % 2) + 2 * u + c, 0:C4], at.q[DH * u:DH * (u + 1), p, b * P:(b + 1) * P],
                                      at.k[DH * u:DH * (u + 1), p, at0:at0 + C4], start=True, stop=True)
                m.then_inc(scored, 1)
            pe.wait_ge(max_ready, 1)
            for b in range(NB):
                t = pe.transpose(k.bank[0:3 * H, b // 5, :].bitcast(BF16)[:, b % 5 * P:(b % 5 + 1) * P],
                                 parts[:, b, :, :].rearrange("p h t -> p (h t)"), k.ident16[:])
            t.then_inc(max_turned, 1)
            pe.wait_ge(max_copied, 2)

            def scores(n):
                p, u, j = units[n]
                for hf in range(2):
                    if n >= 1:
                        pe.wait_ge(exp_done, 2 * (n - 1) + hf + 1)
                    for c, (at0, wide) in enumerate(((hf * HALF, 512), (hf * HALF + 512, HALF - 512))):
                        to = k.bank[:, 2 * hf + c, 0:wide]
                        pe.matmul(to, at.k[DH * u:DH * (u + 1), p, j * P:(j + 1) * P], at.q[DH * u:DH * (u + 1), p, at0:at0 + wide],
                                  start=True, stop=False)
                        pe.matmul(to, k.sel[:, 2 * p + u, :], mt[:, at0:at0 + wide], start=False, stop=False)
                        for b in range(wide // P):
                            m = pe.matmul(to[:, b * P:(b + 1) * P], k.mask[:, at0 // P + b, j * P:(j + 1) * P], k.ident16[:],
                                          start=False, stop=(b == wide // P - 1))
                    m.then_inc(st_done, 1)

            def values(n):
                p, u, j = units[n]
                pe.wait_ge(p_ready, n + 1)
                if j == 0 and n:
                    pe.wait_ge(pv_copied, n // NB)
                for c in range(3):
                    m = pe.matmul(k.bank[:, 4 + c, 0:C3], at.val[:, j, p, u * DH:(u + 2) * DH], pt[:, n % NPT, c * C3:(c + 1) * C3],
                                  start=(j == 0), stop=(j == NB - 1))
                m.then_inc(pv_done, 1)

            for n in range(len(units) + 2):
                if n < len(units):
                    scores(n)
                if n >= 2:
                    values(n - 2)

        @block.scalar
        def _(act):
            def copy_out(h):
                act.wait_ge(pv_done, NB * (h + 1))
                if h:
                    act.wait_ge(head_done, h)
                act.copy(raw[:].rearrange("p (c n) -> p c n", c=3), k.bank[:, 4:7, 0:C3]).then_inc(pv_copied, 1)

            for n in range(len(units)):
                if n >= NPT:
                    act.wait_ge(pv_done, n - NPT + 1)
                for hf in range(2):
                    act.wait_ge(st_done, 2 * n + hf + 1)
                    act.activation(pt[:, n % NPT, hf * HALF:(hf + 1) * HALF],
                                   k.bank[:, 2 * hf:2 * hf + 2, :].rearrange("p c n -> p (c n)")[:, 0:HALF], ACT.Exp).then_inc(exp_done, 1)
                if n % NB == 2 and n > NB:
                    copy_out(n // NB - 1)
            copy_out(H - 1)

        @block.vector
        def _(dve):
            me = Steps(nc, dve, at.sem("attend_dve"))
            for n, (p, b, hf) in enumerate(order):
                dve.wait_ge(scored, n + 1)
                for u in range(2):
                    dve.tensor_tensor_reduce(out=junk[:, n % 2, u, :, :], in0=k.bank[:, 4 * (n % 2) + 2 * u:4 * (n % 2) + 2 * u + 2, 0:C4],
                                             in1=k.mask[:, b, 2 * hf * C4:2 * (hf + 1) * C4].rearrange("p (c n) -> p c n", c=2),
                                             scale=1.0, scalar=NEVER, op0=ALU.add, op1=ALU.max,
                                             accum_out=maxes[:, b, 2 * p + u, hf:hf + 1]).then_inc(maxed, 1)
            dve.wait_ge(maxed, 2 * len(order))
            me.then(dve.tensor_tensor(m1[:], maxes[:, :, :, 0], maxes[:, :, :, 1], ALU.max))
            me.then(dve.tensor_scalar(m1[:], m1[:], -1.0, None, ALU.mult))
            for q in range(3):
                last = dve.tensor_copy(parts[:, :, :, q], m1[:])
                if q < 2:
                    me.then(last)
                    me.then(dve.tensor_copy(m2[:], parts[:, :, :, q]))
                    me.then(dve.tensor_tensor(m1[:], m1[:], m2[:], ALU.subtract))
            last.then_inc(max_ready, 1)
            dve.wait_ge(max_turned, 1)
            for i in range(2):
                dve.tensor_copy(mt[:, i * 5 * P:(i + 1) * 5 * P], k.bank[0:3 * H, i, :].bitcast(BF16)[:, 0:5 * P]).then_inc(max_copied, 1)

            def finish(h):
                dve.wait_ge(pv_copied, h + 1)
                v0 = DH * (h % 2)
                s0 = DH - v0
                me.then(dve.tensor_scalar(inv[v0:v0 + DH, :], raw[s0:s0 + DH, :], 1e-16, None, ALU.add))
                me.then(dve.reciprocal(inv[v0:v0 + DH, :], inv[v0:v0 + DH, :]))
                dve.tensor_tensor(at.q[v0:v0 + DH, h // 2, 0:W3], raw[v0:v0 + DH, :], inv[v0:v0 + DH, :], ALU.mult).then_inc(head_done, 1)

            for n, (p, u, j) in enumerate(units):
                dve.wait_ge(exp_done, 2 * n + 2)
                dve.tensor_tensor(pt[:, n % NPT, :], pt[:, n % NPT, :], k.ct[:, j, :], ALU.mult).then_inc(p_ready, 1)
                if n % NB == 4 and n > NB:
                    finish(n // NB - 1)
            finish(H - 1)


def finish_layer(nc, k, a, l, at):
    S = at.sem
    w_loaded, w_turned, w_copied = [S(f"wo12_loaded{j}") for j in range(3)], S("wo12_turned"), S("wo12_copied")
    o_done, o_added, f_done, f_added, h_done, h_copied = S("o_done"), S("o_added"), S("f_done"), S("f_added"), S("h_done"), S("h_copied")
    var_ready, dev_ready, x_ready = S("bn_var_ready"), S("bn_dev_ready"), S("bn_x_ready")
    r = Region(nc, at.temps, k.tail - 4 * KC * NP)
    rows = r.take("wo12_rows", [P, KC, D], F32)
    wo = r.take("wo_in", [P, KC, D], F32)
    w1 = r.take("w1_in", [P, KC, FF], F32)
    w2 = r.take("w2_in", [P, FF // P, D], F32)
    norm = Norm(nc, r, "bn", KC)
    scale, shift = r.take("bn_scale", [P, KC], F32), r.take("bn_shift", [P, KC], F32)
    hid = at.k[:, 0:FF // P, :]
    FP = FF // P
    turns = [(0, c, KC, wo[:, c, :]) for c in range(KC)] + [(1, c, FP, w1[:, c, :]) for c in range(KC)] + [(2, c, KC, w2[:, c, :]) for c in range(FP)]
    with nc.Block() as block:
        @block.sync
        def _(sp):
            for j, (w, n, m) in enumerate(((a.L1_gnn_Wo, KC, D), (a.L1_gnn_W1, FP, D), (a.L1_gnn_W2, KC, FF))):
                if j:
                    sp.wait_ge(w_turned, 4 * j)
                sp.dma_start(rows[:, 0:n, 0:m], w[bass.ds(l, 1), :, :].rearrange("l (o p) i -> p (l o) i", p=P)).then_inc(w_loaded[j], 16)

        @block.tensor
        def _(pe):
            for n, (j, c, o, to) in enumerate(turns):
                if c == 0:
                    pe.wait_ge(w_loaded[j], 16)
                if n >= 2:
                    pe.wait_ge(w_copied, n - 1)
                turned(pe, k, n % 2, rows, c, o).then_inc(w_turned, 1)
            pe.wait_ge(w_copied, len(turns))
            n = 0

            def product(w, x, inputs, outputs, done, free):
                nonlocal_n = [0]
                for o in range(outputs):
                    for c in range(3):
                        m = nonlocal_n[0]
                        if m >= 4:
                            pe.wait_ge(free, m - 3)
                        for i in range(inputs):
                            last = pe.matmul(k.bank[:, 2 + m % 4, 0:C3], w[:, i, o * P:(o + 1) * P], x[:, i, WIDE[c]:WIDE[c] + C3],
                                             start=(i == 0), stop=(i == inputs - 1))
                        last.then_inc(done, 1)
                        nonlocal_n[0] += 1

            product(wo, at.q, KC, KC, o_done, o_added)
            pe.wait_ge(x_ready, KC)
            product(w1, k.x1t, KC, FP, h_done, h_copied)
            pe.wait_ge(h_copied, 3 * FP)
            product(w2, hid, FP, KC, f_done, f_added)

        @block.scalar
        def _(act):
            for n, (j, c, o, to) in enumerate(turns):
                act.wait_ge(w_turned, n + 1)
                act.copy(to, k.bank[:, n % 2, 0:o * P]).then_inc(w_copied, 1)
            act.wait_ge(var_ready, 1)
            act.sqrt(norm.dev[:], norm.var[:]).then_inc(dev_ready, 1)
            for n in range(3 * FP):
                act.wait_ge(h_done, n + 1)
                c = WIDE[n % 3]
                act.activation(hid[:, n // 3, c:c + C3], k.bank[:, 2 + n % 4, 0:C3], ACT.Relu,
                               bias=at.vec[:, at.B1 + n // 3:at.B1 + n // 3 + 1]).then_inc(h_copied, 1)
            act.wait_ge(var_ready, 2)
            act.sqrt(norm.dev[:], norm.var[:]).then_inc(dev_ready, 1)

        @block.vector
        def _(dve):
            me = Steps(nc, dve, at.sem("finish_dve"))

            def add_and_norm(done, added, bias, gain, beta, turn):
                for n in range(3 * KC):
                    o, c = n // 3, WIDE[n % 3]
                    x = k.x1t[:, o, c:c + C3]
                    dve.wait_ge(done, n + 1)
                    dve.scalar_tensor_tensor(x, k.bank[:, 2 + n % 4, 0:C3], at.vec[:, bias + o:bias + o + 1], x, ALU.add, ALU.add).then_inc(added, 1)
                for o in range(KC):
                    dve.wait_ge(added, 3 * o + 3)
                    norm.stats(dve, me, o, *(k.x1t[:, o, c:min(c + C3, N)] for c in WIDE))
                norm.variance(dve, me, var_ready)
                dve.wait_ge(dev_ready, turn)
                norm.invert(dve, me)
                me.then(dve.tensor_tensor(scale[:], norm.dev[:], at.vec[:, gain:gain + KC], ALU.mult))
                me.then(dve.tensor_tensor(shift[:], norm.mean_var[:, :, 0], scale[:], ALU.mult))
                me.then(dve.tensor_tensor(shift[:], at.vec[:, beta:beta + KC], shift[:], ALU.subtract))
                for o in range(KC):
                    dve.tensor_scalar(k.x1t[:, o, 0:W3], k.x1t[:, o, 0:W3], scale[:, o:o + 1], shift[:, o:o + 1], ALU.mult, ALU.add).then_inc(x_ready, 1)

            add_and_norm(o_done, o_added, at.BO, at.G1, at.BETA1, 1)
            add_and_norm(f_done, f_added, at.B2, at.G2, at.BETA2, 2)
            dve.wait_ge(x_ready, 2 * KC)


def layer1(nc, k, a):
    at = Names()
    at.sems = []

    def sem(name):
        at.sems.append(nc.alloc_semaphore(name))
        return at.sems[-1]

    at.sem = sem
    at.BO, at.G1, at.BETA1, at.B1, at.B2, at.G2, at.BETA2, at.NV = 4, 8, 12, 16, 18, 22, 26, 30
    r = Region(nc, k.shared_end, k.tail - 4 * KC * NP)
    at.q = r.take("q", [P, HP, NP], F32)
    at.k = r.take("k", [P, HP, NP], F32)
    at.val = r.take("val", [P, NB, HP, 3 * DH], F32)
    at.vec_rows = r.take("vec_rows", [at.NV, P], F32)
    at.vec = r.take("vec", [P, at.NV], F32)
    at.bq = r.take("bq8", [P, KC], F32)
    at.temps = r.at
    with nc.Fori(0, LAYERS) as l:
        project(nc, k, a, l, at)
        attend(nc, k, at)
        finish_layer(nc, k, a, l, at)
        with nc.Block() as block:
            @block.gpsimd
            def _(pool):
                for s in at.sems:
                    pool.sem_clear(s)


def layer2(nc, k, a):
    S = nc.alloc_semaphore
    turned_back, z_copied, x1_loaded, rows_loaded, w_loaded, at_loaded = (
        S("l1_turned_back"), S("z_copied"), S("x1_loaded"), [S(f"rows2_loaded{j}") for j in range(4)], S("w2_loaded"), S("at_loaded"))
    var_ready, dev_ready, x2_ready, x2t_done, x2t_copied = S("l2_var_ready"), S("l2_dev_ready"), S("x2_ready"), S("x2t_done"), S("x2t_copied")
    deg_ready, deg_root = S("deg_ready"), S("deg_root")
    x1b_ready, x2b_ready, h_done, h_scaled, sum_done, y_done = (
        S("x1b_ready"), S("x2b_ready"), S("l2_h_done"), S("l2_h_scaled"), S("l2_sum_done"), S("l2_y_done"))
    x3_ready, table_ready, table_stored = S("x3_ready"), S("table_ready"), S("table_stored")
    r = Region(nc, k.x3_end, k.tail - 4 * KC * NP)
    z = r.take("z", [P, NB, D], F32)
    xt = r.take("x2t", [P, KC, NP], F32)
    h = r.take("h_scaled", [P, NB, D], F32)
    w = r.take("w_l2", [P, KC, D], F32)
    part = r.take("l2_part", [P, 2, D], F32)
    gain, shift, bias, b_edge = (r.take(n, [P, D], F32) for n in ("ln_g_row", "ln_b_row", "l2_b_row", "b_edge_row"))
    dinv, has, root = r.take("dinv", [P, NB], F32), r.take("has_deg", [P, NB], F32), r.take("deg_dev", [P, NB], F32)
    norms = [Norm(nc, r, f"norm2{j}", NB) for j in range(3)]
    x = k.x3
    weights = Region(nc, k.tail, ARENA_END).take("at", [P, NB, NP], F32)
    with nc.Block() as block:
        @block.sync
        def _(sp):
            sp.dma_start(x[:], k.x1_dram.rearrange("(b p) f -> p b f", p=P)).then_inc(x1_loaded, 16)
            for j, (row, v) in enumerate(((shift, a.L1_gnn_ln_b), (gain, a.L1_gnn_ln_g), (bias, a.L2_gnn_b), (b_edge, a.L3_gnn_b_edge))):
                sp.dma_start(row[:], row_of(v)).then_inc(rows_loaded[j], 16)
            sp.dma_start(w[:], a.L2_gnn_W.rearrange("(c p) n -> p c n", p=P)).then_inc(w_loaded, 16)
            sp.dma_start(weights[:], k.at_dram.rearrange("(b p) n -> p b n", p=P)).then_inc(at_loaded, 16)
            for b in range(NB):
                sp.wait_ge(table_ready, b + 1)
                sp.dma_start(k.table_dram[b * P:(b + 1) * P, :], z[:, b, :]).then_inc(table_stored, 16)
            sp.wait_ge(table_stored, 16 * NB)

        @block.gpsimd
        def _(pool):
            pool.wait_ge(x1_loaded, 16)
            pool.wait_ge(rows_loaded[0], 16)
            for b in range(NB):
                pool.tensor_tensor(x[:, b, :], x[:, b, :], shift[:], ALU.add).then_inc(x1b_ready, 1)
            pool.wait_ge(rows_loaded[2], 16)
            for b in range(NB):
                pool.wait_ge(x2_ready, b + 1)
                pool.tensor_tensor(x[:, b, :], z[:, b, :], bias[:], ALU.add).then_inc(x2b_ready, 1)
            pool.wait_ge(rows_loaded[3], 16)
            for b in range(NB):
                pool.wait_ge(x3_ready, b + 1)
                pool.tensor_tensor(z[:, b, :], x[:, b, :], b_edge[:], ALU.add).then_inc(table_ready, 1)

        @block.tensor
        def _(pe):
            for b in range(NB):
                if b >= 4:
                    pe.wait_ge(z_copied, b - 3)
                for c in range(KC):
                    t = pe.transpose(k.bank[:, b % 4, c * P:(c + 1) * P], k.x1t[:, c, b * P:(b + 1) * P], k.ident[:])
                t.then_inc(turned_back, 1)
            for b in range(NB):
                pe.wait_ge(x2_ready, b + 1)
                if b >= 4:
                    pe.wait_ge(x2t_copied, b - 3)
                for c in range(KC):
                    t = pe.transpose(k.bank[:, b % 4, c * P:(c + 1) * P], z[:, b, c * P:(c + 1) * P], k.ident[:])
                t.then_inc(x2t_done, 1)
            pe.wait_ge(w_loaded, 16)
            for b in range(NB):
                pe.wait_ge(x2t_copied, b + 1)
                if b >= 2:
                    pe.wait_ge(h_scaled, b - 1)
                for c in range(KC):
                    m = pe.matmul(k.bank[:, 4 + b % 2, :], xt[:, c, b * P:(b + 1) * P], w[:, c, :], start=(c == 0), stop=(c == KC - 1))
                m.then_inc(h_done, 1)
            pe.wait_ge(at_loaded, 16)
            pe.wait_ge(h_scaled, NB)
            for b in range(NB):
                if b >= 2:
                    pe.wait_ge(y_done, b - 1)
                for s in range(NB):
                    m = pe.matmul(k.bank[:, 6 + b % 2, :], weights[:, s, b * P:(b + 1) * P], h[:, s, :], start=(s == 0), stop=(s == NB - 1))
                m.then_inc(sum_done, 1)

        @block.scalar
        def _(act):
            for b in range(NB):
                act.wait_ge(turned_back, b + 1)
                act.copy(z[:, b, :], k.bank[:, b % 4, :]).then_inc(z_copied, 1)
            act.wait_ge(deg_ready, 1)
            act.sqrt(root[:], root[:]).then_inc(deg_root, 1)
            for j in range(2):
                act.wait_ge(var_ready, j + 1)
                act.sqrt(norms[j].dev[:], norms[j].var[:]).then_inc(dev_ready, 1)
            for b in range(NB):
                act.wait_ge(x2t_done, b + 1)
                act.copy(xt[:, :, b * P:(b + 1) * P], k.bank[:, b % 4, :].rearrange("p (c n) -> p c n", c=KC)).then_inc(x2t_copied, 1)
            act.wait_ge(var_ready, 3)
            act.sqrt(norms[2].dev[:], norms[2].var[:]).then_inc(dev_ready, 1)

        @block.vector
        def _(dve):
            me = Steps(nc, dve, "layer2_dve")
            me.then(dve.tensor_scalar(root[:], k.deg[:], 1.0, None, ALU.add))
            me.then(dve.tensor_scalar(has[:], root[:], 0.0, None, ALU.is_gt))
            dve.tensor_scalar(root[:], root[:], 1e-30, None, ALU.max).then_inc(deg_ready, 1)
            for b in range(NB):
                dve.wait_ge(z_copied, b + 1)
                norms[0].stats(dve, me, b, z[:, b, :])
            norms[0].variance(dve, me, var_ready)
            dve.wait_ge(deg_root, 1)
            me.then(dve.reciprocal(dinv[:], root[:]))
            me.then(dve.tensor_tensor(dinv[:], dinv[:], has[:], ALU.mult))
            dve.wait_ge(dev_ready, 1)
            norms[0].invert(dve, me)
            dve.wait_ge(rows_loaded[1], 16)
            for b in range(NB):
                dve.wait_ge(x1b_ready, b + 1)
                me.then(norms[0].affine(dve, me, b, z[:, b, :], gain[:], x[:, b, :]))
                norms[1].stats(dve, me, b, z[:, b, :])
            norms[1].variance(dve, me, var_ready)
            dve.wait_ge(dev_ready, 2)
            norms[1].invert(dve, me)
            for b in range(NB):
                norms[1].apply(dve, b, z[:, b, :]).then_inc(x2_ready, 1)
            for b in range(NB):
                dve.wait_ge(h_done, b + 1)
                dve.tensor_scalar(h[:, b, :], k.bank[:, 4 + b % 2, :], dinv[:, b:b + 1], None, ALU.mult).then_inc(h_scaled, 1)
            for b in range(NB):
                dve.wait_ge(sum_done, b + 1)
                dve.wait_ge(h_scaled, b + 1)
                dve.tensor_tensor(part[:, b % 2, :], k.bank[:, 6 + b % 2, :], h[:, b, :], ALU.add).then_inc(y_done, 1)
                dve.wait_ge(y_done, b + 1)
                dve.wait_ge(x2b_ready, b + 1)
                me.then(dve.scalar_tensor_tensor(x[:, b, :], part[:, b % 2, :], dinv[:, b:b + 1], x[:, b, :], ALU.mult, ALU.add))
                norms[2].stats(dve, me, b, x[:, b, :])
            norms[2].variance(dve, me, var_ready)
            dve.wait_ge(dev_ready, 3)
            norms[2].invert(dve, me)
            for b in range(NB):
                norms[2].apply(dve, b, x[:, b, :]).then_inc(x3_ready, 1)


def edge_messages(nc, k, a):
    S = nc.alloc_semaphore
    w_loaded, staged, got_x, got_e = S("we_loaded"), S("idx_staged"), [S(f"got_x{u}") for u in range(2)], [S(f"got_e{u}") for u in range(2)]
    passed, turned_e, e_copied, emb_done, added_x, relu_done = S("msg_pool_passed"), S("e_turned"), S("e_copied"), S("emb_done"), S("added_x"), S("relu_done")
    hot_ready, summed, agg_added, agg_cleared = S("hot_ready"), S("msgs_summed"), S("agg_added"), S("agg_cleared")
    r = Region(nc, k.agg_end, ARENA_END)
    idx = r.take("st_idx", [P, 2, 2, GT], U32)
    xg = r.take("x_got", [P, 2, GT, D], F32)
    ea = r.take("edge_got", [P, 2, GT, ED], F32)
    et = r.take("edge_turned", [P, 2, GT * P], F32)
    msg = r.take("msg", [P, 2, GT, D], F32)
    hot = r.take("hot_t", [P, 2, GT, P], F32)
    we = r.take("w_edge", [ED, D], F32)
    agg = k.agg[:].rearrange("p b f -> p (b f)")
    with nc.Block() as block:
        @block.sync
        def _(sp):
            sp.dma_start(we[:], a.L3_gnn_W_edge).then_inc(w_loaded, 16)

        @block.gpsimd
        def _(pool):
            with pool.Fori(0, NG // 2) as i:
                for u in range(2):
                    g = i * 2 + u
                    gate(pool, added_x, (g + 1) * GT, passed)
                    gate(pool, turned_e, g + 1, passed)
                    pool.tensor_copy(idx[:, u, 0, :], k.src_idx[:, bass.ds(g * GT, GT)]).then_inc(staged, 1)
                    pool.tensor_copy(idx[:, u, 1, :], k.id_idx[:, bass.ds(g * GT, GT)]).then_inc(staged, 1)
                    gate(pool, staged, g * 2 + 2, passed)
                    for j in range(GT):
                        pool.indirect_dma_start(out=ea[:, u, j, :], out_offset=None, in_=a.edge_attr_128,
                                                in_offset=bass.IndirectOffsetOnAxis(ap=idx[:, u, 1, j:j + 1], axis=0)).then_inc(got_e[u], 16)
                    for j in range(GT):
                        pool.indirect_dma_start(out=xg[:, u, j, :], out_offset=None, in_=k.table_dram,
                                                in_offset=bass.IndirectOffsetOnAxis(ap=idx[:, u, 0, j:j + 1], axis=0)).then_inc(got_x[u], 16)

        @block.tensor
        def _(pe):
            def turn(i, u):
                pe.wait_ge(got_e[u], i * (16 * GT) + 16 * GT)
                pe.wait_ge(e_copied, i * 2 + u + 1)
                for j in range(GT):
                    t = pe.transpose(k.bank[:, u, j * P:(j + 1) * P], ea[:, u, j, :], k.ident[:])
                t.then_inc(turned_e, 1)

            def embed(i, u):
                g = i * 2 + u
                pe.wait_ge(e_copied, g + 3)
                for j in range(GT):
                    pe.wait_ge(added_x, g * GT + GT + j + 1)
                    pe.matmul(k.bank[:, 2 + j, :], et[:, u, j * P:(j + 1) * P], we[:], start=True, stop=True).then_inc(emb_done, 1)

            def collect(i, u):
                g = i * 2 + u
                pe.wait_ge(hot_ready, g + 1)
                pe.wait_ge(agg_added, g + 1)
                for j in range(GT):
                    pe.wait_ge(relu_done, g * GT + j + 1)
                    m = pe.matmul(k.bank[:, 6 + u, :], hot[:, u, j, :], msg[:, u, j, :], start=(j == 0), stop=(j == GT - 1))
                m.then_inc(summed, 1)

            pe.sem_inc(turned_e, 2)
            pe.wait_ge(w_loaded, 16)
            turn(0, 0)
            embed(0, 0)
            turn(0, 1)
            with pe.Fori(0, NG // 2 - 1) as i:
                embed(i, 1)
                turn(i + 1, 0)
                collect(i, 0)
                embed(i + 1, 0)
                turn(i + 1, 1)
                collect(i, 1)
            embed(NG // 2 - 1, 1)
            collect(NG // 2 - 1, 0)
            collect(NG // 2 - 1, 1)

        @block.scalar
        def _(act):
            def copy_turned(i, u, first=False):
                g = i * 2 + u
                act.wait_ge(turned_e, g + 3)
                if not first:
                    act.wait_ge(emb_done, (g - 1) * GT)
                act.copy(et[:, u, :], k.bank[:, u, :]).then_inc(e_copied, 1)

            def relu(i, u):
                g = i * 2 + u
                for j in range(GT):
                    act.wait_ge(added_x, g * GT + 2 * GT + j + 1)
                    act.activation(msg[:, u, j, :], msg[:, u, j, :], ACT.Relu).then_inc(relu_done, 1)

            act.sem_inc(e_copied, 2)
            copy_turned(0, 0, True)
            copy_turned(0, 1, True)
            with act.Fori(0, NG // 2 - 1) as i:
                relu(i, 0)
                copy_turned(i + 1, 0)
                relu(i, 1)
                copy_turned(i + 1, 1)
            relu(NG // 2 - 1, 0)
            relu(NG // 2 - 1, 1)

        @block.vector
        def _(dve):
            def add_x(i, u):
                g = i * 2 + u
                dve.wait_ge(got_x[u], i * (16 * GT) + 16 * GT)
                for j in range(GT):
                    dve.wait_ge(emb_done, g * GT + j + 1)
                    dve.tensor_tensor(msg[:, u, j, :], k.bank[:, 2 + j, :], xg[:, u, j, :], ALU.add).then_inc(added_x, 1)

            def one_hot(i, u):
                for j in range(GT):
                    last = dve.tensor_scalar(hot[:, u, j, :], k.row128f[:], k.slot_dst[:, bass.ds((i * 2 + u) * GT + j, 1)], None, ALU.is_equal)
                last.then_inc(hot_ready, 1)

            def add_sum(i, u):
                g = i * 2 + u
                to = dve.value_load(k.blk[0:1, bass.ds(g, 1)], min_val=0, max_val=NB - 1) * D
                dve.wait_ge(summed, g + 1)
                dve.wait_ge(agg_added, g + 2)
                rows = agg[:, bass.ds(to, D)]
                dve.tensor_tensor(rows, k.bank[:, 6 + u, :], rows, ALU.add).then_inc(agg_added, 1)

            dve.sem_inc(added_x, 2 * GT)
            dve.memset(agg, 0.0).then_inc(agg_added, 2)
            one_hot(0, 0)
            add_x(0, 0)
            one_hot(0, 1)
            add_x(0, 1)
            with dve.Fori(0, NG // 2 - 1) as i:
                add_sum(i, 0)
                one_hot(i + 1, 0)
                add_x(i + 1, 0)
                add_sum(i, 1)
                one_hot(i + 1, 1)
                add_x(i + 1, 1)
            add_sum(NG // 2 - 1, 0)
            add_sum(NG // 2 - 1, 1)


def widen(nc, k, a):
    S = nc.alloc_semaphore
    eps_loaded, w_loaded, rows_loaded = S("eps_loaded"), S("w31_loaded"), S("rows31_loaded")
    h_ready, h_turned, h_copied, wide_done, wide_added = S("h3_ready"), S("h3_turned"), S("h3_copied"), S("wide_done"), S("wide_added")
    var_ready, dev_ready, scaled, gelu_done, g_turned, g_copied = (
        S("wide_var_ready"), S("wide_dev_ready"), S("wide_scaled"), S("wide_gelu"), S("wide_turned"), S("wide_copied"))
    r = Region(nc, k.agg_end, ARENA_END)
    k.wide_t = r.take("wide_t", [P, 2 * KC, NP], F32)
    wide = r.take("wide", [P, NB, D2], F32)
    w = r.take("w31", [P, KC, D2], F32)
    bias, gain, shift = (r.take(n, [P, D2], F32) for n in ("b31_row", "g31_row", "be31_row"))
    ht = k.wide_t[:, 0:KC, :]
    one_eps = r.take("one_eps", [P, 1], F32)
    norm = Norm(nc, r, "norm31", NB)
    h = k.agg
    with nc.Block() as block:
        @block.sync
        def _(sp):
            sp.dma_start(one_eps[:], row_of(a.L3_gnn_eps)).then_inc(eps_loaded, 16)
            sp.dma_start(w[:], a.L3_gnn_W1.rearrange("(c p) n -> p c n", p=P)).then_inc(w_loaded, 16)
            for row, v in ((bias, a.L3_gnn_b1), (gain, a.L3_gnn_g1), (shift, a.L3_gnn_be1)):
                sp.dma_start(row[:], row_of(v)).then_inc(rows_loaded, 16)

        @block.tensor
        def _(pe):
            for b in range(NB):
                pe.wait_ge(h_ready, b + 1)
                if b >= 2:
                    pe.wait_ge(h_copied, b - 1)
                for c in range(KC):
                    t = pe.transpose(k.bank[:, b % 2, c * P:(c + 1) * P], h[:, b, c * P:(c + 1) * P], k.ident[:])
                t.then_inc(h_turned, 1)
            pe.wait_ge(w_loaded, 16)
            for b in range(NB):
                pe.wait_ge(h_copied, b + 1)
                if b >= 2:
                    pe.wait_ge(wide_added, b - 1)
                for o in range(2):
                    for c in range(KC):
                        m = pe.matmul(k.bank[:, 4 + 2 * (b % 2) + o, :], ht[:, c, b * P:(b + 1) * P], w[:, c, o * D:(o + 1) * D],
                                      start=(c == 0), stop=(c == KC - 1))
                m.then_inc(wide_done, 1)
            for b in range(NB):
                pe.wait_ge(gelu_done, b + 1)
                if b >= 2:
                    pe.wait_ge(g_copied, b - 1)
                for c in range(2 * KC):
                    t = pe.transpose(k.bank[:, 2 * (b % 2) + c // 4, c % 4 * P:(c % 4 + 1) * P], wide[:, b, c * P:(c + 1) * P], k.ident[:])
                t.then_inc(g_turned, 1)

        @block.scalar
        def _(act):
            for b in range(NB):
                act.wait_ge(h_turned, b + 1)
                act.copy(ht[:, :, b * P:(b + 1) * P], k.bank[:, b % 2, :].rearrange("p (c n) -> p c n", c=KC)).then_inc(h_copied, 1)
            act.wait_ge(var_ready, 1)
            act.sqrt(norm.dev[:], norm.var[:]).then_inc(dev_ready, 1)
            for b in range(NB + 1):
                if b < NB:
                    act.wait_ge(scaled, b + 1)
                    act.activation(wide[:, b, :], wide[:, b, :], ACT.Gelu).then_inc(gelu_done, 1)
                if b:
                    act.wait_ge(g_turned, b)
                    act.copy(k.wide_t[:, :, (b - 1) * P:b * P], k.bank[:, 2 * ((b - 1) % 2):2 * ((b - 1) % 2) + 2, :]
                             .rearrange("p o (c n) -> p (o c) n", c=KC)).then_inc(g_copied, 1)

        @block.vector
        def _(dve):
            me = Steps(nc, dve, "widen_dve")
            dve.wait_ge(eps_loaded, 16)
            me.then(dve.tensor_scalar(one_eps[:], one_eps[:], 1.0, None, ALU.add))
            for b in range(NB):
                dve.scalar_tensor_tensor(h[:, b, :], k.x3[:, b, :], one_eps[:], h[:, b, :], ALU.mult, ALU.add).then_inc(h_ready, 1)
            dve.wait_ge(rows_loaded, 48)
            for b in range(NB):
                dve.wait_ge(wide_done, b + 1)
                dve.tensor_tensor(wide[:, b, :].rearrange("p (o n) -> p o n", o=2), k.bank[:, 4 + 2 * (b % 2):6 + 2 * (b % 2), :],
                                  bias[:].rearrange("p (o n) -> p o n", o=2), ALU.add).then_inc(wide_added, 1)
                dve.wait_ge(wide_added, b + 1)
                norm.stats(dve, me, b, wide[:, b, 0:D], wide[:, b, D:D2])
            norm.variance(dve, me, var_ready)
            dve.wait_ge(dev_ready, 1)
            norm.invert(dve, me)
            for b in range(NB):
                norm.affine(dve, me, b, wide[:, b, :], gain[:], shift[:]).then_inc(scaled, 1)
            dve.wait_ge(scaled, NB)


def narrow(nc, k, a, second, out):
    S, which = nc.alloc_semaphore, "ab"[second]
    w_loaded, rows_loaded, done, added = S("w32_loaded" + which), S("rows32_loaded" + which), S("narrow_done" + which), S("narrow_added" + which)
    var_ready, dev_ready, scaled, gelu_done = S("n_var_ready" + which), S("n_dev_ready" + which), S("n_scaled" + which), S("n_gelu" + which)
    result, stored = S("n_result" + which), S("out_stored" + which)
    r = Region(nc, k.wide_end, ARENA_END)
    w = r.take("w32" + which, [P, 2 * KC, D], F32)
    y = r.take("y32" + which, [P, NB, D], F32)
    rows = [r.take(f"row32{which}{j}", [P, D], F32) for j in range(5)]
    norms = [Norm(nc, r, f"norm32{which}{j}", NB) for j in range(2)]
    if second:
        matrix, vectors = a.L3_gnn_M2, (a.L3_gnn_gB, a.L3_gnn_bB)
    else:
        matrix, vectors = a.L3_gnn_W2, (a.L3_gnn_b2, a.L3_gnn_g2, a.L3_gnn_be2, a.L3_gnn_gA, a.L3_gnn_bA)
    with nc.Block() as block:
        @block.sync
        def _(sp):
            sp.dma_start(w[:], matrix.rearrange("(c p) n -> p c n", p=P)).then_inc(w_loaded, 16)
            for row, v in zip(rows, vectors):
                sp.dma_start(row[:], row_of(v)).then_inc(rows_loaded, 16)
            if second:
                for b in range(NB):
                    sp.wait_ge(result, b + 1)
                    n = last_rows(b)
                    sp.dma_start(out[b * P:b * P + n, :], y[0:n, b, :]).then_inc(stored, 16)
                sp.wait_ge(stored, 16 * NB)

        @block.tensor
        def _(pe):
            pe.wait_ge(w_loaded, 16)
            for b in range(NB):
                if b >= 4:
                    pe.wait_ge(added, b - 3)
                for c in range(2 * KC):
                    m = pe.matmul(k.bank[:, b % 4, :], k.wide_t[:, c, b * P:(b + 1) * P], w[:, c, :], start=(c == 0), stop=(c == 2 * KC - 1))
                m.then_inc(done, 1)

        @block.scalar
        def _(act):
            act.wait_ge(var_ready, 1)
            act.sqrt(norms[0].dev[:], norms[0].var[:]).then_inc(dev_ready, 1)
            if not second:
                for b in range(NB):
                    act.wait_ge(scaled, b + 1)
                    act.activation(y[:, b, :], y[:, b, :], ACT.Gelu).then_inc(gelu_done, 1)
            act.wait_ge(var_ready, 2)
            act.sqrt(norms[1].dev[:], norms[1].var[:]).then_inc(dev_ready, 1)

        @block.vector
        def _(dve):
            me = Steps(nc, dve, "narrow_dve" + which)
            dve.wait_ge(rows_loaded, 16 * len(vectors))
            for b in range(NB):
                dve.wait_ge(done, b + 1)
                other = k.agg[:, b, :] if second else rows[0][:]
                dve.tensor_tensor(y[:, b, :], k.bank[:, b % 4, :], other, ALU.add).then_inc(added, 1)
                dve.wait_ge(added, b + 1)
                norms[0].stats(dve, me, b, y[:, b, :])
            norms[0].variance(dve, me, var_ready)
            dve.wait_ge(dev_ready, 1)
            norms[0].invert(dve, me)
            gain, shift = (rows[0], rows[1]) if second else (rows[1], rows[2])
            for b in range(NB):
                norms[0].affine(dve, me, b, y[:, b, :], gain[:], shift[:]).then_inc(scaled, 1)
            for b in range(NB):
                if second:
                    dve.wait_ge(scaled, b + 1)
                else:
                    dve.wait_ge(gelu_done, b + 1)
                me.then(dve.tensor_tensor(y[:, b, :], y[:, b, :], k.x3[:, b, :], ALU.add))
                norms[1].stats(dve, me, b, y[:, b, :])
            norms[1].variance(dve, me, var_ready)
            dve.wait_ge(dev_ready, 2)
            norms[1].invert(dve, me)
            for b in range(NB):
                if second:
                    norms[1].apply(dve, b, y[:, b, :]).then_inc(result, 1)
                else:
                    me.then(dve.scalar_tensor_tensor(k.agg[:, b, :], y[:, b, :], norms[1].mean_var[:, b, 0:1], rows[3][:], ALU.subtract, ALU.mult))
                    dve.scalar_tensor_tensor(k.agg[:, b, :], k.agg[:, b, :], norms[1].dev[:, b:b + 1], rows[4][:], ALU.mult, ALU.add).then_inc(result, 1)
            dve.wait_ge(result, NB)


def widen_again(nc, k, a):
    S = nc.alloc_semaphore
    w_loaded, h_turned, h_copied, done, gelu_done = S("m1_loaded"), S("ha_turned"), S("ha_copied"), S("m_done"), S("m_gelu")
    r = Region(nc, k.wide_end, ARENA_END)
    w = r.take("m1_w", [P, KC, D2], F32)
    ht = r.take("ha_t", [P, KC, NP], F32)
    with nc.Block() as block:
        @block.sync
        def _(sp):
            sp.dma_start(w[:], a.L3_gnn_M1.rearrange("(c p) n -> p c n", p=P)).then_inc(w_loaded, 16)

        @block.tensor
        def _(pe):
            for b in range(NB):
                if b >= 2:
                    pe.wait_ge(h_copied, b - 1)
                for c in range(KC):
                    t = pe.transpose(k.bank[:, b % 2, c * P:(c + 1) * P], k.agg[:, b, c * P:(c + 1) * P], k.ident[:])
                t.then_inc(h_turned, 1)
            pe.wait_ge(w_loaded, 16)
            pe.wait_ge(h_copied, NB)
            for n in range(2 * KC * 3):
                o, c = n // 3, WIDE[n % 3]
                if n >= 6:
                    pe.wait_ge(gelu_done, n - 5)
                for i in range(KC):
                    m = pe.matmul(k.bank[:, 2 + n % 6, 0:C3], w[:, i, o * P:(o + 1) * P], ht[:, i, c:c + C3], start=(i == 0), stop=(i == KC - 1))
                m.then_inc(done, 1)

        @block.scalar
        def _(act):
            for b in range(NB):
                act.wait_ge(h_turned, b + 1)
                act.copy(ht[:, :, b * P:(b + 1) * P], k.bank[:, b % 2, :].rearrange("p (c n) -> p c n", c=KC)).then_inc(h_copied, 1)
            for n in range(2 * KC * 3):
                o, c = n // 3, WIDE[n % 3]
                act.wait_ge(done, n + 1)
                act.activation(k.wide_t[:, o, c:c + C3], k.bank[:, 2 + n % 6, 0:C3], ACT.Gelu).then_inc(gelu_done, 1)
            act.wait_ge(gelu_done, 2 * KC * 3)


class Names:
    pass


def program(nc, a, out):
    k = Names()
    k.slots_dram = nc.dram_tensor("slots_dram", (P * NT, REC), F32).ap()
    k.slots3_dram = nc.dram_tensor("slots3_dram", (P * NT3, REC), F32).ap()
    k.at_dram = nc.dram_tensor("at_dram", (NP, NP), F32).ap()
    k.table_dram = nc.dram_tensor("table_dram", (NP, D), F32).ap()
    k.x1_dram = nc.dram_tensor("x1_dram", (NP, D), F32).ap()
    k.bank = nc.alloc_psum_tensor("bank", [P, 8, 512], F32)
    r = Region(nc, ARENA, ARENA_END)
    k.ident = r.take("ident", [P, P], F32)
    k.before = r.take("before", [P, P], F32)
    k.ones = r.take("ones", [P, P], F32)
    k.node_row = r.take("node_row", [P, NP], F16)
    k.row128 = r.take("row128", [P, P], F16)
    k.row128f = r.take("row128f", [P, P], F32)
    k.groups_row = r.take("groups_row", [P, NG3], F32)
    k.blk = r.take("blk", [1, NG], I32)
    k.slot_dst = r.take("slot_dst", [P, NT], F32)
    k.src_idx = r.take("src_idx", [P, NT], U32)
    k.id_idx = r.take("id_idx", [P, NT], U32)
    k.ident16 = r.take("ident16", [P, P], BF16)
    k.sel = r.take("sel", [3 * H, H, P], BF16)
    k.pad_rows = r.take("pad_rows", [P, 1], F32)
    k.counts = r.take("counts", [P, NB], F32)
    k.deg = r.take("deg", [P, NB], F32)
    k.shared_end = r.at
    k.alpha = r.take("alpha", [P, NB, D], F32)
    k.beta = r.take("beta", [P, NB, D], F32)
    k.rec, k.pos = r.take("rec", [P, EC, REC], F32), r.take("pos", [P, EC], U32)
    k.slot3_src, k.slot3_dst = r.take("slot3_src", [P, NT3], F32), r.take("slot3_dst", [P, NT3], F32)
    k.slot_w = r.take("slot_w", [P, 4, NT3], F32)
    k.place3, k.blk_f = r.take("place3", [1, NG3], I32), r.take("blk_f", [1, NG], F32)
    k.prefilled1 = nc.alloc_semaphore("slots1_prefilled")
    k.beta_end = r.at
    k.acc_c = r.take("acc_c", [P, NB, NP], F32)
    k.acc_a = r.take("acc_a", [P, NB, NP], F32)
    k.acc_end = r.at
    k.tail = ARENA_END - 2 * 2 * NB * NP
    r = Region(nc, k.tail, ARENA_END)
    k.ct = r.take("ct", [P, NB, NP], U16)
    k.mask = r.take("mask", [P, NB, NP], BF16)
    k.x1t = nc.alloc_sbuf_tensor_at("x1t", [P, KC, NP], F32, offset=k.tail - 4 * KC * NP)
    constants(nc, k)
    used = nc.snapshot_sems()
    sort_edges(nc, k, a)
    edge_matrices(nc, k)
    transpose_weights_of_edges(nc, k)
    layer0(nc, k)
    layer1(nc, k, a)
    nc.clear_and_free_semaphores(nc.allocated_since(used))
    nc.all_engine_barrier()
    r = Region(nc, k.shared_end, ARENA_END)
    k.x3 = r.take("x3", [P, NB, D], F32)
    k.x3_end = r.at
    layer2(nc, k, a)
    k.agg = r.take("agg", [P, NB, D], F32)
    k.agg_end = r.at
    edge_messages(nc, k, a)
    widen(nc, k, a)
    k.wide_end = k.agg_end + 4 * 2 * KC * NP
    narrow(nc, k, a, False, None)
    widen_again(nc, k, a)
    narrow(nc, k, a, True, out)
    return k


_INS = ["x", "src", "dst", "edge_attr_128", "edge_weight", "L0_gnn_wc", "L0_gnn_wn", "L0_gnn_bias",
        "L1_gnn_Wq", "L1_gnn_bq", "L1_gnn_Wk", "L1_gnn_Wv", "L1_gnn_Wo", "L1_gnn_bo", "L1_gnn_W1", "L1_gnn_b1",
        "L1_gnn_W2", "L1_gnn_b2", "L1_gnn_g1", "L1_gnn_beta1", "L1_gnn_g2", "L1_gnn_beta2", "L1_gnn_ln_g", "L1_gnn_ln_b",
        "L2_gnn_W", "L2_gnn_b", "L3_gnn_W_edge", "L3_gnn_b_edge", "L3_gnn_eps", "L3_gnn_W1", "L3_gnn_b1", "L3_gnn_g1",
        "L3_gnn_be1", "L3_gnn_W2", "L3_gnn_b2", "L3_gnn_g2", "L3_gnn_be2", "L3_gnn_gA", "L3_gnn_bA", "L3_gnn_M1", "L3_gnn_M2",
        "L3_gnn_gB", "L3_gnn_bB"]


def kernel(**inputs):
    import numpy as np
    import concourse.bacc as bacc
    from concourse.bass_utils import run_bass_kernel_spmd

    nc = bacc.Bacc("TRN2", target_bir_lowering=False, num_devices=1)
    arrays, a = {}, Names()
    for name in _INS:
        array = np.ascontiguousarray(inputs[name])
        array = array.reshape(array.shape or (1,))
        arrays[f"in_{name}"] = array
        a.__dict__[name] = nc.dram_tensor(f"in_{name}", array.shape, mybir.dt.from_np(array.dtype), kind="ExternalInput").ap()
    out = nc.dram_tensor("out_0", (N, D), F32, kind="ExternalOutput").ap()
    program(nc, a, out)
    return run_bass_kernel_spmd(nc, [arrays], core_ids=[0]).results[0]["out_0"]
```

```python
import concourse.bass as bass
from concourse import mybir

F32 = mybir.dt.float32
F32R = mybir.dt.float32r
F16 = mybir.dt.float16
BF16 = mybir.dt.bfloat16
I32 = mybir.dt.int32
U32 = mybir.dt.uint32
U16 = mybir.dt.uint16
ALU = mybir.AluOpType
ACT = mybir.ActivationFunctionType
AX = mybir.AxisListType.X

P = 128
N = 1250
D = 512
E = 40000
NB = -(-N // P)
NP = NB * P
KC = D // P
EC = 320
EP = E // EC
assert EP * EC == E and EP <= P
GT = 4
GE = GT * P
REC = 4
C3 = 417
C4 = 313
W3 = 3 * C3
NK3 = 3 * NB
NG = -(-(E // GE + NB) // 2) * 2
NG3 = -(-(E // GE + NK3) // 2) * 2
NT, NT3 = NG * GT, NG3 * GT
W4 = 4 * C4
HALF = NP // 2
H = 8
DH = D // H
HP = H // 2
FF = 256
LAYERS = 2
ED = 128
D2 = 2 * D
EPS = 1e-5
ARENA, ARENA_END = 16512, 229344
NEVER = -2.0 ** 100


class Steps:

    def __init__(self, nc, eng, sem):
        self.sem, self.eng, self.n = nc.alloc_semaphore(sem) if isinstance(sem, str) else sem, eng, 0

    def mark(self, ins):
        ins.then_inc(self.sem, 1)
        self.n += 1
        return self.n

    def then(self, ins):
        self.eng.wait_ge(self.sem, self.mark(ins))


class Region:

    def __init__(self, nc, start, end):
        self.nc, self.at, self.end = nc, start, end

    def take(self, name, shape, dt):
        size = {F32: 4, F32R: 4, I32: 4, U32: 4, F16: 2, BF16: 2, U16: 2}[dt]
        for n in shape[1:]:
            size *= n
        t = self.nc.alloc_sbuf_tensor_at(name, shape, dt, offset=self.at)
        self.at += -(-size // 32) * 32
        assert self.at <= self.end, (name, self.at, self.end)
        return t


class Norm:

    PIECES = 3

    def __init__(self, nc, r, name, n):
        self.n = n
        self.pieces = r.take(name + "_pieces", [P, n, self.PIECES, 6], F32)
        self.mean_var = r.take(name + "_mean_var", [P, n, 2], F32)
        self.var, self.dev = r.take(name + "_var", [P, n], F32), r.take(name + "_dev", [P, n], F32)

    def stats(self, dve, me, b, *rows):
        for j, piece in enumerate(rows):
            me.mark(dve.bn_stats(self.pieces[:, b, j, :], piece))
        dve.wait_ge(me.sem, me.n)
        me.mark(dve.bn_aggr(self.mean_var[:, b, :], self.pieces[:, b, 0:len(rows), :]))

    def variance(self, dve, me, ready):
        dve.wait_ge(me.sem, me.n)
        dve.tensor_scalar(self.var[:], self.mean_var[:, :, 1], EPS, None, ALU.add).then_inc(ready, 1)

    def invert(self, dve, me):
        me.then(dve.reciprocal(self.dev[:], self.dev[:]))

    def affine(self, dve, me, b, rows, gain, shift):
        me.then(dve.scalar_tensor_tensor(rows, rows, self.mean_var[:, b, 0:1], gain, ALU.subtract, ALU.mult))
        return dve.scalar_tensor_tensor(rows, rows, self.dev[:, b:b + 1], shift, ALU.mult, ALU.add)

    def apply(self, dve, b, rows):
        return dve.tensor_scalar(rows, rows, self.mean_var[:, b, 0:1], self.dev[:, b:b + 1], ALU.subtract, ALU.mult)


def gate(eng, sem, value, passed):
    eng.wait_ge(sem, value)
    eng.sem_inc(passed, 1)


def last_rows(b):
    return min(P, N - b * P)


def row_of(vector):
    return vector.rearrange("(o n) -> o n", o=1).to_broadcast([P, vector.shape[0]])


def constants(nc, k):
    made = nc.alloc_semaphore("const_made")
    with nc.Block() as block:
        @block.gpsimd
        def _(pool):
            pool.memset(k.ident[:], 0.0).then_inc(made, 1)
            pool.memset(k.before[:], 1.0).then_inc(made, 1)
            pool.memset(k.ones[:], 1.0).then_inc(made, 1)
            pool.wait_ge(made, 3)
            pool.affine_select(out=k.ident[:], in_=k.ident[:], compare_op=ALU.not_equal, fill=1.0,
                               base=0, pattern=[[-1, P]], channel_multiplier=1).then_inc(made, 1)
            pool.affine_select(out=k.before[:], in_=k.before[:], compare_op=ALU.is_gt, fill=0.0,
                               base=0, pattern=[[1, P]], channel_multiplier=-1).then_inc(made, 1)
            pool.iota(k.node_row[:], pattern=[[1, NP]], base=0, channel_multiplier=0,
                      allow_small_or_imprecise_dtypes=True).then_inc(made, 1)
            pool.iota(k.row128[:], pattern=[[1, P]], base=0, channel_multiplier=0,
                      allow_small_or_imprecise_dtypes=True).then_inc(made, 1)
            pool.iota(k.row128f[:], pattern=[[1, P]], base=0, channel_multiplier=0,
                      allow_small_or_imprecise_dtypes=True).then_inc(made, 1)
            pool.iota(k.groups_row[:], pattern=[[1, NG3]], base=0, channel_multiplier=0,
                      allow_small_or_imprecise_dtypes=True).then_inc(made, 1)
            pool.iota(k.pad_rows[:], pattern=[[0, 1]], base=0, channel_multiplier=1,
                      allow_small_or_imprecise_dtypes=True).then_inc(made, 1)
            pool.wait_ge(made, 10)
            pool.tensor_copy(k.ident16[:], k.ident[:]).then_inc(made, 1)
            pool.tensor_scalar(k.pad_rows[:], k.pad_rows[:], float(last_rows(NB - 1)), 1.0, ALU.is_ge, ALU.mult).then_inc(made, 1)
            pool.wait_ge(made, 12)


def scatter_edges(pool, S, name, edge_pos, rec, stage, slots_dram, slots, scattered, prefilled):
    st_pos, st_rec = stage
    staged, passed = S(name + "_staged"), S(name + "_passed")

    def scatter(i, u):
        pool.tensor_copy(st_pos[:, u, :], edge_pos[:, bass.ds(i * 16 + 8 * u, 8)]).then_inc(staged, 1)
        pool.tensor_copy(st_rec[:, u, :], rec[:].rearrange("p c w -> p (c w)")[:, bass.ds(i * 64 + 32 * u, 32)]).then_inc(staged, 1)
        gate(pool, staged, i * 4 + 2 * u + 2, passed)
        for c in range(8):
            pool.indirect_dma_start(
                out=slots_dram, out_offset=bass.IndirectOffsetOnAxis(ap=st_pos[:, u, c:c + 1], axis=0),
                in_=st_rec[:, u, REC * c:REC * (c + 1)], in_offset=None,
                bounds_check=slots - 1, oob_is_err=False).then_inc(scattered[u], 16)

    pool.wait_ge(prefilled, 16)
    scatter(0, 0)
    scatter(0, 1)
    with pool.Fori(1, EC // 16) as i:
        for u in range(2):
            gate(pool, scattered[u], i * 128, passed)
            scatter(i, u)
    for u in range(2):
        pool.wait_ge(scattered[u], 8 * EC)


def sort_edges(nc, k, a):
    S = nc.alloc_semaphore
    cleared, loaded, prefilled = S("edges_cleared"), S("edges_loaded"), S("slots_prefilled")
    pads_made, totals_ready, offsets_ready, pos_ready = S("pads_made"), S("totals_ready"), S("offsets_ready"), S("pos_ready")
    scattered, read_back = [S(f"scattered3{u}") for u in range(2)], S("read_back3")
    x_loaded, w_loaded, x_transposed, xt_copied = S("x_loaded"), S("w0_loaded"), S("x_transposed"), S("xt_copied")
    dense_done, dense_copied, id_made = S("dense0_done"), S("beta_copied"), S("id_made")
    alpha_done, bias_loaded = S("alpha_done"), S("bias0_loaded")
    r = Region(nc, k.beta_end, ARENA_END)
    xt = r.take("xt_in", [P, KC, NP], F32)
    src_i, dst_i = r.take("src_i", [P, EC], I32), r.take("dst_i", [P, EC], I32)
    bidx, dloc = r.take("bidx", [P, EC], I32), r.take("dloc", [P, EC], I32)
    ew_s, bidx_f = r.take("ew_s", [P, EC], F32), r.take("bidx_f", [P, EC], F32)
    third, bucket3 = r.take("third", [P, EC], F32), r.take("bucket3", [P, EC], F32)
    is_in, one_row = r.take("is_in", [P, NK3, EC], BF16), r.take("one_row", [P, EC], BF16)
    prefix = r.take("prefix", [P, NK3, EC], F32)
    small, small_i = r.take("small", [P, 6, NK3], F32), r.take("small_i", [P, 2, NK3], I32)
    lin, lin_i = r.take("lin", [P, 4, EC], F32), r.take("lin_i", [P, 3, EC], I32)
    pos3 = r.take("pos3", [P, EC], U32)
    stage = r.take("st_pos3", [P, 2, 8], U32), r.take("st_rec3", [P, 2, 8 * REC], F32)
    pads = r.take("pads", [P, NT3, REC], F32)
    slots = r.take("slots3", [P, NT3, REC], F32)
    slot_wb = r.take("slot_wb", [P, NT3], BF16)
    key_f, key_i = r.take("key_f", [P, 3, NG3], F32), r.take("key_i", [P, 2, NG3], I32)
    wc = r.take("wc", [P, KC, D], F32)
    wn = r.take("wn", [P, KC, D], F32)
    bias = r.take("bias0", [P, D], F32)
    ps_off, ps_tot, ps_d = k.bank[:, 4, :], k.bank[:, 5, :], k.bank
    with nc.Block() as block:
        T, OFF, TOT, GRP, GS, M = range(6)

        @block.sync
        def _(sp):
            sp.wait_ge(cleared, 4)
            sp.dma_start(dst_i[0:EP, :], a.dst.rearrange("(p c) -> p c", c=EC)).then_inc(loaded, 16)
            sp.dma_start(src_i[0:EP, :], a.src.rearrange("(p c) -> p c", c=EC)).then_inc(loaded, 16)
            sp.dma_start(ew_s[0:EP, :], a.edge_weight.rearrange("(p c) -> p c", c=EC)).then_inc(loaded, 16)
            whole = (N // P) * P
            sp.dma_start(k.alpha[:, 0:N // P, :], a.x[0:whole, :].rearrange("(b p) f -> p b f", p=P)).then_inc(x_loaded, 16)
            sp.dma_start(k.alpha[0:N - whole, N // P, :], a.x[whole:N, :]).then_inc(x_loaded, 16)
            sp.dma_start(wc[:], a.L0_gnn_wc.rearrange("(c p) n -> p c n", p=P)).then_inc(w_loaded, 16)
            sp.dma_start(wn[:], a.L0_gnn_wn.rearrange("(c p) n -> p c n", p=P)).then_inc(w_loaded, 16)
            sp.dma_start(bias[:], row_of(a.L0_gnn_bias)).then_inc(bias_loaded, 16)
            sp.wait_ge(pads_made, 1)
            sp.dma_start(k.slots3_dram.rearrange("(p t) w -> p (t w)", p=P),
                         pads[:].rearrange("p t w -> p (t w)")).then_inc(prefilled, 16)
            sp.dma_start(k.slots_dram.rearrange("(p t) w -> p (t w)", p=P),
                         pads[:, 0:NT, :].rearrange("p t w -> p (t w)")).then_inc(k.prefilled1, 16)
            for u in range(2):
                sp.wait_ge(scattered[u], 8 * EC)
            sp.dma_start(slots[:].rearrange("p t w -> p (t w)"),
                         k.slots3_dram.rearrange("(p t) w -> p (t w)", p=P)).then_inc(read_back, 16)
            sp.wait_ge(read_back, 16)
            sp.wait_ge(k.prefilled1, 16)

        @block.gpsimd
        def _(pool):
            pool.iota(k.rec[:, :, 3], pattern=[[1, EC]], base=0, channel_multiplier=EC,
                      allow_small_or_imprecise_dtypes=True).then_inc(id_made, 1)
            pool.wait_ge(id_made, 1)
            pool.wait_ge(pos_ready, 1)
            scatter_edges(pool, S, "scatter3", pos3, k.rec, stage, k.slots3_dram, P * NT3, scattered, prefilled)

        @block.vector
        def _(dve):
            me = Steps(nc, dve, "sort_dve")

            def place(bucket, nk, tiles, turn, to):
                def row(j):
                    return small[:, j, 0:nk]

                for b in range(nk):
                    me.mark(dve.tensor_scalar(is_in[:, b, :], bucket[:], float(b), None, ALU.is_equal))
                dve.wait_ge(me.sem, me.n)
                counts = prefix[:, 0:nk, :]
                for b in range(nk):
                    me.mark(dve.tensor_tensor_scan(counts[:, b, :], one_row[:], is_in[:, b, :], 0.0, ALU.mult, ALU.add))
                dve.wait_ge(me.sem, me.n)
                dve.tensor_copy(row(T), counts[:, :, EC - 1]).then_inc(totals_ready, 1)
                dve.wait_ge(offsets_ready, 2 * turn)
                me.mark(dve.tensor_copy(row(OFF), ps_off[:, 0:nk]))
                me.then(dve.tensor_scalar(row(TOT), ps_tot[:, 0:nk], float(GE - 1), None, ALU.add))
                me.then(dve.tensor_copy(small_i[:, 0, 0:nk], row(TOT)))
                me.then(dve.tensor_scalar(small_i[:, 1, 0:nk], small_i[:, 0, 0:nk], GE.bit_length() - 1, None, ALU.arith_shift_right))
                me.then(dve.tensor_copy(row(GRP), small_i[:, 1, 0:nk]))
                me.then(dve.tensor_tensor_scan(row(GS), k.ones[:, 0:nk], row(GRP), 0.0, ALU.mult, ALU.add))
                me.then(dve.tensor_tensor(row(GS), row(GS), row(GRP), ALU.subtract))
                me.then(dve.tensor_scalar(row(M), row(GS), float(GE), -1.0, ALU.mult, ALU.add))
                me.then(dve.tensor_tensor(row(M), row(M), row(OFF), ALU.add))
                me.then(dve.tensor_tensor(counts, counts, row(M).unsqueeze(2).to_broadcast([P, nk, EC]), ALU.add))
                me.then(dve.tensor_tensor(counts, counts, is_in[:, 0:nk, :], ALU.mult))
                me.then(dve.tensor_reduce(lin[:, 0, :], counts.rearrange("p b c -> p c b"), axis=AX, op=ALU.add))
                me.then(dve.tensor_copy(lin_i[:, 0, :], lin[:, 0, :]))
                me.mark(dve.tensor_scalar(lin_i[:, 1, :], lin_i[:, 0, :], P - 1, None, ALU.bitwise_and))
                me.then(dve.tensor_scalar(lin_i[:, 2, :], lin_i[:, 0, :], 7, None, ALU.arith_shift_right))
                me.mark(dve.tensor_copy(lin[:, 1, :], lin_i[:, 1, :]))
                me.then(dve.tensor_copy(lin[:, 2, :], lin_i[:, 2, :]))
                me.mark(dve.scalar_tensor_tensor(lin[:, 3, :], lin[:, 1, :], float(tiles), lin[:, 2, :], ALU.mult, ALU.add))
                me.then(dve.tensor_scalar(lin[:, 0, :], bidx_f[:], float(NB), float(16 * P * NT3), ALU.is_ge, ALU.mult))
                me.then(dve.tensor_tensor(lin[:, 3, :], lin[:, 3, :], lin[:, 0, :], ALU.add))
                return dve.tensor_copy(to[:], lin[:, 3, :])

            dve.memset(dst_i[:], NP).then_inc(cleared, 1)
            dve.memset(src_i[:], 0).then_inc(cleared, 1)
            dve.memset(ew_s[:], 0.0).then_inc(cleared, 1)
            dve.memset(k.alpha[:, NB - 1, :], 0.0).then_inc(cleared, 1)
            me.then(dve.memset(pads[:], 0.0))
            dve.memset(pads[:, :, 1], -1.0).then_inc(pads_made, 1)
            me.mark(dve.memset(one_row[:], 1.0))
            dve.wait_ge(loaded, 48)
            me.mark(dve.tensor_scalar(bidx[:], dst_i[:], 7, None, ALU.arith_shift_right))
            me.mark(dve.tensor_scalar(dloc[:], dst_i[:], P - 1, None, ALU.bitwise_and))
            me.mark(dve.tensor_copy(k.rec[:, :, 0], src_i[:]))
            me.then(dve.tensor_copy(k.rec[:, :, 2], ew_s[:]))
            me.mark(dve.tensor_copy(k.rec[:, :, 1], dloc[:]))
            me.mark(dve.tensor_copy(bidx_f[:], bidx[:]))
            me.then(dve.tensor_scalar(third[:], k.rec[:, :, 0], float(C3), None, ALU.is_ge))
            me.then(dve.scalar_tensor_tensor(third[:], k.rec[:, :, 0], float(2 * C3), third[:], ALU.is_ge, ALU.add))
            me.then(dve.scalar_tensor_tensor(bucket3[:], bidx_f[:], 3.0, third[:], ALU.mult, ALU.add))
            place(bucket3, NK3, NT3, 1, pos3).then_inc(pos_ready, 1)
            key, div, col = key_f[:, 0, :], key_f[:, 1, :], key_f[:, 2, :]
            me.then(dve.tensor_scalar(key, k.groups_row[:], small[:, GS, 1:2], None, ALU.is_ge))
            for b in range(2, NK3):
                me.then(dve.scalar_tensor_tensor(key, k.groups_row[:], small[:, GS, b:b + 1], key, ALU.is_ge, ALU.add))
            me.then(dve.tensor_scalar(div, key, 171.0, None, ALU.mult))
            me.then(dve.tensor_copy(key_i[:, 0, :], div))
            me.then(dve.tensor_scalar(key_i[:, 1, :], key_i[:, 0, :], 9, None, ALU.arith_shift_right))
            me.then(dve.tensor_copy(div, key_i[:, 1, :]))
            me.then(dve.scalar_tensor_tensor(col, div, -3.0, key, ALU.mult, ALU.add))
            me.then(dve.tensor_scalar(col, col, float(C3), None, ALU.mult))
            me.then(dve.scalar_tensor_tensor(key, div, float(NP), col, ALU.mult, ALU.add))
            me.then(dve.tensor_copy(k.place3[:], key[0:1, :]))
            dve.wait_ge(bias_loaded, 16)
            for b in range(NB):
                dve.wait_ge(dense_done, 2 * b + 1)
                me.then(dve.tensor_tensor(k.alpha[:, b, :], ps_d[:, 2 * b % 4, :], k.alpha[:, b, :], ALU.add))
                dve.tensor_tensor(k.alpha[:, b, :], k.alpha[:, b, :], bias[:], ALU.add).then_inc(alpha_done, 1)
            me.then(place(bidx_f, NB, NT, 2, k.pos))
            me.then(dve.tensor_scalar(k.blk_f[:], k.groups_row[0:1, 0:NG], small[0:1, GS, 1:2], None, ALU.is_ge))
            for b in range(2, NB):
                me.then(dve.scalar_tensor_tensor(k.blk_f[:], k.groups_row[0:1, 0:NG], small[0:1, GS, b:b + 1], k.blk_f[:], ALU.is_ge, ALU.add))
            me.then(dve.tensor_copy(k.blk[:], k.blk_f[:]))
            dve.wait_ge(read_back, 16)
            me.mark(dve.tensor_copy(k.slot3_dst[:], slots[:, :, 1]))
            me.mark(dve.tensor_tensor(k.slot3_src[:].rearrange("p (g j) -> p g j", j=GT), slots[:, :, 0].rearrange("p (g j) -> p g j", j=GT),
                                      col.unsqueeze(2).to_broadcast([P, NG3, GT]), ALU.subtract))
            ew = slots[:, :, 2]
            me.then(dve.tensor_copy(slot_wb[:], ew))
            me.then(dve.tensor_copy(k.slot_w[:, 0, :], slot_wb[:]))
            me.then(dve.tensor_tensor(k.slot_w[:, 1, :], ew, k.slot_w[:, 0, :], ALU.subtract))
            me.then(dve.tensor_copy(slot_wb[:], k.slot_w[:, 1, :]))
            me.then(dve.tensor_copy(k.slot_w[:, 3, :], slot_wb[:]))
            me.then(dve.tensor_tensor(k.slot_w[:, 2, :], k.slot_w[:, 1, :], k.slot_w[:, 3, :], ALU.subtract))
            me.then(dve.tensor_copy(k.slot_w[:, 1, :], k.slot_w[:, 3, :]))

        @block.tensor
        def _(pe):
            def offsets(turn, nk):
                pe.wait_ge(totals_ready, turn)
                pe.matmul(ps_off[:, 0:nk], k.before[:], small[:, T, 0:nk], start=True, stop=True).then_inc(offsets_ready, 1)
                pe.matmul(ps_tot[:, 0:nk], k.ones[:, 0:P], small[:, T, 0:nk], start=True, stop=True).then_inc(offsets_ready, 1)

            pe.wait_ge(x_loaded, 32)
            for b in range(NB):
                if b >= 4:
                    pe.wait_ge(xt_copied, b - 3)
                for c in range(KC):
                    t = pe.transpose(ps_d[:, b % 4, c * P:(c + 1) * P], k.alpha[:, b, c * P:(c + 1) * P], k.ident[:])
                t.then_inc(x_transposed, 1)
            offsets(1, NK3)
            pe.wait_ge(w_loaded, 32)
            pe.wait_ge(xt_copied, NB)
            for n in range(2 * NB):
                b, w = n // 2, (wc, wn)[n % 2]
                if n >= 4:
                    pe.wait_ge((alpha_done, dense_copied)[n % 2], (n - 4) // 2 + 1)
                for c in range(KC):
                    m = pe.matmul(ps_d[:, n % 4, :], xt[:, c, b * P:(b + 1) * P], w[:, c, :], start=(c == 0), stop=(c == KC - 1))
                m.then_inc(dense_done, 1)
            offsets(2, NB)

        @block.scalar
        def _(act):
            for b in range(NB):
                act.wait_ge(x_transposed, b + 1)
                act.copy(xt[:, :, b * P:(b + 1) * P], ps_d[:, b % 4, :].rearrange("p (c n) -> p c n", c=KC)).then_inc(xt_copied, 1)
            for b in range(NB):
                act.wait_ge(dense_done, 2 * b + 2)
                act.copy(k.beta[:, b, :], ps_d[:, (2 * b + 1) % 4, :]).then_inc(dense_copied, 1)


def edge_matrices(nc, k):
    S = nc.alloc_semaphore
    acc_cleared, hots_built, chunk_done, added = S("acc_cleared"), S("hots_built"), S("chunk_done"), S("chunk_added")
    weighted, scattered = S("hots_weighted"), [S(f"scattered1{u}") for u in range(2)]
    slots_back, passed = S("slots_back"), S("slots_passed")
    r = Region(nc, k.acc_end, ARENA_END)
    hot_src = r.take("hot_src", [P, 2, GT, C3 + 1], BF16)
    hot_dst = r.take("hot_dst", [P, 2, GT, 4, P], BF16)
    stage = r.take("st_pos", [P, 2, 8], U32), r.take("st_rec", [P, 2, 8 * REC], F32)
    slots = r.take("slots1", [P, NT, REC], F32)
    acc_c, acc_a = (m[:].rearrange("p b n -> p (b n)") for m in (k.acc_c, k.acc_a))
    with nc.Block() as block:
        @block.gpsimd
        def _(pool):
            pool.memset(acc_a, 0.0).then_inc(acc_cleared, 1)
            scatter_edges(pool, S, "scatter1", k.pos, k.rec, stage, k.slots_dram, P * NT, scattered, k.prefilled1)

        @block.sync
        def _(sp):
            for u in range(2):
                sp.wait_ge(scattered[u], 8 * EC)
            sp.dma_start(slots[:].rearrange("p t w -> p (t w)"), k.slots_dram.rearrange("(p t) w -> p (t w)", p=P)).then_inc(slots_back, 16)
            sp.wait_ge(slots_back, 16)

        @block.vector
        def _(dve):
            def build(g, u):
                for j in range(GT):
                    t = g * GT + j
                    dve.tensor_scalar(hot_dst[:, u, j, 0, :], k.row128[:], k.slot3_dst[:, bass.ds(t, 1)], None, ALU.is_equal).then_inc(hots_built, 1)
                for j in range(GT):
                    t = g * GT + j
                    if j < 2:
                        dve.tensor_scalar(hot_dst[:, u, j, 1, :], k.row128[:], k.slot3_dst[:, bass.ds(t, 1)], k.slot_w[:, 0, bass.ds(t, 1)],
                                          ALU.is_equal, ALU.mult)
                    last = dve.tensor_scalar(hot_src[:, u, j, 0:C3], k.node_row[:, 0:C3], k.slot3_src[:, bass.ds(t, 1)], None, ALU.is_equal)
                last.then_inc(hots_built, 1)

            def add(g, u):
                to = dve.value_load(k.place3[0:1, bass.ds(g, 1)], min_val=0, max_val=(NB - 1) * NP + 2 * C3)
                dve.wait_ge(added, g * 2 + 4)
                for c, acc in enumerate((acc_c, acc_a)):
                    dve.wait_ge(chunk_done, g * 2 + c + 5)
                    rows = acc[:, bass.ds(to, C3)]
                    dve.tensor_tensor(rows, k.bank[:, 2 * u + c, 0:C3], rows, ALU.add).then_inc(added, 1)

            dve.memset(acc_c, 0.0).then_inc(added, 4)
            dve.wait_ge(acc_cleared, 1)
            build(0, 0)
            with dve.Fori(0, NG3 // 2 - 1) as i:
                for u in range(2):
                    build(i * 2 + u + 1, 1 - u)
                    add(i * 2 + u, u)
            build(NG3 - 1, 1)
            add(NG3 - 2, 0)
            add(NG3 - 1, 1)
            dve.wait_ge(slots_back, 16)
            dve.tensor_copy(k.slot_dst[:], slots[:, :, 1])
            dve.tensor_copy(k.src_idx[:], slots[:, :, 0])
            dve.tensor_copy(k.id_idx[:], slots[:, :, 3])

        @block.scalar
        def _(act):
            with act.Fori(0, NG3 // 2) as i:
                for u in range(2):
                    g = i * 2 + u
                    act.wait_ge(chunk_done, g * 2 + 2)
                    for j in range(GT):
                        act.wait_ge(hots_built, g * (GT + 1) + j + 1)
                        for q in (1, 2) if j < 2 else (0, 1, 2):
                            last = act.activation(hot_dst[:, u, j, 1 + q, :], hot_dst[:, u, j, 0, :], ACT.Copy,
                                                  scale=k.slot_w[:, q, bass.ds(g * GT + j, 1)])
                    last.then_inc(weighted, 1)

        @block.tensor
        def _(pe):
            pe.sem_inc(chunk_done, 4)
            with pe.Fori(0, NG3 // 2) as i:
                for u in range(2):
                    g = i * 2 + u
                    pe.wait_ge(hots_built, g * (GT + 1) + GT + 1)
                    for c, parts in enumerate(((0,), (1, 2, 3))):
                        pe.wait_ge(added, g * 2 + c + 1)
                        if c:
                            pe.wait_ge(weighted, g + 1)
                        for j in range(GT):
                            for q in parts:
                                m = pe.matmul(k.bank[:, 2 * u + c, 0:C3], hot_dst[:, u, j, q, :], hot_src[:, u, j, 0:C3],
                                              start=(j == 0 and q == parts[0]), stop=(j == GT - 1 and q == parts[-1]))
                        m.then_inc(chunk_done, 1)


def transpose_weights_of_edges(nc, k):
    S = nc.alloc_semaphore
    transposed, copied, stored, summed = S("at_transposed"), S("at_copied"), S("at_stored"), S("deg_summed")
    r = Region(nc, k.acc_end, ARENA_END)
    rows = r.take("at_rows", [P, 2, NP], F32)
    with nc.Block() as block:
        @block.tensor
        def _(pe):
            for s in range(NB):
                if s >= 2:
                    pe.wait_ge(copied, s - 1)
                for b in range(NB):
                    t = pe.transpose(k.bank[:, 4 * (s % 2) + b // 4, b % 4 * P:(b % 4 + 1) * P], k.acc_a[:, b, s * P:(s + 1) * P], k.ident[:])
                t.then_inc(transposed, 1)

        @block.scalar
        def _(act):
            for s in range(NB):
                act.wait_ge(transposed, s + 1)
                if s >= 2:
                    act.wait_ge(stored, 16 * (s - 1))
                act.copy(rows[:, s % 2, 0:2 * 512].rearrange("p (b n) -> p b n", n=512), k.bank[:, 4 * (s % 2):4 * (s % 2) + 2, :])
                act.copy(rows[:, s % 2, 2 * 512:NP], k.bank[:, 4 * (s % 2) + 2, 0:NP - 2 * 512]).then_inc(copied, 1)

        @block.sync
        def _(sp):
            for s in range(NB):
                sp.wait_ge(copied, s + 1)
                sp.dma_start(k.at_dram[s * P:(s + 1) * P, :], rows[:, s % 2, :]).then_inc(stored, 16)
                sp.wait_ge(stored, 16 * (s + 1))

        @block.vector
        def _(dve):
            dve.tensor_reduce(k.deg[:], k.acc_a[:], axis=AX, op=ALU.add).then_inc(summed, 1)
            dve.wait_ge(summed, 1)


def layer0(nc, k):
    S = nc.alloc_semaphore
    ct_transposed, ct_copied, gamma_done, y_done = S("ct_transposed"), S("ct_copied"), S("gamma_done"), S("y0_done")
    inv_ready, var_ready, dev_ready, x1_ready, x1_stored = S("inv0_ready"), S("var0_ready"), S("dev0_ready"), S("x1_ready"), S("x1_stored")
    x1t_done, x1t_copied = S("x1t_transposed"), S("x1t_copied")
    r = Region(nc, k.acc_end - 4 * NB * NP, k.tail - 4 * KC * NP)
    inv = r.take("inv0", [P, NB], F32)
    norm = Norm(nc, r, "norm0", NB)
    y = k.alpha
    with nc.Block() as block:
        @block.tensor
        def _(pe):
            for s in range(NB):
                if s >= 2:
                    pe.wait_ge(ct_copied, s - 1)
                for b in range(NB):
                    t = pe.transpose(k.bank[:, 3 * (s % 2) + b // 4, b % 4 * P:(b % 4 + 1) * P], k.acc_c[:, b, s * P:(s + 1) * P], k.ident[:])
                t.then_inc(ct_transposed, 1)
            for s in range(NB):
                if s >= 2:
                    pe.wait_ge(y_done, s - 1)
                for b in range(NB):
                    m = pe.matmul(k.bank[:, 6 + s % 2, :], k.acc_c[:, b, s * P:(s + 1) * P], k.beta[:, b, :], start=(b == 0), stop=(b == NB - 1))
                m.then_inc(gamma_done, 1)
            pe.wait_ge(ct_copied, NB)
            for b in range(NB):
                pe.wait_ge(x1_ready, b + 1)
                if b >= 4:
                    pe.wait_ge(x1t_copied, b - 3)
                for c in range(KC):
                    t = pe.transpose(k.bank[:, b % 4, c * P:(c + 1) * P], y[:, b, c * P:(c + 1) * P], k.ident[:])
                t.then_inc(x1t_done, 1)

        @block.scalar
        def _(act):
            for s in range(NB):
                act.wait_ge(ct_transposed, s + 1)
                act.copy(k.ct[:, s, 0:2 * 512].rearrange("p (b n) -> p b n", n=512), k.bank[:, 3 * (s % 2):3 * (s % 2) + 2, :])
                act.copy(k.ct[:, s, 2 * 512:NP], k.bank[:, 3 * (s % 2) + 2, 0:NP - 2 * 512]).then_inc(ct_copied, 1)
            act.wait_ge(var_ready, 1)
            act.sqrt(norm.dev[:], norm.var[:]).then_inc(dev_ready, 1)
            for b in range(NB):
                act.wait_ge(x1t_done, b + 1)
                act.copy(k.x1t[:, :, b * P:(b + 1) * P], k.bank[:, b % 4, :].rearrange("p (c n) -> p c n", c=KC)).then_inc(x1t_copied, 1)

        @block.vector
        def _(dve):
            me = Steps(nc, dve, "layer0_dve")
            for b in range(NB):
                me.mark(dve.tensor_scalar(k.mask[:, b, :], k.acc_c[:, b, :], 0.5, NEVER, ALU.is_lt, ALU.mult))
            for s in range(NB):
                dve.wait_ge(ct_copied, s + 1)
                me.mark(dve.tensor_reduce(k.counts[:, s:s + 1], k.ct[:, s, :], axis=AX, op=ALU.add))
            dve.wait_ge(me.sem, me.n)
            me.mark(dve.tensor_copy(inv[:, 0:NB - 1], k.counts[:, 0:NB - 1]))
            me.then(dve.tensor_tensor(inv[:, NB - 1:NB], k.counts[:, NB - 1:NB], k.pad_rows[:], ALU.add))
            me.then(dve.reciprocal(inv[:], inv[:]))
            for s in range(NB):
                dve.wait_ge(gamma_done, s + 1)
                dve.scalar_tensor_tensor(y[:, s, :], k.bank[:, 6 + s % 2, :], inv[:, s:s + 1], y[:, s, :], ALU.mult, ALU.add).then_inc(y_done, 1)
                dve.wait_ge(y_done, s + 1)
                norm.stats(dve, me, s, y[:, s, :])
            norm.variance(dve, me, var_ready)
            dve.wait_ge(dev_ready, 1)
            norm.invert(dve, me)
            for b in range(NB):
                norm.apply(dve, b, y[:, b, :]).then_inc(x1_ready, 1)

        @block.sync
        def _(sp):
            for b in range(NB):
                sp.wait_ge(x1_ready, b + 1)
                sp.dma_start(k.x1_dram[b * P:(b + 1) * P, :], y[:, b, :]).then_inc(x1_stored, 16)
            sp.wait_ge(x1_stored, 16 * NB)


WIDE = (0, C3, 2 * C3)


def turned(pe, k, bank, rows, j, n):
    for o in range(n):
        t = pe.transpose(k.bank[:, bank, o * P:(o + 1) * P], rows[:, o, j * P:(j + 1) * P], k.ident[:])
    return t


def project(nc, k, a, l, at):
    S = at.sem
    w_loaded, w_turned, w_copied = [S(f"wqkv_loaded{j}") for j in range(3)], S("wqkv_turned"), S("wqkv_copied")
    v_loaded, v_turned, v_ready = S("vectors_loaded"), S("vectors_turned"), S("vectors_ready")
    q_done, k_done, val_done = S("q_done"), S("k_done"), S("v_done")
    q_copied, k_copied, val_copied, ones_set = S("q_copied"), S("k_copied"), S("v_copied"), S("v_ones_set")
    cols_done, bq_scaled = S("cols_done"), S("bq_scaled")
    split, saved = S("qk_split"), S("qk_saved")
    r = Region(nc, at.temps, k.tail - 4 * KC * NP)
    w_rows = r.take("wqkv_rows", [P, 2, KC, D], F32)
    w_in = r.take("wqkv_in", [P, 2, KC, D], F32)
    whole = r.take("qk_whole", [P, 2, NP], F32)
    high, low = r.take("qk_high", [P, 2, NP], F32R), r.take("qk_low", [P, 2, NP], F32R)
    weights = (a.L1_gnn_Wq, a.L1_gnn_Wk, a.L1_gnn_Wv)
    with nc.Block() as block:
        @block.sync
        def _(sp):
            row = 0
            for v, n in ((a.L1_gnn_bq, KC), (a.L1_gnn_bo, KC), (a.L1_gnn_g1, KC), (a.L1_gnn_beta1, KC), (a.L1_gnn_b1, FF // P),
                         (a.L1_gnn_b2, KC), (a.L1_gnn_g2, KC), (a.L1_gnn_beta2, KC)):
                sp.dma_start(at.vec_rows[row:row + n, :], v[bass.ds(l, 1), :].rearrange("l (c p) -> (l c) p", p=P)).then_inc(v_loaded, 16)
                row += n
            for j in range(3):
                if j >= 2:
                    sp.wait_ge(w_turned, (j - 1) * KC)
                sp.dma_start(w_rows[:, j % 2, :, :], weights[j][bass.ds(l, 1), :, :].rearrange("l (o p) i -> p (l o) i", p=P)).then_inc(w_loaded[j], 16)
            for n in range(2 * HP):
                sp.wait_ge(split, n + 1)
                sp.dma_start(k.qk_dram[2 * (n // HP), n % HP], high[:, n % 2, :].bitcast(F32)).then_inc(saved, 16)
                sp.dma_start(k.qk_dram[2 * (n // HP) + 1, n % HP], low[:, n % 2, :].bitcast(F32)).then_inc(saved, 16)
                sp.wait_ge(saved, 32 * (n + 1))

        @block.tensor
        def _(pe):
            pe.wait_ge(v_loaded, 16 * 8)
            pe.transpose(k.bank[:, 7, 0:at.NV], at.vec_rows[0:at.NV, :], k.ident[0:at.NV, 0:at.NV]).then_inc(v_turned, 1)

            def turn(j):
                pe.wait_ge(w_loaded[j], 16)
                for c in range(KC):
                    n = j * KC + c
                    if n >= 2:
                        pe.wait_ge(w_copied, n - 1)
                    turned(pe, k, n % 2, w_rows[:, j % 2], c, KC).then_inc(w_turned, 1)

            n = 0
            turn(0)
            for j, done, copied in ((0, q_done, q_copied), (1, k_done, k_copied)):
                turn(j + 1)
                pe.wait_ge(w_copied, (j + 1) * KC)
                for o in range(KC):
                    for c in range(3):
                        if n >= 4:
                            m4 = n - 4
                            pe.wait_ge(q_copied if m4 < 12 else k_copied, m4 % 12 + 1)
                        for i in range(KC):
                            m = pe.matmul(k.bank[:, 2 + n % 4, 0:C3], w_in[:, j % 2, i, o * P:(o + 1) * P],
                                          k.x1t[:, i, WIDE[c]:WIDE[c] + C3], start=(i == 0), stop=(i == KC - 1))
                        m.then_inc(done, 1)
                        n += 1
            pe.wait_ge(w_copied, 3 * KC)
            pe.wait_ge(k_copied, 12)
            for b in range(NB):
                if b >= 4:
                    pe.wait_ge(val_copied, b - 3)
                for i in range(KC):
                    m = pe.matmul(k.bank[:, 2 + b % 4, :], k.x1t[:, i, b * P:(b + 1) * P], w_in[:, 0, i, :], start=(i == 0), stop=(i == KC - 1))
                m.then_inc(val_done, 1)

        @block.scalar
        def _(act):
            def copy_weights(j):
                for c in range(KC):
                    act.wait_ge(w_turned, j * KC + c + 1)
                    if j == 2 and c == 0:
                        act.wait_ge(q_done, 12)
                    act.copy(w_in[:, j % 2, c, :], k.bank[:, (j * KC + c) % 2, :]).then_inc(w_copied, 1)

            copy_weights(0)
            copy_weights(1)
            act.wait_ge(bq_scaled, 1)
            for n in range(12):
                act.wait_ge(q_done, n + 1)
                if n % 3 == 0 and n >= 6:
                    act.wait_ge(split, n // 3 - 1)
                act.activation(whole[:, n // 3 % 2, WIDE[n % 3]:WIDE[n % 3] + C3], k.bank[:, 2 + n % 4, 0:C3], ACT.Identity,
                               bias=at.bq[:, n // 3:n // 3 + 1], scale=DH ** -0.5).then_inc(q_copied, 1)
            copy_weights(2)
            for n in range(12):
                act.wait_ge(k_done, n + 1)
                if n % 3 == 0:
                    act.wait_ge(split, n // 3 + 3)
                act.copy(whole[:, n // 3 % 2, WIDE[n % 3]:WIDE[n % 3] + C3], k.bank[:, 2 + n % 4, 0:C3]).then_inc(k_copied, 1)

        @block.vector
        def _(dve):
            dve.memset(at.val[:, :, :, DH:2 * DH], 1.0).then_inc(ones_set, 1)
            me = Steps(nc, dve, at.sem("project_dve"))
            me.then(dve.memset(whole[:, :, W3:NP], 0.0))
            dve.wait_ge(v_turned, 1)
            dve.tensor_copy(at.vec[:], k.bank[:, 7, 0:at.NV]).then_inc(v_ready, 1)
            dve.wait_ge(v_ready, 1)
            dve.tensor_scalar(at.bq[:], at.vec[:, 0:KC], DH ** -0.5, None, ALU.mult).then_inc(bq_scaled, 1)
            for n in range(2 * HP):
                dve.wait_ge(q_copied if n < HP else k_copied, 3 * (n % HP) + 3)
                if n >= 2:
                    dve.wait_ge(saved, 32 * (n - 1))
                me.then(dve.tensor_copy(high[:, n % 2, :], whole[:, n % 2, :]))
                dve.tensor_tensor(low[:, n % 2, :], whole[:, n % 2, :], high[:, n % 2, :].bitcast(F32), ALU.subtract).then_inc(split, 1)
            for b in range(NB):
                dve.wait_ge(val_done, b + 1)
                heads = k.bank[:, 2 + b % 4, :].rearrange("p (h u d) -> p h u d", u=2, d=DH)
                dve.tensor_copy(at.val[:, b, :, 0:DH], heads[:, :, 0, :])
                dve.tensor_copy(at.val[:, b, :, 2 * DH:3 * DH], heads[:, :, 1, :]).then_inc(val_copied, 1)


CHUNKS = ((0, 512), (512, 512), (1024, NP - 1024))
PIECES = 6
PIECE = -(-W3 // PIECES)
RING = 5


def score_plan():
    plan = [("max", 0, b) for b in range(NB)] + [("turn", 0)]
    for h in range(H):
        b = 0
        for j in range(NB):
            plan.append(("exp", h, j))
            if h + 1 < H and j >= 2:
                for _ in range((2, 2, 2, 2, 1, 1, 0, 0)[j - 2]):
                    plan.append(("max", h + 1, b))
                    b += 1
        if h + 1 < H:
            plan.append(("turn", h + 1))
    return plan


def gather_edge_features(nc, pool, r, k, a, l):
    S = nc.alloc_semaphore
    staged, made, passed = S("ids_staged"), S("parts_made"), S("features_passed")
    got, saved = [S(f"features_got{u}") for u in range(2)], [S(f"features_saved{u}") for u in range(2)]
    idx = r.take("ids", [P, 2, GT], U32)
    rows = r.take("feature_rows", [P, 2, GT * ED], F32)
    parts = r.take("feature_parts", [P, 2, 2, GT * ED], F32R)
    share = NG // LAYERS
    before = l * share

    def gather(i, u):
        g = i * 2 + u
        pool.tensor_copy(idx[:, u, :], k.id_idx[:, bass.ds((before + g) * GT, GT)]).then_inc(staged, 1)
        gate(pool, staged, before + g + 1, passed)
        for j in range(GT):
            pool.indirect_dma_start(out=rows[:, u, j * ED:(j + 1) * ED], out_offset=None, in_=a.edge_attr_128,
                                    in_offset=bass.IndirectOffsetOnAxis(ap=idx[:, u, j:j + 1], axis=0)).then_inc(got[u], 16)

    def split(i, u, first=False):
        g = i * 2 + u
        gate(pool, got[u], before * (8 * GT) + i * (16 * GT) + 16 * GT, passed)
        if not first:
            gate(pool, saved[u], before * 8 + i * 16, passed)
        pool.tensor_copy(parts[:, u, 0, :], rows[:, u, :]).then_inc(made, 1)
        gate(pool, made, before * 2 + g * 2 + 1, passed)
        pool.tensor_tensor(parts[:, u, 1, :], rows[:, u, :], parts[:, u, 0, :].bitcast(F32), ALU.subtract).then_inc(made, 1)
        gate(pool, made, before * 2 + g * 2 + 2, passed)
        pool.dma_start(k.features_dram[bass.ds(l, 1), bass.ds(g * P, P), :].rearrange("l p n -> (l p) n"), parts[:, u, :, :].rearrange("p q n -> p (q n)").bitcast(F32)).then_inc(saved[u], 16)

    gather(0, 0)
    gather(0, 1)
    split(0, 0, True)
    gather(1, 0)
    split(0, 1, True)
    with pool.Fori(1, share // 2 - 1) as i:
        gather(i, 1)
        split(i, 0)
        gather(i + 1, 0)
        split(i, 1)
    last = share // 2 - 1
    gather(last, 1)
    split(last, 0)
    split(last, 1)
    for u in range(2):
        gate(pool, saved[u], before * 8 + 16 * (last + 1), passed)


def attend(nc, k, a, l, at):
    S = at.sem
    loaded, ones_set = [[S(f"tile{u}{j}_loaded") for j in range(6)] for u in range(2)], S("key_ones_set")
    scored, maxed, max_ready, max_turned, max_copied = S("scored"), S("maxed"), S("max_ready"), S("max_turned"), S("max_copied")
    st_done, exp_done, p_ready, pv_done, pv_copied = S("st_done"), S("exp_done"), S("p_ready"), S("pv_done"), S("pv_copied")
    head_done = S("head_done")
    NPT = 3
    r = Region(nc, at.temps, k.tail - 4 * KC * NP)
    keys, queries = r.take("keys", [P, 2, NP], F32R), r.take("queries", [P, 2, NP], F32R)
    keys_more, queries_more = r.take("keys_more", [DH + 3, 2, NP], F32R), r.take("queries_more", [DH + 3, 2, NP], F32R)
    junk = r.take("junk", [P, 2, 512], BF16)
    maxes, m0 = r.take("maxes", [P, NB, 3], F32), r.take("m0", [P, NB], F32)
    m1, m2 = r.take("m1", [P, NB], F32), r.take("m2", [P, NB], F32)
    parts = r.take("m_parts", [P, NB, 3], BF16)
    pt = r.take("pt", [P, NPT, NP], F32)
    raw = r.take("raw", [P, W3], F32)
    inv = r.take("inv_s", [P, PIECE], F32)
    plan = score_plan()
    turns, bank_of = [], {}
    for item in plan:
        for c in range(2 if item[0] == "turn" else 3):
            bank_of[item + (c,)] = len(turns) % RING
            turns.append(item)
    with nc.Block() as block:
        @block.gpsimd
        def _(pool):
            gather_edge_features(nc, pool, r, k, a, l)

        @block.sync
        def _(sp):
            for h in range(H):
                u, p = h % 2, h // 2
                rows = slice(DH * u, DH * (u + 1))
                if h >= 2:
                    sp.wait_ge(st_done, 3 * NB * (h - 1))
                for j, (to, kind) in enumerate(((keys[0:DH, u, :], 2), (keys[DH:P, u, :], 3),
                                                (queries[0:DH, u, :], 0), (queries[DH:P, u, :], 0),
                                                (keys_more[0:DH, u, :], 2), (queries_more[0:DH, u, :], 1))):
                    sp.dma_start(to.bitcast(F32), k.qk_dram[kind, p, rows, :]).then_inc(loaded[u][j], 16)

        @block.tensor
        def _(pe):
            emptied = []
            counts = {"max": 0, "turn": 0, "exp": 0}

            def next_bank(kind):
                if len(emptied) >= RING:
                    pe.wait_ge(*emptied[-RING])
                counts[kind] += 1
                emptied.append(({"max": maxed, "turn": max_copied, "exp": exp_done}[kind], counts[kind]))
                return (len(emptied) - 1) % RING

            def maximum(h, b):
                u = h % 2
                if b == 0:
                    for j in range(6):
                        pe.wait_ge(loaded[u][j], 16 * (h // 2 + 1))
                for at0, wide in CHUNKS:
                    to = k.bank[:, next_bank("max"), 0:wide]
                    pe.matmul(to, queries[:, u, b * P:(b + 1) * P], keys[:, u, at0:at0 + wide], start=True, stop=False)
                    pe.matmul(to, queries_more[0:DH, u, b * P:(b + 1) * P], keys_more[0:DH, u, at0:at0 + wide], start=False, stop=True).then_inc(scored, 1)

            def turn(h):
                pe.wait_ge(max_ready, h + 1)
                for i in range(2):
                    to = k.bank[0:3, next_bank("turn"), :].bitcast(BF16)
                    for b in range(5):
                        t = pe.transpose(to[:, b * P:(b + 1) * P], parts[:, 5 * i + b, :], k.ident16[:])
                    t.then_inc(max_turned, 1)

            def scores(h, j):
                u = h % 2
                if h == 0 and j == 0:
                    pe.wait_ge(ones_set, 1)
                if j == 0:
                    pe.wait_ge(max_copied, 2 * (h + 1))
                for at0, wide in CHUNKS:
                    to = k.bank[:, next_bank("exp"), 0:wide]
                    pe.matmul(to, keys[:, u, j * P:(j + 1) * P], queries[:, u, at0:at0 + wide], start=True, stop=False)
                    pe.matmul(to, keys_more[:, u, j * P:(j + 1) * P], queries_more[:, u, at0:at0 + wide], start=False, stop=False)
                    for b in range(wide // P):
                        m = pe.matmul(to[:, b * P:(b + 1) * P], k.mask[:, at0 // P + b, j * P:(j + 1) * P], k.ident16[:],
                                      start=False, stop=(b == wide // P - 1))
                    m.then_inc(st_done, 1)

            def values(n):
                h, j = n // NB, n % NB
                pe.wait_ge(p_ready, n + 1)
                if j == 0 and h:
                    pe.wait_ge(pv_copied, h)
                for c in range(3):
                    m = pe.matmul(k.bank[:, RING + c, 0:C3], at.val[:, j, h // 2, h % 2 * DH:(h % 2 + 2) * DH], pt[:, n % NPT, c * C3:(c + 1) * C3],
                                  start=(j == 0), stop=(j == NB - 1))
                m.then_inc(pv_done, 1)

            for item in plan:
                if item[0] == "max":
                    maximum(*item[1:])
                elif item[0] == "turn":
                    turn(item[1])
                else:
                    scores(*item[1:])
                    n = item[1] * NB + item[2]
                    if n >= 2:
                        values(n - 2)
            values(H * NB - 2)
            values(H * NB - 1)

        @block.scalar
        def _(act):
            def copy_out(h):
                act.wait_ge(pv_done, NB * (h + 1))
                if h:
                    act.wait_ge(head_done, PIECES * h)
                act.copy(raw[:].rearrange("p (c n) -> p c n", c=3), k.bank[:, RING:RING + 3, 0:C3]).then_inc(pv_copied, 1)

            for n in range(H * NB):
                if n >= NPT:
                    act.wait_ge(pv_done, n - NPT + 1)
                for c, (at0, wide) in enumerate(CHUNKS):
                    act.wait_ge(st_done, 3 * n + c + 1)
                    act.activation(pt[:, n % NPT, at0:at0 + wide], k.bank[:, bank_of["exp", n // NB, n % NB, c], 0:wide], ACT.Exp).then_inc(exp_done, 1)
                if n % NB == 1 and n > NB:
                    copy_out(n // NB - 1)
            copy_out(H - 1)

        @block.vector
        def _(dve):
            me = Steps(nc, dve, at.sem("attend_dve"))
            dve.memset(keys_more[DH:DH + 3, :, :].bitcast(F32), 1.0).then_inc(ones_set, 1)
            taken = [0]

            def maximum(h, b):
                for c, (at0, wide) in enumerate(CHUNKS):
                    n = taken[0] = taken[0] + 1
                    dve.wait_ge(scored, n)
                    if n > 2:
                        dve.wait_ge(maxed, n - 2)
                    dve.tensor_tensor_reduce(out=junk[:, n % 2, 0:wide], in0=k.bank[:, bank_of["max", h, b, c], 0:wide],
                                             in1=k.mask[:, b, at0:at0 + wide], scale=1.0, scalar=NEVER, op0=ALU.add, op1=ALU.max,
                                             accum_out=maxes[:, b, c:c + 1]).then_inc(maxed, 1)

            def negate(h):
                dve.wait_ge(maxed, 3 * NB * (h + 1))
                me.then(dve.tensor_reduce(m0[:], maxes[:], axis=AX, op=ALU.max))
                me.then(dve.tensor_scalar(m1[:], m0[:], -1.0, None, ALU.mult))
                for q in range(3):
                    last = dve.tensor_copy(parts[:, :, q], m1[:])
                    if q < 2:
                        me.then(last)
                        me.then(dve.tensor_copy(m2[:], parts[:, :, q]))
                        me.then(dve.tensor_tensor(m1[:], m1[:], m2[:], ALU.subtract))
                last.then_inc(max_ready, 1)

            def copy_maxima(h):
                for i in range(2):
                    dve.wait_ge(max_turned, 2 * h + i + 1)
                    dve.tensor_copy(queries_more[DH:DH + 3, h % 2, i * 5 * P:(i + 1) * 5 * P], k.bank[0:3, bank_of["turn", h, i], :].bitcast(BF16)[:, 0:5 * P]).then_inc(max_copied, 1)

            def finish(h, c):
                at0, at1 = c * PIECE, min((c + 1) * PIECE, W3)
                dve.wait_ge(pv_copied, h + 1)
                v0 = DH * (h % 2)
                s0 = DH - v0
                if PIECES * h + c:
                    dve.wait_ge(head_done, PIECES * h + c)
                me.then(dve.tensor_scalar(inv[v0:v0 + DH, 0:at1 - at0], raw[s0:s0 + DH, at0:at1], 1e-16, None, ALU.add))
                me.then(dve.reciprocal(inv[v0:v0 + DH, 0:at1 - at0], inv[v0:v0 + DH, 0:at1 - at0]))
                dve.tensor_tensor(at.agg[v0:v0 + DH, h // 2, at0:at1], raw[v0:v0 + DH, at0:at1], inv[v0:v0 + DH, 0:at1 - at0], ALU.mult).then_inc(head_done, 1)

            def count(n):
                dve.wait_ge(exp_done, 3 * n + 3)
                dve.tensor_tensor(pt[:, n % NPT, :], pt[:, n % NPT, :], k.ct[:, n % NB, :], ALU.mult).then_inc(p_ready, 1)

            for item in plan:
                if item[0] == "max":
                    maximum(*item[1:])
                    if item[2] == NB - 1:
                        negate(item[1])
                elif item[0] == "turn":
                    copy_maxima(item[1])
                else:
                    _, h, j = item
                    n = h * NB + j
                    if n:
                        count(n - 1)
                    if 3 <= j < 3 + PIECES and h:
                        finish(h - 1, j - 3)
            count(H * NB - 1)
            for c in range(PIECES):
                finish(H - 1, c)


def finish_layer(nc, k, a, l, at):
    S = at.sem
    w_loaded, w_turned, w_copied = [S(f"wo12_loaded{j}") for j in range(3)], S("wo12_turned"), S("wo12_copied")
    o_done, o_added, f_done, f_added, h_done, h_copied = S("o_done"), S("o_added"), S("f_done"), S("f_added"), S("h_done"), S("h_copied")
    var_ready, dev_ready, x_ready = S("bn_var_ready"), S("bn_dev_ready"), S("bn_x_ready")
    r = Region(nc, at.temps, k.tail - 4 * KC * NP)
    rows = r.take("wo12_rows", [P, KC, D], F32)
    wo = r.take("wo_in", [P, KC, D], F32)
    w1 = r.take("w1_in", [P, KC, FF], F32)
    w2 = r.take("w2_in", [P, FF // P, D], F32)
    norm = Norm(nc, r, "bn", KC)
    scale, shift = r.take("bn_scale", [P, KC], F32), r.take("bn_shift", [P, KC], F32)
    hid = r.take("hidden", [P, FF // P, NP], F32)
    FP = FF // P
    turns = [(0, c, KC, wo[:, c, :]) for c in range(KC)] + [(1, c, FP, w1[:, c, :]) for c in range(KC)] + [(2, c, KC, w2[:, c, :]) for c in range(FP)]
    with nc.Block() as block:
        @block.sync
        def _(sp):
            for j, (w, n, m) in enumerate(((a.L1_gnn_Wo, KC, D), (a.L1_gnn_W1, FP, D), (a.L1_gnn_W2, KC, FF))):
                if j:
                    sp.wait_ge(w_turned, 4 * j)
                sp.dma_start(rows[:, 0:n, 0:m], w[bass.ds(l, 1), :, :].rearrange("l (o p) i -> p (l o) i", p=P)).then_inc(w_loaded[j], 16)

        @block.tensor
        def _(pe):
            for n, (j, c, o, to) in enumerate(turns):
                if c == 0:
                    pe.wait_ge(w_loaded[j], 16)
                if n >= 2:
                    pe.wait_ge(w_copied, n - 1)
                turned(pe, k, n % 2, rows, c, o).then_inc(w_turned, 1)
            pe.wait_ge(w_copied, len(turns))
            n = 0

            def product(w, x, inputs, outputs, done, free):
                nonlocal_n = [0]
                for o in range(outputs):
                    for c in range(3):
                        m = nonlocal_n[0]
                        if m >= 4:
                            pe.wait_ge(free, m - 3)
                        for i in range(inputs):
                            last = pe.matmul(k.bank[:, 2 + m % 4, 0:C3], w[:, i, o * P:(o + 1) * P], x[:, i, WIDE[c]:WIDE[c] + C3],
                                             start=(i == 0), stop=(i == inputs - 1))
                        last.then_inc(done, 1)
                        nonlocal_n[0] += 1

            product(wo, at.agg, KC, KC, o_done, o_added)
            pe.wait_ge(x_ready, KC)
            product(w1, k.x1t, KC, FP, h_done, h_copied)
            pe.wait_ge(h_copied, 3 * FP)
            product(w2, hid, FP, KC, f_done, f_added)

        @block.scalar
        def _(act):
            for n, (j, c, o, to) in enumerate(turns):
                act.wait_ge(w_turned, n + 1)
                act.copy(to, k.bank[:, n % 2, 0:o * P]).then_inc(w_copied, 1)
            act.wait_ge(var_ready, 1)
            act.sqrt(norm.dev[:], norm.var[:]).then_inc(dev_ready, 1)
            for n in range(3 * FP):
                act.wait_ge(h_done, n + 1)
                c = WIDE[n % 3]
                act.activation(hid[:, n // 3, c:c + C3], k.bank[:, 2 + n % 4, 0:C3], ACT.Relu,
                               bias=at.vec[:, at.B1 + n // 3:at.B1 + n // 3 + 1]).then_inc(h_copied, 1)
            act.wait_ge(var_ready, 2)
            act.sqrt(norm.dev[:], norm.var[:]).then_inc(dev_ready, 1)

        @block.vector
        def _(dve):
            me = Steps(nc, dve, at.sem("finish_dve"))

            def add_and_norm(done, added, bias, gain, beta, turn):
                for n in range(3 * KC):
                    o, c = n // 3, WIDE[n % 3]
                    x = k.x1t[:, o, c:c + C3]
                    dve.wait_ge(done, n + 1)
                    dve.scalar_tensor_tensor(x, k.bank[:, 2 + n % 4, 0:C3], at.vec[:, bias + o:bias + o + 1], x, ALU.add, ALU.add).then_inc(added, 1)
                for o in range(KC):
                    dve.wait_ge(added, 3 * o + 3)
                    norm.stats(dve, me, o, *(k.x1t[:, o, c:min(c + C3, N)] for c in WIDE))
                norm.variance(dve, me, var_ready)
                dve.wait_ge(dev_ready, turn)
                norm.invert(dve, me)
                me.then(dve.tensor_tensor(scale[:], norm.dev[:], at.vec[:, gain:gain + KC], ALU.mult))
                me.then(dve.tensor_tensor(shift[:], norm.mean_var[:, :, 0], scale[:], ALU.mult))
                me.then(dve.tensor_tensor(shift[:], at.vec[:, beta:beta + KC], shift[:], ALU.subtract))
                for o in range(KC):
                    dve.tensor_scalar(k.x1t[:, o, 0:W3], k.x1t[:, o, 0:W3], scale[:, o:o + 1], shift[:, o:o + 1], ALU.mult, ALU.add).then_inc(x_ready, 1)

            add_and_norm(o_done, o_added, at.BO, at.G1, at.BETA1, 1)
            add_and_norm(f_done, f_added, at.B2, at.G2, at.BETA2, 2)
            dve.wait_ge(x_ready, 2 * KC)


def layer1(nc, k, a):
    at = Names()
    at.sems = []

    def sem(name):
        at.sems.append(nc.alloc_semaphore(name))
        return at.sems[-1]

    at.sem = sem
    at.BO, at.G1, at.BETA1, at.B1, at.B2, at.G2, at.BETA2, at.NV = 4, 8, 12, 16, 18, 22, 26, 30
    r = Region(nc, k.shared_end, k.tail - 4 * KC * NP)
    at.agg = r.take("agg_t", [P, HP, NP], F32)
    at.val = r.take("val", [P, NB, HP, 3 * DH], F32)
    at.vec_rows = r.take("vec_rows", [at.NV, P], F32)
    at.vec = r.take("vec", [P, at.NV], F32)
    at.bq = r.take("bq8", [P, KC], F32)
    at.temps = r.at
    with nc.Fori(0, LAYERS) as l:
        project(nc, k, a, l, at)
        attend(nc, k, a, l, at)
        finish_layer(nc, k, a, l, at)
        with nc.Block() as block:
            @block.gpsimd
            def _(pool):
                for s in at.sems:
                    pool.sem_clear(s)


def layer2(nc, k, a):
    S = nc.alloc_semaphore
    turned_back, z_copied, x1_loaded, rows_loaded, w_loaded, at_loaded = (
        S("l1_turned_back"), S("z_copied"), S("x1_loaded"), [S(f"rows2_loaded{j}") for j in range(4)], S("w2_loaded"), S("at_loaded"))
    var_ready, dev_ready, x2_ready, x2t_done, x2t_copied = S("l2_var_ready"), S("l2_dev_ready"), S("x2_ready"), S("x2t_done"), S("x2t_copied")
    deg_ready, deg_root = S("deg_ready"), S("deg_root")
    x1b_ready, x2b_ready, h_done, h_scaled, sum_done, y_done = (
        S("x1b_ready"), S("x2b_ready"), S("l2_h_done"), S("l2_h_scaled"), S("l2_sum_done"), S("l2_y_done"))
    x3_ready, table_ready, table_stored = S("x3_ready"), S("table_ready"), S("table_stored")
    r = Region(nc, k.x3_end, k.tail - 4 * KC * NP)
    z = r.take("z", [P, NB, D], F32)
    xt = r.take("x2t", [P, KC, NP], F32)
    h = r.take("h_scaled", [P, NB, D], F32)
    w = r.take("w_l2", [P, KC, D], F32)
    part = r.take("l2_part", [P, 2, D], F32)
    gain, shift, bias, b_edge = (r.take(n, [P, D], F32) for n in ("ln_g_row", "ln_b_row", "l2_b_row", "b_edge_row"))
    dinv, has, root = r.take("dinv", [P, NB], F32), r.take("has_deg", [P, NB], F32), r.take("deg_dev", [P, NB], F32)
    norms = [Norm(nc, r, f"norm2{j}", NB) for j in range(3)]
    x = k.x3
    weights = Region(nc, k.tail, ARENA_END).take("at", [P, NB, NP], F32)
    with nc.Block() as block:
        @block.sync
        def _(sp):
            sp.dma_start(x[:], k.x1_dram.rearrange("(b p) f -> p b f", p=P)).then_inc(x1_loaded, 16)
            for j, (row, v) in enumerate(((shift, a.L1_gnn_ln_b), (gain, a.L1_gnn_ln_g), (bias, a.L2_gnn_b), (b_edge, a.L3_gnn_b_edge))):
                sp.dma_start(row[:], row_of(v)).then_inc(rows_loaded[j], 16)
            sp.dma_start(w[:], a.L2_gnn_W.rearrange("(c p) n -> p c n", p=P)).then_inc(w_loaded, 16)
            sp.dma_start(weights[:], k.at_dram.rearrange("(b p) n -> p b n", p=P)).then_inc(at_loaded, 16)
            for b in range(NB):
                sp.wait_ge(table_ready, b + 1)
                sp.dma_start(k.table_dram[b * P:(b + 1) * P, :], z[:, b, :]).then_inc(table_stored, 16)
            sp.wait_ge(table_stored, 16 * NB)

        @block.gpsimd
        def _(pool):
            pool.wait_ge(x1_loaded, 16)
            pool.wait_ge(rows_loaded[0], 16)
            for b in range(NB):
                pool.tensor_tensor(x[:, b, :], x[:, b, :], shift[:], ALU.add).then_inc(x1b_ready, 1)
            pool.wait_ge(rows_loaded[2], 16)
            for b in range(NB):
                pool.wait_ge(x2_ready, b + 1)
                pool.tensor_tensor(x[:, b, :], z[:, b, :], bias[:], ALU.add).then_inc(x2b_ready, 1)
            pool.wait_ge(rows_loaded[3], 16)
            for b in range(NB):
                pool.wait_ge(x3_ready, b + 1)
                pool.tensor_tensor(z[:, b, :], x[:, b, :], b_edge[:], ALU.add).then_inc(table_ready, 1)

        @block.tensor
        def _(pe):
            for b in range(NB):
                if b >= 4:
                    pe.wait_ge(z_copied, b - 3)
                for c in range(KC):
                    t = pe.transpose(k.bank[:, b % 4, c * P:(c + 1) * P], k.x1t[:, c, b * P:(b + 1) * P], k.ident[:])
                t.then_inc(turned_back, 1)
            for b in range(NB):
                pe.wait_ge(x2_ready, b + 1)
                if b >= 4:
                    pe.wait_ge(x2t_copied, b - 3)
                for c in range(KC):
                    t = pe.transpose(k.bank[:, b % 4, c * P:(c + 1) * P], z[:, b, c * P:(c + 1) * P], k.ident[:])
                t.then_inc(x2t_done, 1)
            pe.wait_ge(w_loaded, 16)
            for b in range(NB):
                pe.wait_ge(x2t_copied, b + 1)
                if b >= 2:
                    pe.wait_ge(h_scaled, b - 1)
                for c in range(KC):
                    m = pe.matmul(k.bank[:, 4 + b % 2, :], xt[:, c, b * P:(b + 1) * P], w[:, c, :], start=(c == 0), stop=(c == KC - 1))
                m.then_inc(h_done, 1)
            pe.wait_ge(at_loaded, 16)
            pe.wait_ge(h_scaled, NB)
            for b in range(NB):
                if b >= 2:
                    pe.wait_ge(y_done, b - 1)
                for s in range(NB):
                    m = pe.matmul(k.bank[:, 6 + b % 2, :], weights[:, s, b * P:(b + 1) * P], h[:, s, :], start=(s == 0), stop=(s == NB - 1))
                m.then_inc(sum_done, 1)

        @block.scalar
        def _(act):
            for b in range(NB):
                act.wait_ge(turned_back, b + 1)
                act.copy(z[:, b, :], k.bank[:, b % 4, :]).then_inc(z_copied, 1)
            act.wait_ge(deg_ready, 1)
            act.sqrt(root[:], root[:]).then_inc(deg_root, 1)
            for j in range(2):
                act.wait_ge(var_ready, j + 1)
                act.sqrt(norms[j].dev[:], norms[j].var[:]).then_inc(dev_ready, 1)
            for b in range(NB):
                act.wait_ge(x2t_done, b + 1)
                act.copy(xt[:, :, b * P:(b + 1) * P], k.bank[:, b % 4, :].rearrange("p (c n) -> p c n", c=KC)).then_inc(x2t_copied, 1)
            act.wait_ge(var_ready, 3)
            act.sqrt(norms[2].dev[:], norms[2].var[:]).then_inc(dev_ready, 1)

        @block.vector
        def _(dve):
            me = Steps(nc, dve, "layer2_dve")
            me.then(dve.tensor_scalar(root[:], k.deg[:], 1.0, None, ALU.add))
            me.then(dve.tensor_scalar(has[:], root[:], 0.0, None, ALU.is_gt))
            dve.tensor_scalar(root[:], root[:], 1e-30, None, ALU.max).then_inc(deg_ready, 1)
            for b in range(NB):
                dve.wait_ge(z_copied, b + 1)
                norms[0].stats(dve, me, b, z[:, b, :])
            norms[0].variance(dve, me, var_ready)
            dve.wait_ge(deg_root, 1)
            me.then(dve.reciprocal(dinv[:], root[:]))
            me.then(dve.tensor_tensor(dinv[:], dinv[:], has[:], ALU.mult))
            dve.wait_ge(dev_ready, 1)
            norms[0].invert(dve, me)
            dve.wait_ge(rows_loaded[1], 16)
            for b in range(NB):
                dve.wait_ge(x1b_ready, b + 1)
                me.then(norms[0].affine(dve, me, b, z[:, b, :], gain[:], x[:, b, :]))
                norms[1].stats(dve, me, b, z[:, b, :])
            norms[1].variance(dve, me, var_ready)
            dve.wait_ge(dev_ready, 2)
            norms[1].invert(dve, me)
            for b in range(NB):
                norms[1].apply(dve, b, z[:, b, :]).then_inc(x2_ready, 1)
            for b in range(NB):
                dve.wait_ge(h_done, b + 1)
                dve.tensor_scalar(h[:, b, :], k.bank[:, 4 + b % 2, :], dinv[:, b:b + 1], None, ALU.mult).then_inc(h_scaled, 1)
            for b in range(NB):
                dve.wait_ge(sum_done, b + 1)
                dve.wait_ge(h_scaled, b + 1)
                dve.tensor_tensor(part[:, b % 2, :], k.bank[:, 6 + b % 2, :], h[:, b, :], ALU.add).then_inc(y_done, 1)
                dve.wait_ge(y_done, b + 1)
                dve.wait_ge(x2b_ready, b + 1)
                me.then(dve.scalar_tensor_tensor(x[:, b, :], part[:, b % 2, :], dinv[:, b:b + 1], x[:, b, :], ALU.mult, ALU.add))
                norms[2].stats(dve, me, b, x[:, b, :])
            norms[2].variance(dve, me, var_ready)
            dve.wait_ge(dev_ready, 3)
            norms[2].invert(dve, me)
            for b in range(NB):
                norms[2].apply(dve, b, x[:, b, :]).then_inc(x3_ready, 1)


WHOLE = (0,)
SPLIT = [j for j in range(GT) if j not in WHOLE]


def edge_messages(nc, k, a):
    S = nc.alloc_semaphore
    w_loaded, staged, got_x, got_e = S("we_loaded"), S("idx_staged"), [S(f"got_x{u}") for u in range(2)], [S(f"got_e{u}") for u in range(2)]
    passed, turned_e, e_copied, emb_done, added_x, relu_done = S("msg_pool_passed"), S("e_turned"), S("e_copied"), S("emb_done"), S("added_x"), S("relu_done")
    low_done, w_split = S("low_done"), S("we_split")
    hot_ready, summed, agg_added = S("hot_ready"), S("msgs_summed"), S("agg_added")
    r = Region(nc, k.agg_end, ARENA_END)
    idx = r.take("st_idx", [P, 2, GT], U32)
    xg = r.take("x_got", [P, 2, GT, D], F32)
    ea = r.take("edge_got", [P, 2, 2, GT, ED], F32R)
    et = r.take("edge_turned", [P, 2, 2, GT * P], F32R)
    msg = r.take("msg", [P, GT, D], F32)
    high, low = r.take("msg_high", [P, 2, len(SPLIT), D], F32R), r.take("msg_low", [P, 2, len(SPLIT), D], F32R)
    whole = r.take("msg_whole", [P, 2, len(WHOLE), D], F32)
    hot = r.take("hot_t", [P, 2, GT, P], F32R)
    we = r.take("w_edge", [ED, D], F32)
    w_high, w_low = r.take("w_edge_high", [ED, D], F32R), r.take("w_edge_low", [ED, D], F32R)
    ident_r = r.take("ident_r", [P, P], F32R)
    agg = k.agg[:].rearrange("p b f -> p (b f)")
    features = k.features_dram.rearrange("l p n -> (l p) n")
    with nc.Block() as block:
        @block.sync
        def _(sp):
            def load(i, u):
                sp.dma_start(ea[:, u].rearrange("p q j n -> p (q j n)").bitcast(F32),
                             features[bass.ds((i * 2 + u) * P, P), :]).then_inc(got_e[u], 16)

            sp.dma_start(we[:], a.L3_gnn_W_edge).then_inc(w_loaded, 16)
            load(0, 0)
            load(0, 1)
            with sp.Fori(1, NG // 2) as i:
                for u in range(2):
                    sp.wait_ge(turned_e, (i * 2 + u) * 2 - 2)
                    load(i, u)

        @block.gpsimd
        def _(pool):
            with pool.Fori(0, NG // 2) as i:
                for u in range(2):
                    g = i * 2 + u
                    gate(pool, added_x, (g + 1) * GT, passed)
                    pool.tensor_copy(idx[:, u, :], k.src_idx[:, bass.ds(g * GT, GT)]).then_inc(staged, 1)
                    gate(pool, staged, g + 1, passed)
                    for j in range(GT):
                        pool.indirect_dma_start(out=xg[:, u, j, :], out_offset=None, in_=k.table_dram,
                                                in_offset=bass.IndirectOffsetOnAxis(ap=idx[:, u, j:j + 1], axis=0)).then_inc(got_x[u], 16)

        @block.tensor
        def _(pe):
            def turn(i, u):
                pe.wait_ge(got_e[u], i * 16 + 16)
                for q in range(2):
                    for j in range(GT):
                        t = pe.matmul(k.bank[:, q, j * P:(j + 1) * P], ea[:, u, q, j, :], ident_r[:], start=True, stop=True)
                    t.then_inc(turned_e, 1)

            def embed(i, u):
                g = i * 2 + u
                pe.wait_ge(e_copied, g * 2 + 2)
                for j in range(GT):
                    pe.wait_ge(added_x, g * GT + GT + j + 1)
                    to, at = k.bank[:, 2 + j, :], slice(j * P, (j + 1) * P)
                    pe.matmul(to, et[:, u, 0, at], w_high[:], start=True, stop=False)
                    pe.matmul(to, et[:, u, 0, at], w_low[:], start=False, stop=False)
                    pe.matmul(to, et[:, u, 1, at], w_high[:], start=False, stop=True).then_inc(emb_done, 1)

            def collect(i, u):
                g = i * 2 + u
                pe.wait_ge(hot_ready, g + 1)
                pe.wait_ge(agg_added, g + 1)
                for j in range(GT):
                    if j in WHOLE:
                        pe.wait_ge(relu_done, g * GT + j + 1)
                        m = pe.matmul(k.bank[:, 6 + u, :], hot[:, u, j, :].bitcast(F32), whole[:, u, WHOLE.index(j), :], start=(j == 0), stop=(j == GT - 1))
                    else:
                        pe.wait_ge(low_done, g * len(SPLIT) + SPLIT.index(j) + 1)
                        pe.matmul(k.bank[:, 6 + u, :], hot[:, u, j, :], high[:, u, SPLIT.index(j), :], start=(j == 0), stop=False)
                        m = pe.matmul(k.bank[:, 6 + u, :], hot[:, u, j, :], low[:, u, SPLIT.index(j), :], start=False, stop=(j == GT - 1))
                m.then_inc(summed, 1)

            pe.wait_ge(w_split, 3)
            turn(0, 0)
            embed(0, 0)
            turn(0, 1)
            with pe.Fori(0, NG // 2 - 1) as i:
                embed(i, 1)
                turn(i + 1, 0)
                collect(i, 0)
                embed(i + 1, 0)
                turn(i + 1, 1)
                collect(i, 1)
            embed(NG // 2 - 1, 1)
            collect(NG // 2 - 1, 0)
            collect(NG // 2 - 1, 1)

        @block.scalar
        def _(act):
            def copy_turned(i, u, first=False):
                g = i * 2 + u
                if not first:
                    act.wait_ge(emb_done, (g - 1) * GT)
                for q in range(2):
                    act.wait_ge(turned_e, g * 2 + q + 1)
                    act.copy(et[:, u, q, :], k.bank[:, q, :]).then_inc(e_copied, 1)

            def relu(i, u, first=False):
                g = i * 2 + u
                if not first:
                    act.wait_ge(summed, g - 1)
                for j in range(GT):
                    act.wait_ge(added_x, g * GT + 2 * GT + j + 1)
                    to = whole[:, u, WHOLE.index(j), :] if j in WHOLE else high[:, u, SPLIT.index(j), :]
                    act.activation(to, msg[:, j, :], ACT.Relu).then_inc(relu_done, 1)

            copy_turned(0, 0, True)
            copy_turned(0, 1, True)
            relu(0, 0, True)
            copy_turned(1, 0)
            relu(0, 1, True)
            copy_turned(1, 1)
            with act.Fori(1, NG // 2 - 1) as i:
                relu(i, 0)
                copy_turned(i + 1, 0)
                relu(i, 1)
                copy_turned(i + 1, 1)
            relu(NG // 2 - 1, 0)
            relu(NG // 2 - 1, 1)

        @block.vector
        def _(dve):
            def lower(g, u, j):
                if j in WHOLE:
                    return
                dve.wait_ge(relu_done, g * GT + j + 1)
                dve.scalar_tensor_tensor(low[:, u, SPLIT.index(j), :], msg[:, j, :], 0.0, high[:, u, SPLIT.index(j), :].bitcast(F32), ALU.max, ALU.subtract).then_inc(low_done, 1)

            def add_x(i, u, first=False):
                g = i * 2 + u
                dve.wait_ge(got_x[u], i * (16 * GT) + 16 * GT)
                for j in range(GT):
                    dve.wait_ge(emb_done, g * GT + j + 1)
                    if not first and j in WHOLE:
                        dve.wait_ge(relu_done, g * GT - GT + j + 1)
                    elif not first:
                        dve.wait_ge(low_done, g * len(SPLIT) - len(SPLIT) + SPLIT.index(j) + 1)
                    dve.tensor_tensor(msg[:, j, :], k.bank[:, 2 + j, :], xg[:, u, j, :], ALU.add).then_inc(added_x, 1)
                    if j >= 2:
                        lower(g, u, j - 2)
                    elif not first:
                        lower(g - 1, 1 - u, j + 2)

            def one_hot(i, u):
                for j in range(GT):
                    last = dve.tensor_scalar(hot[:, u, j, :], k.row128f[:], k.slot_dst[:, bass.ds((i * 2 + u) * GT + j, 1)], None, ALU.is_equal)
                last.then_inc(hot_ready, 1)

            def add_sum(i, u):
                g = i * 2 + u
                to = dve.value_load(k.blk[0:1, bass.ds(g, 1)], min_val=0, max_val=NB - 1) * D
                dve.wait_ge(summed, g + 1)
                dve.wait_ge(agg_added, g + 2)
                rows = agg[:, bass.ds(to, D)]
                dve.tensor_tensor(rows, k.bank[:, 6 + u, :], rows, ALU.add).then_inc(agg_added, 1)

            dve.sem_inc(added_x, 2 * GT)
            dve.memset(agg, 0.0).then_inc(agg_added, 2)
            dve.tensor_copy(ident_r[:], k.ident[:]).then_inc(w_split, 1)
            dve.wait_ge(w_loaded, 16)
            dve.tensor_copy(w_high[:], we[:]).then_inc(w_split, 1)
            dve.wait_ge(w_split, 2)
            dve.tensor_tensor(w_low[:], we[:], w_high[:].bitcast(F32), ALU.subtract).then_inc(w_split, 1)
            one_hot(0, 0)
            add_x(0, 0, True)
            one_hot(0, 1)
            add_x(0, 1)
            with dve.Fori(0, NG // 2 - 1) as i:
                add_sum(i, 0)
                one_hot(i + 1, 0)
                add_x(i + 1, 0)
                add_sum(i, 1)
                one_hot(i + 1, 1)
                add_x(i + 1, 1)
            lower(NG - 1, 1, GT - 2)
            lower(NG - 1, 1, GT - 1)
            add_sum(NG // 2 - 1, 0)
            add_sum(NG // 2 - 1, 1)


def widen(nc, k, a):
    S = nc.alloc_semaphore
    eps_loaded, w_loaded, rows_loaded = S("eps_loaded"), S("w31_loaded"), S("rows31_loaded")
    h_ready, h_turned, h_copied, wide_done, wide_added = S("h3_ready"), S("h3_turned"), S("h3_copied"), S("wide_done"), S("wide_added")
    var_ready, dev_ready, scaled, gelu_done, g_turned, g_copied = (
        S("wide_var_ready"), S("wide_dev_ready"), S("wide_scaled"), S("wide_gelu"), S("wide_turned"), S("wide_copied"))
    r = Region(nc, k.agg_end, ARENA_END)
    k.wide_t = r.take("wide_t", [P, 2 * KC, NP], F32)
    wide = r.take("wide", [P, NB, D2], F32)
    w = r.take("w31", [P, KC, D2], F32)
    bias, gain, shift = (r.take(n, [P, D2], F32) for n in ("b31_row", "g31_row", "be31_row"))
    ht = k.wide_t[:, 0:KC, :]
    one_eps = r.take("one_eps", [P, 1], F32)
    norm = Norm(nc, r, "norm31", NB)
    h = k.agg
    with nc.Block() as block:
        @block.sync
        def _(sp):
            sp.dma_start(one_eps[:], row_of(a.L3_gnn_eps)).then_inc(eps_loaded, 16)
            sp.dma_start(w[:], a.L3_gnn_W1.rearrange("(c p) n -> p c n", p=P)).then_inc(w_loaded, 16)
            for row, v in ((bias, a.L3_gnn_b1), (gain, a.L3_gnn_g1), (shift, a.L3_gnn_be1)):
                sp.dma_start(row[:], row_of(v)).then_inc(rows_loaded, 16)

        @block.tensor
        def _(pe):
            for b in range(NB):
                pe.wait_ge(h_ready, b + 1)
                if b >= 2:
                    pe.wait_ge(h_copied, b - 1)
                for c in range(KC):
                    t = pe.transpose(k.bank[:, b % 2, c * P:(c + 1) * P], h[:, b, c * P:(c + 1) * P], k.ident[:])
                t.then_inc(h_turned, 1)
            pe.wait_ge(w_loaded, 16)
            for b in range(NB):
                pe.wait_ge(h_copied, b + 1)
                if b >= 2:
                    pe.wait_ge(wide_added, b - 1)
                for o in range(2):
                    for c in range(KC):
                        m = pe.matmul(k.bank[:, 4 + 2 * (b % 2) + o, :], ht[:, c, b * P:(b + 1) * P], w[:, c, o * D:(o + 1) * D],
                                      start=(c == 0), stop=(c == KC - 1))
                m.then_inc(wide_done, 1)
            for b in range(NB):
                pe.wait_ge(gelu_done, b + 1)
                if b >= 2:
                    pe.wait_ge(g_copied, b - 1)
                for c in range(2 * KC):
                    t = pe.transpose(k.bank[:, 2 * (b % 2) + c // 4, c % 4 * P:(c % 4 + 1) * P], wide[:, b, c * P:(c + 1) * P], k.ident[:])
                t.then_inc(g_turned, 1)

        @block.scalar
        def _(act):
            for b in range(NB):
                act.wait_ge(h_turned, b + 1)
                act.copy(ht[:, :, b * P:(b + 1) * P], k.bank[:, b % 2, :].rearrange("p (c n) -> p c n", c=KC)).then_inc(h_copied, 1)
            act.wait_ge(var_ready, 1)
            act.sqrt(norm.dev[:], norm.var[:]).then_inc(dev_ready, 1)
            for b in range(NB + 1):
                if b < NB:
                    act.wait_ge(scaled, b + 1)
                    act.activation(wide[:, b, :], wide[:, b, :], ACT.Gelu).then_inc(gelu_done, 1)
                if b:
                    act.wait_ge(g_turned, b)
                    act.copy(k.wide_t[:, :, (b - 1) * P:b * P], k.bank[:, 2 * ((b - 1) % 2):2 * ((b - 1) % 2) + 2, :]
                             .rearrange("p o (c n) -> p (o c) n", c=KC)).then_inc(g_copied, 1)

        @block.vector
        def _(dve):
            me = Steps(nc, dve, "widen_dve")
            dve.wait_ge(eps_loaded, 16)
            me.then(dve.tensor_scalar(one_eps[:], one_eps[:], 1.0, None, ALU.add))
            for b in range(NB):
                dve.scalar_tensor_tensor(h[:, b, :], k.x3[:, b, :], one_eps[:], h[:, b, :], ALU.mult, ALU.add).then_inc(h_ready, 1)
            dve.wait_ge(rows_loaded, 48)
            for b in range(NB):
                dve.wait_ge(wide_done, b + 1)
                dve.tensor_tensor(wide[:, b, :].rearrange("p (o n) -> p o n", o=2), k.bank[:, 4 + 2 * (b % 2):6 + 2 * (b % 2), :],
                                  bias[:].rearrange("p (o n) -> p o n", o=2), ALU.add).then_inc(wide_added, 1)
                dve.wait_ge(wide_added, b + 1)
                norm.stats(dve, me, b, wide[:, b, 0:D], wide[:, b, D:D2])
            norm.variance(dve, me, var_ready)
            dve.wait_ge(dev_ready, 1)
            norm.invert(dve, me)
            for b in range(NB):
                norm.affine(dve, me, b, wide[:, b, :], gain[:], shift[:]).then_inc(scaled, 1)
            dve.wait_ge(scaled, NB)


def narrow(nc, k, a, second, out):
    S, which = nc.alloc_semaphore, "ab"[second]
    w_loaded, rows_loaded, done, added = S("w32_loaded" + which), S("rows32_loaded" + which), S("narrow_done" + which), S("narrow_added" + which)
    var_ready, dev_ready, scaled, gelu_done = S("n_var_ready" + which), S("n_dev_ready" + which), S("n_scaled" + which), S("n_gelu" + which)
    result, stored = S("n_result" + which), S("out_stored" + which)
    r = Region(nc, k.wide_end, ARENA_END)
    w = r.take("w32" + which, [P, 2 * KC, D], F32)
    y = r.take("y32" + which, [P, NB, D], F32)
    rows = [r.take(f"row32{which}{j}", [P, D], F32) for j in range(5)]
    norms = [Norm(nc, r, f"norm32{which}{j}", NB) for j in range(2)]
    if second:
        matrix, vectors = a.L3_gnn_M2, (a.L3_gnn_gB, a.L3_gnn_bB)
    else:
        matrix, vectors = a.L3_gnn_W2, (a.L3_gnn_b2, a.L3_gnn_g2, a.L3_gnn_be2, a.L3_gnn_gA, a.L3_gnn_bA)
    with nc.Block() as block:
        @block.sync
        def _(sp):
            sp.dma_start(w[:], matrix.rearrange("(c p) n -> p c n", p=P)).then_inc(w_loaded, 16)
            for row, v in zip(rows, vectors):
                sp.dma_start(row[:], row_of(v)).then_inc(rows_loaded, 16)
            if second:
                for b in range(NB):
                    sp.wait_ge(result, b + 1)
                    n = last_rows(b)
                    sp.dma_start(out[b * P:b * P + n, :], y[0:n, b, :]).then_inc(stored, 16)
                sp.wait_ge(stored, 16 * NB)

        @block.tensor
        def _(pe):
            pe.wait_ge(w_loaded, 16)
            for b in range(NB):
                if b >= 4:
                    pe.wait_ge(added, b - 3)
                for c in range(2 * KC):
                    m = pe.matmul(k.bank[:, b % 4, :], k.wide_t[:, c, b * P:(b + 1) * P], w[:, c, :], start=(c == 0), stop=(c == 2 * KC - 1))
                m.then_inc(done, 1)

        @block.scalar
        def _(act):
            act.wait_ge(var_ready, 1)
            act.sqrt(norms[0].dev[:], norms[0].var[:]).then_inc(dev_ready, 1)
            if not second:
                for b in range(NB):
                    act.wait_ge(scaled, b + 1)
                    act.activation(y[:, b, :], y[:, b, :], ACT.Gelu).then_inc(gelu_done, 1)
            act.wait_ge(var_ready, 2)
            act.sqrt(norms[1].dev[:], norms[1].var[:]).then_inc(dev_ready, 1)

        @block.vector
        def _(dve):
            me = Steps(nc, dve, "narrow_dve" + which)
            dve.wait_ge(rows_loaded, 16 * len(vectors))
            for b in range(NB):
                dve.wait_ge(done, b + 1)
                other = k.agg[:, b, :] if second else rows[0][:]
                dve.tensor_tensor(y[:, b, :], k.bank[:, b % 4, :], other, ALU.add).then_inc(added, 1)
                dve.wait_ge(added, b + 1)
                norms[0].stats(dve, me, b, y[:, b, :])
            norms[0].variance(dve, me, var_ready)
            dve.wait_ge(dev_ready, 1)
            norms[0].invert(dve, me)
            gain, shift = (rows[0], rows[1]) if second else (rows[1], rows[2])
            for b in range(NB):
                norms[0].affine(dve, me, b, y[:, b, :], gain[:], shift[:]).then_inc(scaled, 1)
            for b in range(NB):
                if second:
                    dve.wait_ge(scaled, b + 1)
                else:
                    dve.wait_ge(gelu_done, b + 1)
                me.then(dve.tensor_tensor(y[:, b, :], y[:, b, :], k.x3[:, b, :], ALU.add))
                norms[1].stats(dve, me, b, y[:, b, :])
            norms[1].variance(dve, me, var_ready)
            dve.wait_ge(dev_ready, 2)
            norms[1].invert(dve, me)
            for b in range(NB):
                if second:
                    norms[1].apply(dve, b, y[:, b, :]).then_inc(result, 1)
                else:
                    me.then(dve.scalar_tensor_tensor(k.agg[:, b, :], y[:, b, :], norms[1].mean_var[:, b, 0:1], rows[3][:], ALU.subtract, ALU.mult))
                    dve.scalar_tensor_tensor(k.agg[:, b, :], k.agg[:, b, :], norms[1].dev[:, b:b + 1], rows[4][:], ALU.mult, ALU.add).then_inc(result, 1)
            dve.wait_ge(result, NB)


def widen_again(nc, k, a):
    S = nc.alloc_semaphore
    w_loaded, h_turned, h_copied, done, gelu_done = S("m1_loaded"), S("ha_turned"), S("ha_copied"), S("m_done"), S("m_gelu")
    r = Region(nc, k.wide_end, ARENA_END)
    w = r.take("m1_w", [P, KC, D2], F32)
    ht = r.take("ha_t", [P, KC, NP], F32)
    with nc.Block() as block:
        @block.sync
        def _(sp):
            sp.dma_start(w[:], a.L3_gnn_M1.rearrange("(c p) n -> p c n", p=P)).then_inc(w_loaded, 16)

        @block.tensor
        def _(pe):
            for b in range(NB):
                if b >= 2:
                    pe.wait_ge(h_copied, b - 1)
                for c in range(KC):
                    t = pe.transpose(k.bank[:, b % 2, c * P:(c + 1) * P], k.agg[:, b, c * P:(c + 1) * P], k.ident[:])
                t.then_inc(h_turned, 1)
            pe.wait_ge(w_loaded, 16)
            pe.wait_ge(h_copied, NB)
            for n in range(2 * KC * 3):
                o, c = n // 3, WIDE[n % 3]
                if n >= 6:
                    pe.wait_ge(gelu_done, n - 5)
                for i in range(KC):
                    m = pe.matmul(k.bank[:, 2 + n % 6, 0:C3], w[:, i, o * P:(o + 1) * P], ht[:, i, c:c + C3], start=(i == 0), stop=(i == KC - 1))
                m.then_inc(done, 1)

        @block.scalar
        def _(act):
            for b in range(NB):
                act.wait_ge(h_turned, b + 1)
                act.copy(ht[:, :, b * P:(b + 1) * P], k.bank[:, b % 2, :].rearrange("p (c n) -> p c n", c=KC)).then_inc(h_copied, 1)
            for n in range(2 * KC * 3):
                o, c = n // 3, WIDE[n % 3]
                act.wait_ge(done, n + 1)
                act.activation(k.wide_t[:, o, c:c + C3], k.bank[:, 2 + n % 6, 0:C3], ACT.Gelu).then_inc(gelu_done, 1)
            act.wait_ge(gelu_done, 2 * KC * 3)


class Names:
    pass


def program(nc, a, out):
    k = Names()
    k.slots_dram = nc.dram_tensor("slots_dram", (P * NT, REC), F32).ap()
    k.slots3_dram = nc.dram_tensor("slots3_dram", (P * NT3, REC), F32).ap()
    k.at_dram = nc.dram_tensor("at_dram", (NP, NP), F32).ap()
    k.table_dram = nc.dram_tensor("table_dram", (NP, D), F32).ap()
    k.qk_dram = nc.dram_tensor("qk_dram", (4, HP, P, NP), F32).ap()
    k.features_dram = nc.dram_tensor("features_dram", (LAYERS, NG // LAYERS * P, 2 * GT * ED), F32).ap()
    k.x1_dram = nc.dram_tensor("x1_dram", (NP, D), F32).ap()
    k.bank = nc.alloc_psum_tensor("bank", [P, 8, 512], F32)
    r = Region(nc, ARENA, ARENA_END)
    k.ident = r.take("ident", [P, P], F32)
    k.before = r.take("before", [P, P], F32)
    k.ones = r.take("ones", [P, P], F32)
    k.node_row = r.take("node_row", [P, NP], F16)
    k.row128 = r.take("row128", [P, P], F16)
    k.row128f = r.take("row128f", [P, P], F32)
    k.groups_row = r.take("groups_row", [P, NG3], F32)
    k.blk = r.take("blk", [1, NG], I32)
    k.slot_dst = r.take("slot_dst", [P, NT], F32)
    k.src_idx = r.take("src_idx", [P, NT], U32)
    k.id_idx = r.take("id_idx", [P, NT], U32)
    k.ident16 = r.take("ident16", [P, P], BF16)
    k.pad_rows = r.take("pad_rows", [P, 1], F32)
    k.counts = r.take("counts", [P, NB], F32)
    k.deg = r.take("deg", [P, NB], F32)
    k.shared_end = r.at
    k.alpha = r.take("alpha", [P, NB, D], F32)
    k.beta = r.take("beta", [P, NB, D], F32)
    k.rec, k.pos = r.take("rec", [P, EC, REC], F32), r.take("pos", [P, EC], U32)
    k.slot3_src, k.slot3_dst = r.take("slot3_src", [P, NT3], F32), r.take("slot3_dst", [P, NT3], F32)
    k.slot_w = r.take("slot_w", [P, 4, NT3], F32)
    k.place3, k.blk_f = r.take("place3", [1, NG3], I32), r.take("blk_f", [1, NG], F32)
    k.prefilled1 = nc.alloc_semaphore("slots1_prefilled")
    k.beta_end = r.at
    k.acc_c = r.take("acc_c", [P, NB, NP], F32)
    k.acc_a = r.take("acc_a", [P, NB, NP], F32)
    k.acc_end = r.at
    k.tail = ARENA_END - 2 * 2 * NB * NP
    r = Region(nc, k.tail, ARENA_END)
    k.ct = r.take("ct", [P, NB, NP], U16)
    k.mask = r.take("mask", [P, NB, NP], BF16)
    k.x1t = nc.alloc_sbuf_tensor_at("x1t", [P, KC, NP], F32, offset=k.tail - 4 * KC * NP)
    constants(nc, k)
    used = nc.snapshot_sems()
    sort_edges(nc, k, a)
    edge_matrices(nc, k)
    transpose_weights_of_edges(nc, k)
    layer0(nc, k)
    layer1(nc, k, a)
    nc.clear_and_free_semaphores(nc.allocated_since(used))
    nc.all_engine_barrier()
    r = Region(nc, k.shared_end, ARENA_END)
    k.x3 = r.take("x3", [P, NB, D], F32)
    k.x3_end = r.at
    layer2(nc, k, a)
    k.agg = r.take("agg", [P, NB, D], F32)
    k.agg_end = r.at
    edge_messages(nc, k, a)
    widen(nc, k, a)
    k.wide_end = k.agg_end + 4 * 2 * KC * NP
    narrow(nc, k, a, False, None)
    widen_again(nc, k, a)
    narrow(nc, k, a, True, out)
    return k


_INS = ["x", "src", "dst", "edge_attr_128", "edge_weight", "L0_gnn_wc", "L0_gnn_wn", "L0_gnn_bias",
        "L1_gnn_Wq", "L1_gnn_bq", "L1_gnn_Wk", "L1_gnn_Wv", "L1_gnn_Wo", "L1_gnn_bo", "L1_gnn_W1", "L1_gnn_b1",
        "L1_gnn_W2", "L1_gnn_b2", "L1_gnn_g1", "L1_gnn_beta1", "L1_gnn_g2", "L1_gnn_beta2", "L1_gnn_ln_g", "L1_gnn_ln_b",
        "L2_gnn_W", "L2_gnn_b", "L3_gnn_W_edge", "L3_gnn_b_edge", "L3_gnn_eps", "L3_gnn_W1", "L3_gnn_b1", "L3_gnn_g1",
        "L3_gnn_be1", "L3_gnn_W2", "L3_gnn_b2", "L3_gnn_g2", "L3_gnn_be2", "L3_gnn_gA", "L3_gnn_bA", "L3_gnn_M1", "L3_gnn_M2",
        "L3_gnn_gB", "L3_gnn_bB"]


def kernel(**inputs):
    import numpy as np
    import concourse.bacc as bacc
    from concourse.bass_utils import run_bass_kernel_spmd

    nc = bacc.Bacc("TRN2", target_bir_lowering=False, num_devices=1)
    arrays, a = {}, Names()
    for name in _INS:
        array = np.ascontiguousarray(inputs[name])
        array = array.reshape(array.shape or (1,))
        arrays[f"in_{name}"] = array
        a.__dict__[name] = nc.dram_tensor(f"in_{name}", array.shape, mybir.dt.from_np(array.dtype), kind="ExternalInput").ap()
    out = nc.dram_tensor("out_0", (N, D), F32, kind="ExternalOutput").ap()
    program(nc, a, out)
    return run_bass_kernel_spmd(nc, [arrays], core_ids=[0]).results[0]["out_0"]
```

```python
import concourse.bass as bass
from concourse import mybir

F32 = mybir.dt.float32
F32R = mybir.dt.float32r
F16 = mybir.dt.float16
BF16 = mybir.dt.bfloat16
I32 = mybir.dt.int32
U32 = mybir.dt.uint32
U16 = mybir.dt.uint16
ALU = mybir.AluOpType
ACT = mybir.ActivationFunctionType
AX = mybir.AxisListType.X

P = 128
N = 1250
D = 512
E = 40000
NB = -(-N // P)
NP = NB * P
KC = D // P
EC = 320
EP = E // EC
assert EP * EC == E and EP <= P
GT = 4
GE = GT * P
REC = 4
C3 = 417
W3 = 3 * C3
WIDE = (0, C3, 2 * C3)
NK3 = 3 * NB
NG = -(-(E // GE + NB) // 2) * 2
NG3 = -(-(E // GE + NK3) // 2) * 2
NT, NT3 = NG * GT, NG3 * GT
H = 8
DH = D // H
HP = H // 2
FF = 256
LAYERS = 2
ED = 128
D2 = 2 * D
EPS = 1e-5
BATCHES = ((0, 4), (4, 8), (8, NB))
ARENA, ARENA_END = 16512, 229344
NEVER = -2.0 ** 100


class Steps:

    def __init__(self, nc, eng, sem):
        self.sem, self.eng, self.n = nc.alloc_semaphore(sem) if isinstance(sem, str) else sem, eng, 0

    def mark(self, ins):
        ins.then_inc(self.sem, 1)
        self.n += 1
        return self.n

    def then(self, ins):
        self.eng.wait_ge(self.sem, self.mark(ins))


class Region:

    def __init__(self, nc, start, end):
        self.nc, self.at, self.end = nc, start, end

    def take(self, name, shape, dt):
        size = {F32: 4, F32R: 4, I32: 4, U32: 4, F16: 2, BF16: 2, U16: 2}[dt]
        for n in shape[1:]:
            size *= n
        t = self.nc.alloc_sbuf_tensor_at(name, shape, dt, offset=self.at)
        self.at += -(-size // 32) * 32
        assert self.at <= self.end, (name, self.at, self.end)
        return t


class Norm:

    PIECES = 3

    def __init__(self, nc, r, name, n):
        self.n = n
        self.pieces = r.take(name + "_pieces", [P, n, self.PIECES, 6], F32)
        self.mean_var = r.take(name + "_mean_var", [P, n, 2], F32)
        self.var, self.dev = r.take(name + "_var", [P, n], F32), r.take(name + "_dev", [P, n], F32)

    def stats(self, dve, me, b, *rows):
        for j, piece in enumerate(rows):
            me.mark(dve.bn_stats(self.pieces[:, b, j, :], piece))
        dve.wait_ge(me.sem, me.n)
        me.mark(dve.bn_aggr(self.mean_var[:, b, :], self.pieces[:, b, 0:len(rows), :]))

    def variance(self, dve, me, ready, first=0, end=None):
        dve.wait_ge(me.sem, me.n)
        dve.tensor_scalar(self.var[:, first:end], self.mean_var[:, first:end, 1], EPS, None, ALU.add).then_inc(ready, 1)

    def invert(self, dve, me, first=0, end=None):
        me.then(dve.reciprocal(self.dev[:, first:end], self.dev[:, first:end]))

    def affine(self, dve, me, b, rows, gain, shift):
        me.then(dve.scalar_tensor_tensor(rows, rows, self.mean_var[:, b, 0:1], gain, ALU.subtract, ALU.mult))
        return dve.scalar_tensor_tensor(rows, rows, self.dev[:, b:b + 1], shift, ALU.mult, ALU.add)

    def apply(self, dve, b, rows):
        return dve.tensor_scalar(rows, rows, self.mean_var[:, b, 0:1], self.dev[:, b:b + 1], ALU.subtract, ALU.mult)


def gate(eng, sem, value, passed):
    eng.wait_ge(sem, value)
    eng.sem_inc(passed, 1)


def last_rows(b):
    return min(P, N - b * P)


def row_of(vector):
    return vector.rearrange("(o n) -> o n", o=1).to_broadcast([P, vector.shape[0]])


def constants(nc, k):
    made = nc.alloc_semaphore("const_made")
    with nc.Block() as block:
        @block.gpsimd
        def _(pool):
            pool.memset(k.ident[:], 0.0).then_inc(made, 1)
            pool.memset(k.before[:], 1.0).then_inc(made, 1)
            pool.memset(k.ones[:], 1.0).then_inc(made, 1)
            pool.wait_ge(made, 3)
            pool.affine_select(out=k.ident[:], in_=k.ident[:], compare_op=ALU.not_equal, fill=1.0,
                               base=0, pattern=[[-1, P]], channel_multiplier=1).then_inc(made, 1)
            pool.affine_select(out=k.before[:], in_=k.before[:], compare_op=ALU.is_gt, fill=0.0,
                               base=0, pattern=[[1, P]], channel_multiplier=-1).then_inc(made, 1)
            pool.iota(k.node_row[:], pattern=[[1, NP]], base=0, channel_multiplier=0,
                      allow_small_or_imprecise_dtypes=True).then_inc(made, 1)
            pool.iota(k.row128[:], pattern=[[1, P]], base=0, channel_multiplier=0,
                      allow_small_or_imprecise_dtypes=True).then_inc(made, 1)
            pool.iota(k.row128f[:], pattern=[[1, P]], base=0, channel_multiplier=0,
                      allow_small_or_imprecise_dtypes=True).then_inc(made, 1)
            pool.iota(k.groups_row[:], pattern=[[1, NG3]], base=0, channel_multiplier=0,
                      allow_small_or_imprecise_dtypes=True).then_inc(made, 1)
            pool.iota(k.pad_rows[:], pattern=[[0, 1]], base=0, channel_multiplier=1,
                      allow_small_or_imprecise_dtypes=True).then_inc(made, 1)
            pool.wait_ge(made, 10)
            pool.tensor_copy(k.ident16[:], k.ident[:]).then_inc(made, 1)
            pool.tensor_scalar(k.pad_rows[:], k.pad_rows[:], float(last_rows(NB - 1)), 1.0, ALU.is_ge, ALU.mult).then_inc(made, 1)
            pool.wait_ge(made, 12)


def scatter_edges(pool, S, name, edge_pos, rec, stage, slots_dram, slots, scattered, prefilled):
    st_pos, st_rec = stage
    staged, passed = S(name + "_staged"), S(name + "_passed")

    def scatter(i, u):
        pool.tensor_copy(st_pos[:, u, :], edge_pos[:, bass.ds(i * 16 + 8 * u, 8)]).then_inc(staged, 1)
        pool.tensor_copy(st_rec[:, u, :], rec[:].rearrange("p c w -> p (c w)")[:, bass.ds(i * 64 + 32 * u, 32)]).then_inc(staged, 1)
        gate(pool, staged, i * 4 + 2 * u + 2, passed)
        for c in range(8):
            pool.indirect_dma_start(
                out=slots_dram, out_offset=bass.IndirectOffsetOnAxis(ap=st_pos[:, u, c:c + 1], axis=0),
                in_=st_rec[:, u, REC * c:REC * (c + 1)], in_offset=None,
                bounds_check=slots - 1, oob_is_err=False).then_inc(scattered[u], 16)

    pool.wait_ge(prefilled, 16)
    scatter(0, 0)
    scatter(0, 1)
    with pool.Fori(1, EC // 16) as i:
        for u in range(2):
            gate(pool, scattered[u], i * 128, passed)
            scatter(i, u)
    for u in range(2):
        pool.wait_ge(scattered[u], 8 * EC)


def sort_edges(nc, k, a):
    S = nc.alloc_semaphore
    cleared, loaded, prefilled = S("edges_cleared"), S("edges_loaded"), S("slots_prefilled")
    pads_made, totals_ready, offsets_ready, pos_ready = S("pads_made"), S("totals_ready"), S("offsets_ready"), S("pos_ready")
    scattered, read_back = [S(f"scattered3{u}") for u in range(2)], S("read_back3")
    x_loaded, w_loaded, x_transposed, xt_copied = S("x_loaded"), S("w0_loaded"), S("x_transposed"), S("xt_copied")
    dense_done, dense_copied, id_made = S("dense0_done"), S("beta_copied"), S("id_made")
    alpha_done, bias_loaded = S("alpha_done"), S("bias0_loaded")
    r = Region(nc, k.beta_end, ARENA_END)
    xt = r.take("xt_in", [P, KC, NP], F32)
    src_i, dst_i = r.take("src_i", [P, EC], I32), r.take("dst_i", [P, EC], I32)
    bidx, dloc = r.take("bidx", [P, EC], I32), r.take("dloc", [P, EC], I32)
    ew_s, bidx_f = r.take("ew_s", [P, EC], F32), r.take("bidx_f", [P, EC], F32)
    third, bucket3 = r.take("third", [P, EC], F32), r.take("bucket3", [P, EC], F32)
    is_in, one_row = r.take("is_in", [P, NK3, EC], BF16), r.take("one_row", [P, EC], BF16)
    prefix = r.take("prefix", [P, NK3, EC], F32)
    small, small_i = r.take("small", [P, 6, NK3], F32), r.take("small_i", [P, 2, NK3], I32)
    lin, lin_i = r.take("lin", [P, 4, EC], F32), r.take("lin_i", [P, 3, EC], I32)
    pos3 = r.take("pos3", [P, EC], U32)
    stage = r.take("st_pos3", [P, 2, 8], U32), r.take("st_rec3", [P, 2, 8 * REC], F32)
    pads = r.take("pads", [P, NT3, REC], F32)
    slots = r.take("slots3", [P, NT3, REC], F32)
    slot_wb = r.take("slot_wb", [P, NT3], BF16)
    key_f, key_i = r.take("key_f", [P, 3, NG3], F32), r.take("key_i", [P, 2, NG3], I32)
    wc = r.take("wc", [P, KC, D], F32)
    wn = r.take("wn", [P, KC, D], F32)
    bias = r.take("bias0", [P, D], F32)
    ps_off, ps_tot, ps_d = k.bank[:, 4, :], k.bank[:, 5, :], k.bank
    with nc.Block() as block:
        T, OFF, TOT, GRP, GS, M = range(6)

        @block.sync
        def _(sp):
            sp.wait_ge(cleared, 4)
            sp.dma_start(dst_i[0:EP, :], a.dst.rearrange("(p c) -> p c", c=EC)).then_inc(loaded, 16)
            sp.dma_start(src_i[0:EP, :], a.src.rearrange("(p c) -> p c", c=EC)).then_inc(loaded, 16)
            sp.dma_start(ew_s[0:EP, :], a.edge_weight.rearrange("(p c) -> p c", c=EC)).then_inc(loaded, 16)
            whole = (N // P) * P
            sp.dma_start(k.alpha[:, 0:N // P, :], a.x[0:whole, :].rearrange("(b p) f -> p b f", p=P)).then_inc(x_loaded, 16)
            sp.dma_start(k.alpha[0:N - whole, N // P, :], a.x[whole:N, :]).then_inc(x_loaded, 16)
            sp.dma_start(wc[:], a.L0_gnn_wc.rearrange("(c p) n -> p c n", p=P)).then_inc(w_loaded, 16)
            sp.dma_start(wn[:], a.L0_gnn_wn.rearrange("(c p) n -> p c n", p=P)).then_inc(w_loaded, 16)
            sp.dma_start(bias[:], row_of(a.L0_gnn_bias)).then_inc(bias_loaded, 16)
            sp.wait_ge(pads_made, 1)
            sp.dma_start(k.slots3_dram.rearrange("(p t) w -> p (t w)", p=P),
                         pads[:].rearrange("p t w -> p (t w)")).then_inc(prefilled, 16)
            sp.dma_start(k.slots_dram.rearrange("(p t) w -> p (t w)", p=P),
                         pads[:, 0:NT, :].rearrange("p t w -> p (t w)")).then_inc(k.prefilled1, 16)
            for u in range(2):
                sp.wait_ge(scattered[u], 8 * EC)
            sp.dma_start(slots[:].rearrange("p t w -> p (t w)"),
                         k.slots3_dram.rearrange("(p t) w -> p (t w)", p=P)).then_inc(read_back, 16)
            sp.wait_ge(read_back, 16)
            sp.wait_ge(k.prefilled1, 16)

        @block.gpsimd
        def _(pool):
            pool.iota(k.rec[:, :, 3], pattern=[[1, EC]], base=0, channel_multiplier=EC,
                      allow_small_or_imprecise_dtypes=True).then_inc(id_made, 1)
            pool.wait_ge(id_made, 1)
            pool.wait_ge(pos_ready, 1)
            scatter_edges(pool, S, "scatter3", pos3, k.rec, stage, k.slots3_dram, P * NT3, scattered, prefilled)

        @block.vector
        def _(dve):
            me = Steps(nc, dve, "sort_dve")

            def place(bucket, nk, tiles, turn, to):
                def row(j):
                    return small[:, j, 0:nk]

                for b in range(nk):
                    me.mark(dve.tensor_scalar(is_in[:, b, :], bucket[:], float(b), None, ALU.is_equal))
                dve.wait_ge(me.sem, me.n)
                counts = prefix[:, 0:nk, :]
                for b in range(nk):
                    me.mark(dve.tensor_tensor_scan(counts[:, b, :], one_row[:], is_in[:, b, :], 0.0, ALU.mult, ALU.add))
                dve.wait_ge(me.sem, me.n)
                dve.tensor_copy(row(T), counts[:, :, EC - 1]).then_inc(totals_ready, 1)
                dve.wait_ge(offsets_ready, 2 * turn)
                me.mark(dve.tensor_copy(row(OFF), ps_off[:, 0:nk]))
                me.then(dve.tensor_scalar(row(TOT), ps_tot[:, 0:nk], float(GE - 1), None, ALU.add))
                me.then(dve.tensor_copy(small_i[:, 0, 0:nk], row(TOT)))
                me.then(dve.tensor_scalar(small_i[:, 1, 0:nk], small_i[:, 0, 0:nk], GE.bit_length() - 1, None, ALU.arith_shift_right))
                me.then(dve.tensor_copy(row(GRP), small_i[:, 1, 0:nk]))
                me.then(dve.tensor_tensor_scan(row(GS), k.ones[:, 0:nk], row(GRP), 0.0, ALU.mult, ALU.add))
                me.then(dve.tensor_tensor(row(GS), row(GS), row(GRP), ALU.subtract))
                me.then(dve.tensor_scalar(row(M), row(GS), float(GE), -1.0, ALU.mult, ALU.add))
                me.then(dve.tensor_tensor(row(M), row(M), row(OFF), ALU.add))
                me.then(dve.tensor_tensor(counts, counts, row(M).unsqueeze(2).to_broadcast([P, nk, EC]), ALU.add))
                me.then(dve.tensor_tensor(counts, counts, is_in[:, 0:nk, :], ALU.mult))
                me.then(dve.tensor_reduce(lin[:, 0, :], counts.rearrange("p b c -> p c b"), axis=AX, op=ALU.add))
                me.then(dve.tensor_copy(lin_i[:, 0, :], lin[:, 0, :]))
                me.mark(dve.tensor_scalar(lin_i[:, 1, :], lin_i[:, 0, :], P - 1, None, ALU.bitwise_and))
                me.then(dve.tensor_scalar(lin_i[:, 2, :], lin_i[:, 0, :], 7, None, ALU.arith_shift_right))
                me.mark(dve.tensor_copy(lin[:, 1, :], lin_i[:, 1, :]))
                me.then(dve.tensor_copy(lin[:, 2, :], lin_i[:, 2, :]))
                me.mark(dve.scalar_tensor_tensor(lin[:, 3, :], lin[:, 1, :], float(tiles), lin[:, 2, :], ALU.mult, ALU.add))
                me.then(dve.tensor_scalar(lin[:, 0, :], bidx_f[:], float(NB), float(16 * P * NT3), ALU.is_ge, ALU.mult))
                me.then(dve.tensor_tensor(lin[:, 3, :], lin[:, 3, :], lin[:, 0, :], ALU.add))
                return dve.tensor_copy(to[:], lin[:, 3, :])

            dve.memset(dst_i[:], NP).then_inc(cleared, 1)
            dve.memset(src_i[:], 0).then_inc(cleared, 1)
            dve.memset(ew_s[:], 0.0).then_inc(cleared, 1)
            dve.memset(k.alpha[:, NB - 1, :], 0.0).then_inc(cleared, 1)
            me.then(dve.memset(pads[:], 0.0))
            dve.memset(pads[:, :, 1], -1.0).then_inc(pads_made, 1)
            me.mark(dve.memset(one_row[:], 1.0))
            dve.wait_ge(loaded, 48)
            me.mark(dve.tensor_scalar(bidx[:], dst_i[:], 7, None, ALU.arith_shift_right))
            me.mark(dve.tensor_scalar(dloc[:], dst_i[:], P - 1, None, ALU.bitwise_and))
            me.mark(dve.tensor_copy(k.rec[:, :, 0], src_i[:]))
            me.then(dve.tensor_copy(k.rec[:, :, 2], ew_s[:]))
            me.mark(dve.tensor_copy(k.rec[:, :, 1], dloc[:]))
            me.mark(dve.tensor_copy(bidx_f[:], bidx[:]))
            me.then(dve.tensor_scalar(third[:], k.rec[:, :, 0], float(C3), None, ALU.is_ge))
            me.then(dve.scalar_tensor_tensor(third[:], k.rec[:, :, 0], float(2 * C3), third[:], ALU.is_ge, ALU.add))
            me.then(dve.scalar_tensor_tensor(bucket3[:], bidx_f[:], 3.0, third[:], ALU.mult, ALU.add))
            place(bucket3, NK3, NT3, 1, pos3).then_inc(pos_ready, 1)
            key, div, col = key_f[:, 0, :], key_f[:, 1, :], key_f[:, 2, :]
            me.then(dve.tensor_scalar(key, k.groups_row[:], small[:, GS, 1:2], None, ALU.is_ge))
            for b in range(2, NK3):
                me.then(dve.scalar_tensor_tensor(key, k.groups_row[:], small[:, GS, b:b + 1], key, ALU.is_ge, ALU.add))
            me.then(dve.tensor_scalar(div, key, 171.0, None, ALU.mult))
            me.then(dve.tensor_copy(key_i[:, 0, :], div))
            me.then(dve.tensor_scalar(key_i[:, 1, :], key_i[:, 0, :], 9, None, ALU.arith_shift_right))
            me.then(dve.tensor_copy(div, key_i[:, 1, :]))
            me.then(dve.scalar_tensor_tensor(col, div, -3.0, key, ALU.mult, ALU.add))
            me.then(dve.tensor_scalar(col, col, float(C3), None, ALU.mult))
            me.then(dve.scalar_tensor_tensor(key, div, float(NP), col, ALU.mult, ALU.add))
            me.then(dve.tensor_copy(k.place3[:], key[0:1, :]))
            dve.wait_ge(bias_loaded, 16)
            for b in range(NB):
                dve.wait_ge(dense_done, 2 * b + 1)
                me.then(dve.tensor_tensor(k.alpha[:, b, :], ps_d[:, 2 * b % 4, :], k.alpha[:, b, :], ALU.add))
                dve.tensor_tensor(k.alpha[:, b, :], k.alpha[:, b, :], bias[:], ALU.add).then_inc(alpha_done, 1)
            me.then(place(bidx_f, NB, NT, 2, k.pos))
            me.then(dve.tensor_scalar(k.blk_f[:], k.groups_row[0:1, 0:NG], small[0:1, GS, 1:2], None, ALU.is_ge))
            for b in range(2, NB):
                me.then(dve.scalar_tensor_tensor(k.blk_f[:], k.groups_row[0:1, 0:NG], small[0:1, GS, b:b + 1], k.blk_f[:], ALU.is_ge, ALU.add))
            me.then(dve.tensor_copy(k.blk[:], k.blk_f[:]))
            dve.wait_ge(read_back, 16)
            me.mark(dve.tensor_copy(k.slot3_dst[:], slots[:, :, 1]))
            me.mark(dve.tensor_tensor(k.slot3_src[:].rearrange("p (g j) -> p g j", j=GT), slots[:, :, 0].rearrange("p (g j) -> p g j", j=GT),
                                      col.unsqueeze(2).to_broadcast([P, NG3, GT]), ALU.subtract))
            ew = slots[:, :, 2]
            me.then(dve.tensor_copy(slot_wb[:], ew))
            me.then(dve.tensor_copy(k.slot_w[:, 0, :], slot_wb[:]))
            me.then(dve.tensor_tensor(k.slot_w[:, 1, :], ew, k.slot_w[:, 0, :], ALU.subtract))
            me.then(dve.tensor_copy(slot_wb[:], k.slot_w[:, 1, :]))
            me.then(dve.tensor_copy(k.slot_w[:, 3, :], slot_wb[:]))
            me.then(dve.tensor_tensor(k.slot_w[:, 2, :], k.slot_w[:, 1, :], k.slot_w[:, 3, :], ALU.subtract))
            me.then(dve.tensor_copy(k.slot_w[:, 1, :], k.slot_w[:, 3, :]))

        @block.tensor
        def _(pe):
            def offsets(turn, nk):
                pe.wait_ge(totals_ready, turn)
                pe.matmul(ps_off[:, 0:nk], k.before[:], small[:, T, 0:nk], start=True, stop=True).then_inc(offsets_ready, 1)
                pe.matmul(ps_tot[:, 0:nk], k.ones[:, 0:P], small[:, T, 0:nk], start=True, stop=True).then_inc(offsets_ready, 1)

            pe.wait_ge(x_loaded, 32)
            for b in range(NB):
                if b >= 4:
                    pe.wait_ge(xt_copied, b - 3)
                for c in range(KC):
                    t = pe.transpose(ps_d[:, b % 4, c * P:(c + 1) * P], k.alpha[:, b, c * P:(c + 1) * P], k.ident[:])
                t.then_inc(x_transposed, 1)
            offsets(1, NK3)
            pe.wait_ge(w_loaded, 32)
            pe.wait_ge(xt_copied, NB)
            for n in range(2 * NB):
                b, w = n // 2, (wc, wn)[n % 2]
                if n >= 4:
                    pe.wait_ge((alpha_done, dense_copied)[n % 2], (n - 4) // 2 + 1)
                for c in range(KC):
                    m = pe.matmul(ps_d[:, n % 4, :], xt[:, c, b * P:(b + 1) * P], w[:, c, :], start=(c == 0), stop=(c == KC - 1))
                m.then_inc(dense_done, 1)
            offsets(2, NB)

        @block.scalar
        def _(act):
            for b in range(NB):
                act.wait_ge(x_transposed, b + 1)
                act.copy(xt[:, :, b * P:(b + 1) * P], ps_d[:, b % 4, :].rearrange("p (c n) -> p c n", c=KC)).then_inc(xt_copied, 1)
            for b in range(NB):
                act.wait_ge(dense_done, 2 * b + 2)
                act.copy(k.beta[:, b, :], ps_d[:, (2 * b + 1) % 4, :]).then_inc(dense_copied, 1)


def edge_matrices(nc, k):
    S = nc.alloc_semaphore
    acc_cleared, hots_built, chunk_done, added = S("acc_cleared"), S("hots_built"), S("chunk_done"), S("chunk_added")
    weighted, scattered = S("hots_weighted"), [S(f"scattered1{u}") for u in range(2)]
    slots_back = S("slots_back")
    r = Region(nc, k.acc_end, ARENA_END)
    hot_src = r.take("hot_src", [P, 2, GT, C3 + 1], BF16)
    hot_dst = r.take("hot_dst", [P, 2, GT, 4, P], BF16)
    stage = r.take("st_pos", [P, 2, 8], U32), r.take("st_rec", [P, 2, 8 * REC], F32)
    slots = r.take("slots1", [P, NT, REC], F32)
    acc_c, acc_a = (m[:].rearrange("p b n -> p (b n)") for m in (k.acc_c, k.acc_a))
    with nc.Block() as block:
        @block.gpsimd
        def _(pool):
            pool.memset(acc_a, 0.0).then_inc(acc_cleared, 1)
            scatter_edges(pool, S, "scatter1", k.pos, k.rec, stage, k.slots_dram, P * NT, scattered, k.prefilled1)

        @block.sync
        def _(sp):
            for u in range(2):
                sp.wait_ge(scattered[u], 8 * EC)
            sp.dma_start(slots[:].rearrange("p t w -> p (t w)"), k.slots_dram.rearrange("(p t) w -> p (t w)", p=P)).then_inc(slots_back, 16)
            sp.wait_ge(slots_back, 16)

        @block.vector
        def _(dve):
            def build(g, u):
                for j in range(GT):
                    t = g * GT + j
                    dve.tensor_scalar(hot_dst[:, u, j, 0, :], k.row128[:], k.slot3_dst[:, bass.ds(t, 1)], None, ALU.is_equal).then_inc(hots_built, 1)
                for j in range(GT):
                    t = g * GT + j
                    if j < 2:
                        dve.tensor_scalar(hot_dst[:, u, j, 1, :], k.row128[:], k.slot3_dst[:, bass.ds(t, 1)], k.slot_w[:, 0, bass.ds(t, 1)],
                                          ALU.is_equal, ALU.mult)
                    last = dve.tensor_scalar(hot_src[:, u, j, 0:C3], k.node_row[:, 0:C3], k.slot3_src[:, bass.ds(t, 1)], None, ALU.is_equal)
                last.then_inc(hots_built, 1)

            def add(g, u):
                to = dve.value_load(k.place3[0:1, bass.ds(g, 1)], min_val=0, max_val=(NB - 1) * NP + 2 * C3)
                dve.wait_ge(added, g * 2 + 4)
                for c, acc in enumerate((acc_c, acc_a)):
                    dve.wait_ge(chunk_done, g * 2 + c + 5)
                    rows = acc[:, bass.ds(to, C3)]
                    dve.tensor_tensor(rows, k.bank[:, 2 * u + c, 0:C3], rows, ALU.add).then_inc(added, 1)

            dve.memset(acc_c, 0.0).then_inc(added, 4)
            dve.wait_ge(acc_cleared, 1)
            build(0, 0)
            with dve.Fori(0, NG3 // 2 - 1) as i:
                for u in range(2):
                    build(i * 2 + u + 1, 1 - u)
                    add(i * 2 + u, u)
            build(NG3 - 1, 1)
            add(NG3 - 2, 0)
            add(NG3 - 1, 1)
            dve.wait_ge(slots_back, 16)
            dve.tensor_copy(k.slot_dst[:], slots[:, :, 1])
            dve.tensor_copy(k.src_idx[:], slots[:, :, 0])
            dve.tensor_copy(k.id_idx[:], slots[:, :, 3])

        @block.scalar
        def _(act):
            with act.Fori(0, NG3 // 2) as i:
                for u in range(2):
                    g = i * 2 + u
                    act.wait_ge(chunk_done, g * 2 + 2)
                    for j in range(GT):
                        act.wait_ge(hots_built, g * (GT + 1) + j + 1)
                        for q in (1, 2) if j < 2 else (0, 1, 2):
                            last = act.activation(hot_dst[:, u, j, 1 + q, :], hot_dst[:, u, j, 0, :], ACT.Copy,
                                                  scale=k.slot_w[:, q, bass.ds(g * GT + j, 1)])
                    last.then_inc(weighted, 1)

        @block.tensor
        def _(pe):
            pe.sem_inc(chunk_done, 4)
            with pe.Fori(0, NG3 // 2) as i:
                for u in range(2):
                    g = i * 2 + u
                    pe.wait_ge(hots_built, g * (GT + 1) + GT + 1)
                    for c, parts in enumerate(((0,), (1, 2, 3))):
                        pe.wait_ge(added, g * 2 + c + 1)
                        if c:
                            pe.wait_ge(weighted, g + 1)
                        for j in range(GT):
                            for q in parts:
                                m = pe.matmul(k.bank[:, 2 * u + c, 0:C3], hot_dst[:, u, j, q, :], hot_src[:, u, j, 0:C3],
                                              start=(j == 0 and q == parts[0]), stop=(j == GT - 1 and q == parts[-1]))
                        m.then_inc(chunk_done, 1)


def transpose_weights_of_edges(nc, k):
    S = nc.alloc_semaphore
    ROWS = 3
    transposed, copied, stored, summed = S("at_transposed"), S("at_copied"), [S(f"at_stored{u}") for u in range(ROWS)], S("deg_summed")
    r = Region(nc, k.acc_end, ARENA_END)
    rows = r.take("at_rows", [P, ROWS, NP], F32)
    with nc.Block() as block:
        @block.tensor
        def _(pe):
            for s in range(NB):
                if s >= 2:
                    pe.wait_ge(copied, s - 1)
                for b in range(NB):
                    t = pe.transpose(k.bank[:, 4 * (s % 2) + b // 4, b % 4 * P:(b % 4 + 1) * P], k.acc_a[:, b, s * P:(s + 1) * P], k.ident[:])
                t.then_inc(transposed, 1)

        @block.scalar
        def _(act):
            for s in range(NB):
                act.wait_ge(transposed, s + 1)
                if s >= ROWS:
                    act.wait_ge(stored[s % ROWS], 16 * (s // ROWS))
                act.copy(rows[:, s % ROWS, 0:2 * 512].rearrange("p (b n) -> p b n", n=512), k.bank[:, 4 * (s % 2):4 * (s % 2) + 2, :])
                act.copy(rows[:, s % ROWS, 2 * 512:NP], k.bank[:, 4 * (s % 2) + 2, 0:NP - 2 * 512]).then_inc(copied, 1)

        @block.sync
        def _(sp):
            for s in range(NB):
                sp.wait_ge(copied, s + 1)
                sp.dma_start(k.at_dram[:, :, s, :].rearrange("b p n -> p b n"),
                             rows[:, s % ROWS, :].rearrange("p (b n) -> p b n", n=P)).then_inc(stored[s % ROWS], 16)
            for u in range(ROWS):
                sp.wait_ge(stored[u], 16 * len(range(u, NB, ROWS)))

        @block.vector
        def _(dve):
            dve.tensor_reduce(k.deg[:], k.acc_a[:], axis=AX, op=ALU.add).then_inc(summed, 1)
            dve.wait_ge(summed, 1)


def layer0(nc, k):
    S = nc.alloc_semaphore
    ct_transposed, ct_copied, gamma_done, y_done = S("ct_transposed"), S("ct_copied"), S("gamma_done"), S("y0_done")
    var_ready, dev_ready, x1_ready, x1_stored = S("var0_ready"), S("dev0_ready"), S("x1_ready"), S("x1_stored")
    x1t_done, x1t_copied = S("x1t_transposed"), S("x1t_copied")
    r = Region(nc, k.acc_end - 4 * NB * NP, k.tail - 4 * KC * NP)
    inv = r.take("inv0", [P, NB], F32)
    norm = Norm(nc, r, "norm0", NB)
    y = k.alpha
    with nc.Block() as block:
        @block.tensor
        def _(pe):
            for s in range(NB):
                if s >= 2:
                    pe.wait_ge(ct_copied, s - 1)
                for b in range(NB):
                    t = pe.transpose(k.bank[:, 3 * (s % 2) + b // 4, b % 4 * P:(b % 4 + 1) * P], k.acc_c[:, b, s * P:(s + 1) * P], k.ident[:])
                t.then_inc(ct_transposed, 1)
            for s in range(NB):
                if s >= 2:
                    pe.wait_ge(y_done, s - 1)
                for b in range(NB):
                    m = pe.matmul(k.bank[:, 6 + s % 2, :], k.acc_c[:, b, s * P:(s + 1) * P], k.beta[:, b, :], start=(b == 0), stop=(b == NB - 1))
                m.then_inc(gamma_done, 1)
            pe.wait_ge(ct_copied, NB)
            for b in range(NB):
                pe.wait_ge(x1_ready, b + 1)
                if b >= 4:
                    pe.wait_ge(x1t_copied, b - 3)
                for c in range(KC):
                    t = pe.transpose(k.bank[:, b % 4, c * P:(c + 1) * P], y[:, b, c * P:(c + 1) * P], k.ident[:])
                t.then_inc(x1t_done, 1)

        @block.scalar
        def _(act):
            for s in range(NB):
                act.wait_ge(ct_transposed, s + 1)
                act.copy(k.ct[:, s, 0:2 * 512].rearrange("p (b n) -> p b n", n=512), k.bank[:, 3 * (s % 2):3 * (s % 2) + 2, :])
                act.copy(k.ct[:, s, 2 * 512:NP], k.bank[:, 3 * (s % 2) + 2, 0:NP - 2 * 512]).then_inc(ct_copied, 1)
            act.wait_ge(var_ready, 1)
            act.sqrt(norm.dev[:], norm.var[:]).then_inc(dev_ready, 1)
            for b in range(NB):
                act.wait_ge(x1t_done, b + 1)
                act.copy(k.x1t[:, :, b * P:(b + 1) * P], k.bank[:, b % 4, :].rearrange("p (c n) -> p c n", c=KC)).then_inc(x1t_copied, 1)

        @block.vector
        def _(dve):
            me = Steps(nc, dve, "layer0_dve")
            for s in range(NB):
                dve.wait_ge(ct_copied, s + 1)
                me.mark(dve.tensor_reduce(k.counts[:, s:s + 1], k.ct[:, s, :], axis=AX, op=ALU.add))
            dve.wait_ge(me.sem, me.n)
            me.mark(dve.tensor_copy(inv[:, 0:NB - 1], k.counts[:, 0:NB - 1]))
            me.then(dve.tensor_tensor(inv[:, NB - 1:NB], k.counts[:, NB - 1:NB], k.pad_rows[:], ALU.add))
            me.then(dve.reciprocal(inv[:], inv[:]))
            for s in range(NB):
                dve.wait_ge(gamma_done, s + 1)
                dve.scalar_tensor_tensor(y[:, s, :], k.bank[:, 6 + s % 2, :], inv[:, s:s + 1], y[:, s, :], ALU.mult, ALU.add).then_inc(y_done, 1)
                dve.wait_ge(y_done, s + 1)
                norm.stats(dve, me, s, y[:, s, :])
                me.mark(dve.tensor_scalar(k.mask[:, s, :], k.acc_c[:, s, :], 0.5, NEVER, ALU.is_lt, ALU.mult))
            norm.variance(dve, me, var_ready)
            dve.wait_ge(dev_ready, 1)
            norm.invert(dve, me)
            for b in range(NB):
                norm.apply(dve, b, y[:, b, :]).then_inc(x1_ready, 1)

        @block.sync
        def _(sp):
            for b in range(NB):
                sp.wait_ge(x1_ready, b + 1)
                sp.dma_start(k.x1_dram[b * P:(b + 1) * P, :], y[:, b, :]).then_inc(x1_stored, 16)
            sp.wait_ge(x1_stored, 16 * NB)


def exact(pe, to, left, right, chunks, arrive=None):
    for n, c in enumerate(chunks):
        if arrive:
            arrive(c)
        pe.matmul(to, left(0, c), right(0, c), start=(n == 0), stop=False)
        pe.matmul(to, left(0, c), right(1, c), start=False, stop=False)
        m = pe.matmul(to, left(1, c), right(0, c), start=False, stop=(n == len(chunks) - 1))
    return m


def turned(pe, k, bank, rows, j, n):
    for o in range(n):
        t = pe.transpose(k.bank[:, bank, o * P:(o + 1) * P], rows[:, o, j * P:(j + 1) * P], k.ident[:])
    return t


EVEN = ((0, C3 + 1), (C3 + 1, C3 + 1), (2 * C3 + 2, C3 - 1))
W3E = EVEN[2][0] + EVEN[2][1]


def project(nc, k, a, l, at):
    S = at.sem
    w_loaded, w_turned, w_high, w_low = [S(f"wqkv_loaded{j}") for j in range(3)], S("wqkv_turned"), S("wqkv_high"), S("wqkv_low")
    x_high_made, x_low_made = S("px_high_made"), S("px_low_made")
    v_loaded, v_turned, v_ready = S("vectors_loaded"), S("vectors_turned"), S("vectors_ready")
    q_done, k_done, val_done = S("q_done"), S("k_done"), S("v_done")
    q_copied, k_copied, val_copied, ones_set = S("q_copied"), S("k_copied"), S("v_copied"), S("v_ones_set")
    bq_scaled = S("bq_scaled")
    split, saved = S("qk_split"), S("qk_saved")
    r = Region(nc, at.temps, k.tail - 4 * KC * NP)
    whole = r.take("qk_whole", [P, 2, NP], F32)
    high, low = r.take("qk_high", [P, 2, NP], F32R), r.take("qk_low", [P, 2, NP], F32R)
    x_low = r.take("px_low", [P, KC, NP], F32R)
    rows_a, w_a = r.take("wqkv_rows_a", [P, KC, D], F32), r.take("wqkv_a", [P, 2, KC, D], F32R)
    x_high = Region(nc, at.agg_start, at.temps).take("px_high", [P, KC, NP], F32R)
    r = Region(nc, at.val_start, at.temps)
    rows_b, w_b = r.take("wqkv_rows_b", [P, KC, D], F32), r.take("wqkv_b", [P, 2, KC, D], F32R)
    x = (x_high, x_low)
    weights = (a.L1_gnn_Wq, a.L1_gnn_Wk, a.L1_gnn_Wv)
    rows, w_in = (rows_a, rows_b, rows_a), (w_b, w_a, w_a)
    with nc.Block() as block:
        @block.sync
        def _(sp):
            def load(j):
                sp.dma_start(rows[j][:], weights[j][bass.ds(l, 1), :, :].rearrange("l (o p) i -> p (l o) i", p=P)).then_inc(w_loaded[j], 16)

            load(0)
            load(1)
            row = 0
            for v, n in ((a.L1_gnn_bq, KC), (a.L1_gnn_bo, KC), (a.L1_gnn_g1, KC), (a.L1_gnn_beta1, KC), (a.L1_gnn_b1, FF // P),
                         (a.L1_gnn_b2, KC), (a.L1_gnn_g2, KC), (a.L1_gnn_beta2, KC)):
                sp.dma_start(at.vec_rows[row:row + n, :], v[bass.ds(l, 1), :].rearrange("l (c p) -> (l c) p", p=P)).then_inc(v_loaded, 16)
                row += n
            sp.wait_ge(w_turned, KC)
            load(2)
            for n in range(2 * HP):
                sp.wait_ge(split, n + 1)
                sp.dma_start(k.qk_dram[2 * (n // HP), n % HP], high[:, n % 2, :].bitcast(F32)).then_inc(saved, 16)
                sp.dma_start(k.qk_dram[2 * (n // HP) + 1, n % HP], low[:, n % 2, :].bitcast(F32)).then_inc(saved, 16)
                sp.wait_ge(saved, 32 * (n + 1))

        @block.tensor
        def _(pe):
            def turn(j):
                pe.wait_ge(w_loaded[j], 16)
                for c in range(KC):
                    n = j * KC + c
                    if n >= 2:
                        pe.wait_ge(w_low, n - 1)
                    turned(pe, k, n % 2, rows[j], c, KC).then_inc(w_turned, 1)

            turn(0)
            turn(1)
            pe.wait_ge(v_loaded, 16 * 8)
            pe.transpose(k.bank[:, 7, 0:at.NV], at.vec_rows[0:at.NV, :], k.ident[0:at.NV, 0:at.NV]).then_inc(v_turned, 1)
            pe.wait_ge(x_low_made, KC)
            n = 0
            for j, done in ((0, q_done), (1, k_done)):
                pe.wait_ge(w_low, (j + 1) * KC)
                for o in range(KC):
                    for at0, wide in EVEN:
                        if n >= 4:
                            m4 = n - 4
                            pe.wait_ge(q_copied if m4 < 12 else k_copied, m4 % 12 + 1)
                        exact(pe, k.bank[:, 2 + n % 4, 0:wide], lambda q, i: w_in[j][:, q, i, o * P:(o + 1) * P],
                              lambda q, i: x[q][:, i, at0:at0 + wide], range(KC)).then_inc(done, 1)
                        n += 1
            turn(2)
            pe.wait_ge(w_low, 3 * KC)
            pe.wait_ge(k_copied, 12)
            for b in range(NB):
                if b >= 4:
                    pe.wait_ge(val_copied, b - 3)
                exact(pe, k.bank[:, 2 + b % 4, :], lambda q, i: x[q][:, i, b * P:(b + 1) * P],
                      lambda q, i: w_in[2][:, q, i, :], range(KC)).then_inc(val_done, 1)

        @block.scalar
        def _(act):
            def high_part(j, c):
                act.wait_ge(w_turned, j * KC + c + 1)
                act.copy(w_in[j][:, 0, c, :], k.bank[:, (j * KC + c) % 2, :]).then_inc(w_high, 1)

            for i in range(KC):
                act.copy(x_high[:, i, :], k.x1t[:, i, :]).then_inc(x_high_made, 1)
                high_part(0, i)
            for c in range(KC):
                high_part(1, c)
            act.wait_ge(bq_scaled, 1)
            for n in range(12):
                act.wait_ge(q_done, n + 1)
                if n % 3 == 0 and n >= 6:
                    act.wait_ge(split, n // 3 - 1)
                at0, wide = EVEN[n % 3]
                act.activation(whole[:, n // 3 % 2, at0:at0 + wide], k.bank[:, 2 + n % 4, 0:wide], ACT.Identity,
                               bias=at.bq[:, n // 3:n // 3 + 1], scale=DH ** -0.5).then_inc(q_copied, 1)
            for n in range(12):
                act.wait_ge(k_done, n + 1)
                if n % 3 == 0:
                    act.wait_ge(split, n // 3 + 3)
                at0, wide = EVEN[n % 3]
                act.copy(whole[:, n // 3 % 2, at0:at0 + wide], k.bank[:, 2 + n % 4, 0:wide]).then_inc(k_copied, 1)
            for c in range(KC):
                high_part(2, c)

        @block.vector
        def _(dve):
            me = Steps(nc, dve, at.sem("project_dve"))

            def low_part(j, c):
                n = j * KC + c
                dve.wait_ge(w_high, n + 1)
                dve.tensor_tensor(w_in[j][:, 1, c, :], k.bank[:, n % 2, :], w_in[j][:, 0, c, :].bitcast(F32), ALU.subtract).then_inc(w_low, 1)

            me.then(dve.memset(whole[:, :, W3E:NP], 0.0))
            for i in range(KC):
                dve.wait_ge(x_high_made, i + 1)
                dve.tensor_tensor(x_low[:, i, :], k.x1t[:, i, :], x_high[:, i, :].bitcast(F32), ALU.subtract).then_inc(x_low_made, 1)
                low_part(0, i)
            for c in range(KC):
                low_part(1, c)
            dve.wait_ge(v_turned, 1)
            dve.tensor_copy(at.vec[:], k.bank[:, 7, 0:at.NV]).then_inc(v_ready, 1)
            dve.wait_ge(v_ready, 1)
            dve.tensor_scalar(at.bq[:], at.vec[:, 0:KC], DH ** -0.5, None, ALU.mult).then_inc(bq_scaled, 1)
            for n in range(2 * HP):
                dve.wait_ge(q_copied if n < HP else k_copied, 3 * (n % HP) + 3)
                if n >= 2:
                    dve.wait_ge(saved, 32 * (n - 1))
                me.then(dve.tensor_copy(high[:, n % 2, :], whole[:, n % 2, :]))
                dve.tensor_tensor(low[:, n % 2, :], whole[:, n % 2, :], high[:, n % 2, :].bitcast(F32), ALU.subtract).then_inc(split, 1)
            for c in range(KC):
                low_part(2, c)
            dve.wait_ge(q_done, 12)
            dve.memset(at.val[:, :, :, DH:2 * DH], 1.0).then_inc(ones_set, 1)
            for b in range(NB):
                dve.wait_ge(val_done, b + 1)
                heads = k.bank[:, 2 + b % 4, :].rearrange("p (h u d) -> p h u d", u=2, d=DH)
                dve.tensor_copy(at.val[:, b, :, 0:DH], heads[:, :, 0, :])
                dve.tensor_copy(at.val[:, b, :, 2 * DH:3 * DH], heads[:, :, 1, :]).then_inc(val_copied, 1)


CHUNKS = ((0, 512), (512, 512), (1024, NP - 1024))
PIECES = 6
PIECE = -(-W3 // PIECES)
RING = 5


def score_plan():
    plan = [("max", 0, b) for b in range(NB)] + [("turn", 0)]
    for h in range(H):
        b = 0
        for j in range(NB):
            plan.append(("exp", h, j))
            if h + 1 < H and j >= 2:
                for _ in range((2, 2, 2, 2, 1, 1, 0, 0)[j - 2]):
                    plan.append(("max", h + 1, b))
                    b += 1
        if h + 1 < H:
            plan.append(("turn", h + 1))
    return plan


def gather_edge_features(nc, pool, r, k, a, l):
    S = nc.alloc_semaphore
    staged, made, passed = S("ids_staged"), S("parts_made"), S("features_passed")
    got, saved = [S(f"features_got{u}") for u in range(2)], [S(f"features_saved{u}") for u in range(2)]
    idx = r.take("ids", [P, 2, GT], U32)
    rows = r.take("feature_rows", [P, 2, GT * ED], F32)
    parts = r.take("feature_parts", [P, 2, 2, GT * ED], F32R)
    share = NG // LAYERS
    before = l * share

    def gather(i, u):
        g = i * 2 + u
        pool.tensor_copy(idx[:, u, :], k.id_idx[:, bass.ds((before + g) * GT, GT)]).then_inc(staged, 1)
        gate(pool, staged, before + g + 1, passed)
        for j in range(GT):
            pool.indirect_dma_start(out=rows[:, u, j * ED:(j + 1) * ED], out_offset=None, in_=a.edge_attr_128,
                                    in_offset=bass.IndirectOffsetOnAxis(ap=idx[:, u, j:j + 1], axis=0)).then_inc(got[u], 16)

    def split(i, u, first=False):
        g = i * 2 + u
        gate(pool, got[u], before * (8 * GT) + i * (16 * GT) + 16 * GT, passed)
        if not first:
            gate(pool, saved[u], before * 8 + i * 16, passed)
        pool.tensor_copy(parts[:, u, 0, :], rows[:, u, :]).then_inc(made, 1)
        gate(pool, made, before * 2 + g * 2 + 1, passed)
        pool.tensor_tensor(parts[:, u, 1, :], rows[:, u, :], parts[:, u, 0, :].bitcast(F32), ALU.subtract).then_inc(made, 1)
        gate(pool, made, before * 2 + g * 2 + 2, passed)
        pool.dma_start(k.features_dram[bass.ds(l, 1), bass.ds(g * P, P), :].rearrange("l p n -> (l p) n"), parts[:, u, :, :].rearrange("p q n -> p (q n)").bitcast(F32)).then_inc(saved[u], 16)

    gather(0, 0)
    gather(0, 1)
    split(0, 0, True)
    gather(1, 0)
    split(0, 1, True)
    with pool.Fori(1, share // 2 - 1) as i:
        gather(i, 1)
        split(i, 0)
        gather(i + 1, 0)
        split(i, 1)
    last = share // 2 - 1
    gather(last, 1)
    split(last, 0)
    split(last, 1)
    for u in range(2):
        gate(pool, saved[u], before * 8 + 16 * (last + 1), passed)


def attend(nc, k, a, l, at):
    S = at.sem
    loaded, ones_set = [[S(f"tile{u}{j}_loaded") for j in range(6)] for u in range(2)], S("key_ones_set")
    scored, maxed, max_ready, max_turned, max_copied = S("scored"), S("maxed"), S("max_ready"), S("max_turned"), S("max_copied")
    st_done, exp_done, p_ready, pv_done, pv_copied = S("st_done"), S("exp_done"), S("p_ready"), S("pv_done"), S("pv_copied")
    head_done = S("head_done")
    NPT = 3
    r = Region(nc, at.temps, k.tail - 4 * KC * NP)
    keys, queries = r.take("keys", [P, 2, NP], F32R), r.take("queries", [P, 2, NP], F32R)
    keys_more, queries_more = r.take("keys_more", [DH + 3, 2, NP], F32R), r.take("queries_more", [DH + 3, 2, NP], F32R)
    junk = r.take("junk", [P, 2, 512], BF16)
    maxes, m0 = r.take("maxes", [P, NB, 3], F32), r.take("m0", [P, NB], F32)
    m1, m2 = r.take("m1", [P, NB], F32), r.take("m2", [P, NB], F32)
    parts = r.take("m_parts", [P, NB, 3], BF16)
    pt = r.take("pt", [P, NPT, NP], F32)
    raw = r.take("raw", [P, W3], F32)
    inv = r.take("inv_s", [P, PIECE], F32)
    plan = score_plan()
    turns, bank_of = [], {}
    for item in plan:
        for c in range(2 if item[0] == "turn" else 3):
            bank_of[item + (c,)] = len(turns) % RING
            turns.append(item)
    with nc.Block() as block:
        @block.gpsimd
        def _(pool):
            gather_edge_features(nc, pool, r, k, a, l)

        @block.sync
        def _(sp):
            for h in range(H):
                u, p = h % 2, h // 2
                rows = slice(DH * u, DH * (u + 1))
                if h >= 2:
                    sp.wait_ge(st_done, 3 * NB * (h - 1))
                for j, (to, kind) in enumerate(((keys[0:DH, u, :], 2), (keys[DH:P, u, :], 3),
                                                (queries[0:DH, u, :], 0), (queries[DH:P, u, :], 0),
                                                (keys_more[0:DH, u, :], 2), (queries_more[0:DH, u, :], 1))):
                    sp.dma_start(to.bitcast(F32), k.qk_dram[kind, p, rows, :]).then_inc(loaded[u][j], 16)

        @block.tensor
        def _(pe):
            emptied = []
            counts = {"max": 0, "turn": 0, "exp": 0}

            def next_bank(kind):
                if len(emptied) >= RING:
                    pe.wait_ge(*emptied[-RING])
                counts[kind] += 1
                emptied.append(({"max": maxed, "turn": max_copied, "exp": exp_done}[kind], counts[kind]))
                return (len(emptied) - 1) % RING

            def maximum(h, b):
                u = h % 2
                if b == 0:
                    for j in range(6):
                        pe.wait_ge(loaded[u][j], 16 * (h // 2 + 1))
                for at0, wide in CHUNKS:
                    to = k.bank[:, next_bank("max"), 0:wide]
                    pe.matmul(to, queries[:, u, b * P:(b + 1) * P], keys[:, u, at0:at0 + wide], start=True, stop=False)
                    pe.matmul(to, queries_more[0:DH, u, b * P:(b + 1) * P], keys_more[0:DH, u, at0:at0 + wide], start=False, stop=True).then_inc(scored, 1)

            def turn(h):
                pe.wait_ge(max_ready, h + 1)
                for i in range(2):
                    to = k.bank[0:3, next_bank("turn"), :].bitcast(BF16)
                    for b in range(5):
                        t = pe.transpose(to[:, b * P:(b + 1) * P], parts[:, 5 * i + b, :], k.ident16[:])
                    t.then_inc(max_turned, 1)

            def scores(h, j):
                u = h % 2
                if h == 0 and j == 0:
                    pe.wait_ge(ones_set, 1)
                if j == 0:
                    pe.wait_ge(max_copied, 2 * (h + 1))
                for at0, wide in CHUNKS:
                    to = k.bank[:, next_bank("exp"), 0:wide]
                    pe.matmul(to, keys[:, u, j * P:(j + 1) * P], queries[:, u, at0:at0 + wide], start=True, stop=False)
                    pe.matmul(to, keys_more[:, u, j * P:(j + 1) * P], queries_more[:, u, at0:at0 + wide], start=False, stop=False)
                    for b in range(wide // P):
                        m = pe.matmul(to[:, b * P:(b + 1) * P], k.mask[:, at0 // P + b, j * P:(j + 1) * P], k.ident16[:],
                                      start=False, stop=(b == wide // P - 1))
                    m.then_inc(st_done, 1)

            def values(n):
                h, j = n // NB, n % NB
                pe.wait_ge(p_ready, n + 1)
                if j == 0 and h:
                    pe.wait_ge(pv_copied, h)
                for c in range(3):
                    m = pe.matmul(k.bank[:, RING + c, 0:C3], at.val[:, j, h // 2, h % 2 * DH:(h % 2 + 2) * DH], pt[:, n % NPT, c * C3:(c + 1) * C3],
                                  start=(j == 0), stop=(j == NB - 1))
                m.then_inc(pv_done, 1)

            for item in plan:
                if item[0] == "max":
                    maximum(*item[1:])
                elif item[0] == "turn":
                    turn(item[1])
                else:
                    scores(*item[1:])
                    n = item[1] * NB + item[2]
                    if n >= 2:
                        values(n - 2)
            values(H * NB - 2)
            values(H * NB - 1)

        @block.scalar
        def _(act):
            def copy_out(h):
                act.wait_ge(pv_done, NB * (h + 1))
                if h:
                    act.wait_ge(head_done, PIECES * h)
                act.copy(raw[:].rearrange("p (c n) -> p c n", c=3), k.bank[:, RING:RING + 3, 0:C3]).then_inc(pv_copied, 1)

            for n in range(H * NB):
                if n >= NPT:
                    act.wait_ge(pv_done, n - NPT + 1)
                for c, (at0, wide) in enumerate(CHUNKS):
                    act.wait_ge(st_done, 3 * n + c + 1)
                    act.activation(pt[:, n % NPT, at0:at0 + wide], k.bank[:, bank_of["exp", n // NB, n % NB, c], 0:wide], ACT.Exp).then_inc(exp_done, 1)
                if n % NB == 1 and n > NB:
                    copy_out(n // NB - 1)
            copy_out(H - 1)

        @block.vector
        def _(dve):
            me = Steps(nc, dve, at.sem("attend_dve"))
            dve.memset(keys_more[DH:DH + 3, :, :].bitcast(F32), 1.0).then_inc(ones_set, 1)
            taken = [0]

            def maximum(h, b):
                for c, (at0, wide) in enumerate(CHUNKS):
                    n = taken[0] = taken[0] + 1
                    dve.wait_ge(scored, n)
                    if n > 2:
                        dve.wait_ge(maxed, n - 2)
                    dve.tensor_tensor_reduce(out=junk[:, n % 2, 0:wide], in0=k.bank[:, bank_of["max", h, b, c], 0:wide],
                                             in1=k.mask[:, b, at0:at0 + wide], scale=1.0, scalar=NEVER, op0=ALU.add, op1=ALU.max,
                                             accum_out=maxes[:, b, c:c + 1]).then_inc(maxed, 1)

            def negate(h):
                dve.wait_ge(maxed, 3 * NB * (h + 1))
                me.then(dve.tensor_reduce(m0[:], maxes[:], axis=AX, op=ALU.max))
                me.then(dve.tensor_scalar(m1[:], m0[:], -1.0, None, ALU.mult))
                for q in range(3):
                    last = dve.tensor_copy(parts[:, :, q], m1[:])
                    if q < 2:
                        me.then(last)
                        me.then(dve.tensor_copy(m2[:], parts[:, :, q]))
                        me.then(dve.tensor_tensor(m1[:], m1[:], m2[:], ALU.subtract))
                last.then_inc(max_ready, 1)

            def copy_maxima(h):
                for i in range(2):
                    dve.wait_ge(max_turned, 2 * h + i + 1)
                    dve.tensor_copy(queries_more[DH:DH + 3, h % 2, i * 5 * P:(i + 1) * 5 * P], k.bank[0:3, bank_of["turn", h, i], :].bitcast(BF16)[:, 0:5 * P]).then_inc(max_copied, 1)

            def finish(h, c):
                at0, at1 = c * PIECE, min((c + 1) * PIECE, W3)
                dve.wait_ge(pv_copied, h + 1)
                v0 = DH * (h % 2)
                s0 = DH - v0
                if PIECES * h + c:
                    dve.wait_ge(head_done, PIECES * h + c)
                me.then(dve.tensor_scalar(inv[v0:v0 + DH, 0:at1 - at0], raw[s0:s0 + DH, at0:at1], 1e-16, None, ALU.add))
                me.then(dve.reciprocal(inv[v0:v0 + DH, 0:at1 - at0], inv[v0:v0 + DH, 0:at1 - at0]))
                dve.tensor_tensor(at.agg[v0:v0 + DH, h // 2, at0:at1], raw[v0:v0 + DH, at0:at1], inv[v0:v0 + DH, 0:at1 - at0], ALU.mult).then_inc(head_done, 1)

            def count(n):
                dve.wait_ge(exp_done, 3 * n + 3)
                dve.tensor_tensor(pt[:, n % NPT, :], pt[:, n % NPT, :], k.ct[:, n % NB, :], ALU.mult).then_inc(p_ready, 1)

            for item in plan:
                if item[0] == "max":
                    maximum(*item[1:])
                    if item[2] == NB - 1:
                        negate(item[1])
                elif item[0] == "turn":
                    copy_maxima(item[1])
                else:
                    _, h, j = item
                    n = h * NB + j
                    if n:
                        count(n - 1)
                    if 3 <= j < 3 + PIECES and h:
                        finish(h - 1, j - 3)
            count(H * NB - 1)
            for c in range(PIECES):
                finish(H - 1, c)


def finish_layer(nc, k, a, l, at):
    S = at.sem
    w_loaded, w_turned, w_copied = [S(f"wo12_loaded{j}") for j in range(3)], S("wo12_turned"), S("wo12_copied")
    o_done, o_added, f_done, f_added, h_done, h_copied = S("o_done"), S("o_added"), S("f_done"), S("f_added"), S("h_done"), S("h_copied")
    var_ready, dev_ready, x_ready = S("bn_var_ready"), S("bn_dev_ready"), S("bn_x_ready")
    r = Region(nc, at.val_start, k.tail - 4 * KC * NP)
    rows = [r.take(f"wo12_rows{j}", [P, n, m], F32) for j, (n, m) in enumerate(((KC, D), (FF // P, D), (KC, FF)))]
    wo = r.take("wo_in", [P, KC, D], F32)
    w1 = r.take("w1_in", [P, KC, FF], F32)
    w2 = r.take("w2_in", [P, FF // P, D], F32)
    norm = Norm(nc, r, "bn", KC)
    scale, shift = r.take("bn_scale", [P, KC], F32), r.take("bn_shift", [P, KC], F32)
    hid = r.take("hidden", [P, FF // P, NP], F32)
    FP = FF // P
    turns = [(0, c, KC, wo[:, c, :]) for c in range(KC)] + [(1, c, FP, w1[:, c, :]) for c in range(KC)] + [(2, c, KC, w2[:, c, :]) for c in range(FP)]
    with nc.Block() as block:
        @block.sync
        def _(sp):
            for j, (w, n, m) in enumerate(((a.L1_gnn_Wo, KC, D), (a.L1_gnn_W1, FP, D), (a.L1_gnn_W2, KC, FF))):
                sp.dma_start(rows[j][:], w[bass.ds(l, 1), :, :].rearrange("l (o p) i -> p (l o) i", p=P)).then_inc(w_loaded[j], 16)

        @block.tensor
        def _(pe):
            for n, (j, c, o, to) in enumerate(turns):
                if c == 0:
                    pe.wait_ge(w_loaded[j], 16)
                if n >= 2:
                    pe.wait_ge(w_copied, n - 1)
                turned(pe, k, n % 2, rows[j], c, o).then_inc(w_turned, 1)
            pe.wait_ge(w_copied, len(turns))

            def product(w, x, inputs, outputs, done, free):
                for n in range(3 * outputs):
                    o, c = n // 3, WIDE[n % 3]
                    if n >= 4:
                        pe.wait_ge(free, n - 3)
                    for i in range(inputs):
                        m = pe.matmul(k.bank[:, 2 + n % 4, 0:C3], w[:, i, o * P:(o + 1) * P], x[:, i, c:c + C3],
                                      start=(i == 0), stop=(i == inputs - 1))
                    m.then_inc(done, 1)

            product(wo, at.agg, KC, KC, o_done, o_added)
            pe.wait_ge(x_ready, KC)
            product(w1, k.x1t, KC, FP, h_done, h_copied)
            pe.wait_ge(h_copied, 3 * FP)
            product(w2, hid, FP, KC, f_done, f_added)

        @block.scalar
        def _(act):
            for n, (j, c, o, to) in enumerate(turns):
                act.wait_ge(w_turned, n + 1)
                act.copy(to, k.bank[:, n % 2, 0:o * P]).then_inc(w_copied, 1)
            act.wait_ge(var_ready, 1)
            act.sqrt(norm.dev[:], norm.var[:]).then_inc(dev_ready, 1)
            for n in range(3 * FP):
                act.wait_ge(h_done, n + 1)
                c = WIDE[n % 3]
                act.activation(hid[:, n // 3, c:c + C3], k.bank[:, 2 + n % 4, 0:C3], ACT.Relu,
                               bias=at.vec[:, at.B1 + n // 3:at.B1 + n // 3 + 1]).then_inc(h_copied, 1)
            act.wait_ge(var_ready, 2)
            act.sqrt(norm.dev[:], norm.var[:]).then_inc(dev_ready, 1)

        @block.vector
        def _(dve):
            me = Steps(nc, dve, at.sem("finish_dve"))

            def add_and_norm(done, added, bias, gain, beta, turn):
                for n in range(3 * KC):
                    o, c = n // 3, WIDE[n % 3]
                    x = k.x1t[:, o, c:c + C3]
                    dve.wait_ge(done, n + 1)
                    dve.scalar_tensor_tensor(x, k.bank[:, 2 + n % 4, 0:C3], at.vec[:, bias + o:bias + o + 1], x, ALU.add, ALU.add).then_inc(added, 1)
                    if n % 3 == 2:
                        dve.wait_ge(added, n + 1)
                        norm.stats(dve, me, o, *(k.x1t[:, o, c:min(c + C3, N)] for c in WIDE))
                norm.variance(dve, me, var_ready)
                dve.wait_ge(dev_ready, turn)
                norm.invert(dve, me)
                me.then(dve.tensor_tensor(scale[:], norm.dev[:], at.vec[:, gain:gain + KC], ALU.mult))
                me.then(dve.tensor_tensor(shift[:], norm.mean_var[:, :, 0], scale[:], ALU.mult))
                me.then(dve.tensor_tensor(shift[:], at.vec[:, beta:beta + KC], shift[:], ALU.subtract))
                for o in range(KC):
                    dve.tensor_scalar(k.x1t[:, o, 0:W3], k.x1t[:, o, 0:W3], scale[:, o:o + 1], shift[:, o:o + 1], ALU.mult, ALU.add).then_inc(x_ready, 1)

            add_and_norm(o_done, o_added, at.BO, at.G1, at.BETA1, 1)
            add_and_norm(f_done, f_added, at.B2, at.G2, at.BETA2, 2)
            dve.wait_ge(x_ready, 2 * KC)


def layer1(nc, k, a):
    at = Names()
    at.sems = []

    def sem(name):
        at.sems.append(nc.alloc_semaphore(name))
        return at.sems[-1]

    at.sem = sem
    at.BO, at.G1, at.BETA1, at.B1, at.B2, at.G2, at.BETA2, at.NV = 4, 8, 12, 16, 18, 22, 26, 30
    r = Region(nc, k.shared_end, k.tail - 4 * KC * NP)
    at.agg_start = r.at
    at.agg = r.take("agg_t", [P, HP, NP], F32)
    at.vec_rows = r.take("vec_rows", [at.NV, P], F32)
    at.vec = r.take("vec", [P, at.NV], F32)
    at.bq = r.take("bq8", [P, KC], F32)
    at.val_start = r.at
    at.val = r.take("val", [P, NB, HP, 3 * DH], F32)
    at.temps = r.at
    with nc.Fori(0, LAYERS) as l:
        project(nc, k, a, l, at)
        attend(nc, k, a, l, at)
        finish_layer(nc, k, a, l, at)
        with nc.Block() as block:
            @block.gpsimd
            def _(pool):
                for s in at.sems:
                    pool.sem_clear(s)


def layer2(nc, k, a):
    S = nc.alloc_semaphore
    TILES = 2
    turned_back, z_copied, x1_loaded, rows_loaded, w_loaded, at_loaded = (
        S("l1_turned_back"), S("z_copied"), S("x1_loaded"), [S(f"rows2_loaded{j}") for j in range(4)], S("w2_loaded"), [S(f"at_loaded{u}") for u in range(TILES)])
    var_ready, dev_ready, x2_ready, x2t_done, x2t_copied = S("l2_var_ready"), S("l2_dev_ready"), S("x2_ready"), S("x2t_done"), S("x2t_copied")
    deg_ready, deg_root = S("deg_ready"), S("deg_root")
    x1b_ready, x2b_ready, h_done, h_scaled, sum_done, y_done = (
        S("x1b_ready"), S("x2b_ready"), S("l2_h_done"), S("l2_h_scaled"), S("l2_sum_done"), S("l2_y_done"))
    h_high_made, h_low_made, at_high_made, at_low_made = S("l2_h_high"), S("l2_h_low"), S("l2_at_high"), S("l2_at_low")
    x3_ready, table_ready, table_stored = S("x3_ready"), S("table_ready"), S("table_stored")
    r = Region(nc, k.x3_end, k.tail - 4 * KC * NP)
    z = r.take("z", [P, NB, D], F32)
    xt = r.take("x2t", [P, KC, NP], F32)
    h = r.take("h_scaled", [P, NB, D], F32)
    w = r.take("w_l2", [P, KC, D], F32)
    part = r.take("l2_part", [P, 2, D], F32)
    gain, shift, bias, b_edge = (r.take(n, [P, D], F32) for n in ("ln_g_row", "ln_b_row", "l2_b_row", "b_edge_row"))
    dinv, has, deg_dev = r.take("dinv", [P, NB], F32), r.take("has_deg", [P, NB], F32), r.take("deg_dev", [P, NB], F32)
    norms = [Norm(nc, r, f"norm2{j}", NB) for j in range(3)]
    last_batches = ((0, 4), (4, 6), (6, 8), (8, 9), (9, NB))
    x = k.x3
    h_low = r.take("h_low", [P, NB, D], F32R)
    r = Region(nc, k.tail, ARENA_END)
    raw, weights = r.take("at_raw", [P, TILES, NB, P], F32), r.take("at", [P, TILES, 2, NB, P], F32R)
    h_high = r.take("h_high", [P, NB, D], F32R)
    with nc.Block() as block:
        @block.sync
        def _(sp):
            sp.dma_start(x[:], k.x1_dram.rearrange("(b p) f -> p b f", p=P)).then_inc(x1_loaded, 16)
            for j, (row, v) in enumerate(((shift, a.L1_gnn_ln_b), (gain, a.L1_gnn_ln_g), (bias, a.L2_gnn_b), (b_edge, a.L3_gnn_b_edge))):
                sp.dma_start(row[:], row_of(v)).then_inc(rows_loaded[j], 16)
            sp.dma_start(w[:], a.L2_gnn_W.rearrange("(c p) n -> p c n", p=P)).then_inc(w_loaded, 16)
            for b in range(NB):
                if b >= TILES:
                    sp.wait_ge(at_low_made, b - TILES + 1)
                sp.dma_start(raw[:, b % TILES], k.at_dram[b]).then_inc(at_loaded[b % TILES], 16)
            for b in range(NB):
                sp.wait_ge(table_ready, b + 1)
                sp.dma_start(k.table_dram[b * P:(b + 1) * P, :], z[:, b, :]).then_inc(table_stored, 16)
            sp.wait_ge(table_stored, 16 * NB)

        @block.gpsimd
        def _(pool):
            pool.wait_ge(x1_loaded, 16)
            pool.wait_ge(rows_loaded[0], 16)
            for b in range(NB):
                pool.tensor_tensor(x[:, b, :], x[:, b, :], shift[:], ALU.add).then_inc(x1b_ready, 1)
            pool.wait_ge(rows_loaded[2], 16)
            for b in range(NB):
                pool.wait_ge(x2_ready, b + 1)
                pool.tensor_tensor(x[:, b, :], z[:, b, :], bias[:], ALU.add).then_inc(x2b_ready, 1)
            pool.wait_ge(rows_loaded[3], 16)
            for b in range(NB):
                pool.wait_ge(x3_ready, b + 1)
                pool.tensor_tensor(z[:, b, :], x[:, b, :], b_edge[:], ALU.add).then_inc(table_ready, 1)

        @block.tensor
        def _(pe):
            for b in range(NB):
                if b >= 4:
                    pe.wait_ge(z_copied, b - 3)
                for c in range(KC):
                    t = pe.transpose(k.bank[:, b % 4, c * P:(c + 1) * P], k.x1t[:, c, b * P:(b + 1) * P], k.ident[:])
                t.then_inc(turned_back, 1)
            pe.wait_ge(w_loaded, 16)
            for first, end in BATCHES:
                for b in range(first, end):
                    pe.wait_ge(x2_ready, b + 1)
                    if b >= 4:
                        pe.wait_ge(x2t_copied, b - 3)
                    for c in range(KC):
                        t = pe.transpose(k.bank[:, b % 4, c * P:(c + 1) * P], z[:, b, c * P:(c + 1) * P], k.ident[:])
                    t.then_inc(x2t_done, 1)
                for b in range(first, end):
                    pe.wait_ge(x2t_copied, b + 1)
                    if b >= 2:
                        pe.wait_ge(h_high_made, b - 1)
                    for c in range(KC):
                        m = pe.matmul(k.bank[:, 4 + b % 2, :], xt[:, c, b * P:(b + 1) * P], w[:, c, :], start=(c == 0), stop=(c == KC - 1))
                    m.then_inc(h_done, 1)
            pe.wait_ge(h_low_made, NB)
            for b in range(NB):
                pe.wait_ge(at_low_made, b + 1)
                if b >= 2:
                    pe.wait_ge(y_done, b - 1)
                exact(pe, k.bank[:, 6 + b % 2, :], lambda q, s: weights[:, b % TILES, q, s, :], lambda q, s: (h_high, h_low)[q][:, s, :],
                      range(NB)).then_inc(sum_done, 1)

        @block.scalar
        def _(act):
            for b in range(NB):
                act.wait_ge(turned_back, b + 1)
                act.copy(z[:, b, :], k.bank[:, b % 4, :]).then_inc(z_copied, 1)
            act.wait_ge(deg_ready, 1)
            act.sqrt(deg_dev[:], deg_dev[:]).then_inc(deg_root, 1)
            act.wait_ge(var_ready, 1)
            act.sqrt(norms[0].dev[:], norms[0].var[:]).then_inc(dev_ready, 1)

            def root(j, n):
                first, end = (BATCHES, last_batches)[j - 1][n]
                act.wait_ge(var_ready, 2 + (j - 1) * len(BATCHES) + n)
                act.sqrt(norms[j].dev[:, first:end], norms[j].var[:, first:end]).then_inc(dev_ready, 1)

            root(1, 0)
            for n, (first, end) in enumerate(BATCHES):
                for b in range(first, end):
                    act.wait_ge(x2t_done, b + 1)
                    act.copy(xt[:, :, b * P:(b + 1) * P], k.bank[:, b % 4, :].rearrange("p (c n) -> p c n", c=KC)).then_inc(x2t_copied, 1)
                if n + 1 < len(BATCHES):
                    root(1, n + 1)
                for b in range(first, end):
                    act.wait_ge(h_done, b + 1)
                    act.activation(h[:, b, :], k.bank[:, 4 + b % 2, :], ACT.Copy, scale=dinv[:, b:b + 1]).then_inc(h_scaled, 1)
                    act.activation(h_high[:, b, :], k.bank[:, 4 + b % 2, :], ACT.Copy, scale=dinv[:, b:b + 1]).then_inc(h_high_made, 1)

            def split_weights(b):
                act.wait_ge(at_loaded[b % TILES], 16 * (b // TILES + 1))
                if b >= TILES:
                    act.wait_ge(sum_done, b - TILES + 1)
                act.copy(weights[:, b % TILES, 0], raw[:, b % TILES]).then_inc(at_high_made, 1)

            for b in range(TILES):
                split_weights(b)
            for n, (first, end) in enumerate(last_batches):
                for b in range(first + TILES, min(end + TILES, NB)):
                    split_weights(b)
                root(2, n)

        @block.vector
        def _(dve):
            me = Steps(nc, dve, "layer2_dve")
            me.then(dve.tensor_scalar(deg_dev[:], k.deg[:], 1.0, None, ALU.add))
            me.then(dve.tensor_scalar(has[:], deg_dev[:], 0.0, None, ALU.is_gt))
            dve.tensor_scalar(deg_dev[:], deg_dev[:], 1e-30, None, ALU.max).then_inc(deg_ready, 1)
            for b in range(NB):
                dve.wait_ge(z_copied, b + 1)
                norms[0].stats(dve, me, b, z[:, b, :])
            norms[0].variance(dve, me, var_ready)
            dve.wait_ge(deg_root, 1)
            me.then(dve.reciprocal(dinv[:], deg_dev[:]))
            me.then(dve.tensor_tensor(dinv[:], dinv[:], has[:], ALU.mult))
            dve.wait_ge(dev_ready, 1)
            norms[0].invert(dve, me)
            dve.wait_ge(rows_loaded[1], 16)
            for n, (first, end) in enumerate(BATCHES):
                for b in range(first, end):
                    dve.wait_ge(x1b_ready, b + 1)
                    me.then(norms[0].affine(dve, me, b, z[:, b, :], gain[:], x[:, b, :]))
                    norms[1].stats(dve, me, b, z[:, b, :])
                norms[1].variance(dve, me, var_ready, first, end)
                dve.wait_ge(dev_ready, 2 + n)
                norms[1].invert(dve, me, first, end)
                for b in range(first, end):
                    norms[1].apply(dve, b, z[:, b, :]).then_inc(x2_ready, 1)
            for b in range(NB):
                dve.wait_ge(h_high_made, b + 1)
                dve.tensor_tensor(h_low[:, b, :], h[:, b, :], h_high[:, b, :].bitcast(F32), ALU.subtract).then_inc(h_low_made, 1)

            def low_weights(b):
                dve.wait_ge(at_high_made, b + 1)
                dve.tensor_tensor(weights[:, b % TILES, 1], raw[:, b % TILES], weights[:, b % TILES, 0].bitcast(F32), ALU.subtract).then_inc(at_low_made, 1)

            for b in range(TILES):
                low_weights(b)
            for n, (first, end) in enumerate(last_batches):
                for b in range(first, end):
                    dve.wait_ge(sum_done, b + 1)
                    if b + TILES < NB:
                        low_weights(b + TILES)
                    dve.wait_ge(h_scaled, b + 1)
                    dve.tensor_tensor(part[:, b % 2, :], k.bank[:, 6 + b % 2, :], h[:, b, :], ALU.add).then_inc(y_done, 1)
                    dve.wait_ge(y_done, b + 1)
                    dve.wait_ge(x2b_ready, b + 1)
                    me.then(dve.scalar_tensor_tensor(x[:, b, :], part[:, b % 2, :], dinv[:, b:b + 1], x[:, b, :], ALU.mult, ALU.add))
                    norms[2].stats(dve, me, b, x[:, b, :])
                norms[2].variance(dve, me, var_ready, first, end)
                dve.wait_ge(dev_ready, 2 + len(BATCHES) + n)
                norms[2].invert(dve, me, first, end)
                for b in range(first, end):
                    norms[2].apply(dve, b, x[:, b, :]).then_inc(x3_ready, 1)


WHOLE = (0,)
SPLIT = [j for j in range(GT) if j not in WHOLE]


def edge_messages(nc, k, a):
    S = nc.alloc_semaphore
    w_loaded, staged, got_x, got_e = S("we_loaded"), S("idx_staged"), [S(f"got_x{u}") for u in range(2)], [S(f"got_e{u}") for u in range(2)]
    passed, turned_e, e_copied, emb_done, added_x, relu_done = S("msg_pool_passed"), S("e_turned"), S("e_copied"), S("emb_done"), S("added_x"), S("relu_done")
    low_done, w_split = S("low_done"), S("we_split")
    hot_ready, summed, agg_added = S("hot_ready"), S("msgs_summed"), S("agg_added")
    r = Region(nc, k.agg_end, ARENA_END)
    idx = r.take("st_idx", [P, 2, GT], U32)
    xg = r.take("x_got", [P, 2, GT, D], F32)
    ea = r.take("edge_got", [P, 2, 2, GT, ED], F32R)
    et = r.take("edge_turned", [P, 2, 2, GT * P], F32R)
    msg = r.take("msg", [P, GT, D], F32)
    high, low = r.take("msg_high", [P, 2, len(SPLIT), D], F32R), r.take("msg_low", [P, 2, len(SPLIT), D], F32R)
    whole = r.take("msg_whole", [P, 2, len(WHOLE), D], F32)
    hot = r.take("hot_t", [P, 2, GT, P], F32R)
    we = r.take("w_edge", [ED, D], F32)
    w_high, w_low = r.take("w_edge_high", [ED, D], F32R), r.take("w_edge_low", [ED, D], F32R)
    ident_r = r.take("ident_r", [P, P], F32R)
    agg = k.agg[:].rearrange("p b f -> p (b f)")
    features = k.features_dram.rearrange("l p n -> (l p) n")
    with nc.Block() as block:
        @block.sync
        def _(sp):
            def load(i, u):
                sp.dma_start(ea[:, u].rearrange("p q j n -> p (q j n)").bitcast(F32),
                             features[bass.ds((i * 2 + u) * P, P), :]).then_inc(got_e[u], 16)

            sp.dma_start(we[:], a.L3_gnn_W_edge).then_inc(w_loaded, 16)
            load(0, 0)
            load(0, 1)
            with sp.Fori(1, NG // 2) as i:
                for u in range(2):
                    sp.wait_ge(turned_e, (i * 2 + u) * 2 - 2)
                    load(i, u)

        @block.gpsimd
        def _(pool):
            with pool.Fori(0, NG // 2) as i:
                for u in range(2):
                    g = i * 2 + u
                    gate(pool, added_x, (g + 1) * GT, passed)
                    pool.tensor_copy(idx[:, u, :], k.src_idx[:, bass.ds(g * GT, GT)]).then_inc(staged, 1)
                    gate(pool, staged, g + 1, passed)
                    for j in range(GT):
                        pool.indirect_dma_start(out=xg[:, u, j, :], out_offset=None, in_=k.table_dram,
                                                in_offset=bass.IndirectOffsetOnAxis(ap=idx[:, u, j:j + 1], axis=0)).then_inc(got_x[u], 16)

        @block.tensor
        def _(pe):
            def turn(i, u):
                pe.wait_ge(got_e[u], i * 16 + 16)
                for q in range(2):
                    for j in range(GT):
                        t = pe.matmul(k.bank[:, q, j * P:(j + 1) * P], ea[:, u, q, j, :], ident_r[:], start=True, stop=True)
                    t.then_inc(turned_e, 1)

            def embed(i, u):
                g = i * 2 + u
                pe.wait_ge(e_copied, g * 2 + 2)
                for j in range(GT):
                    pe.wait_ge(added_x, g * GT + GT + j + 1)
                    to, at = k.bank[:, 2 + j, :], slice(j * P, (j + 1) * P)
                    pe.matmul(to, et[:, u, 0, at], w_high[:], start=True, stop=False)
                    pe.matmul(to, et[:, u, 0, at], w_low[:], start=False, stop=False)
                    pe.matmul(to, et[:, u, 1, at], w_high[:], start=False, stop=True).then_inc(emb_done, 1)

            def collect(i, u):
                g = i * 2 + u
                pe.wait_ge(hot_ready, g + 1)
                pe.wait_ge(agg_added, g + 1)
                for j in range(GT):
                    if j in WHOLE:
                        pe.wait_ge(relu_done, g * GT + j + 1)
                        m = pe.matmul(k.bank[:, 6 + u, :], hot[:, u, j, :].bitcast(F32), whole[:, u, WHOLE.index(j), :], start=(j == 0), stop=(j == GT - 1))
                    else:
                        pe.wait_ge(low_done, g * len(SPLIT) + SPLIT.index(j) + 1)
                        pe.matmul(k.bank[:, 6 + u, :], hot[:, u, j, :], high[:, u, SPLIT.index(j), :], start=(j == 0), stop=False)
                        m = pe.matmul(k.bank[:, 6 + u, :], hot[:, u, j, :], low[:, u, SPLIT.index(j), :], start=False, stop=(j == GT - 1))
                m.then_inc(summed, 1)

            pe.wait_ge(w_split, 3)
            turn(0, 0)
            embed(0, 0)
            turn(0, 1)
            with pe.Fori(0, NG // 2 - 1) as i:
                embed(i, 1)
                turn(i + 1, 0)
                collect(i, 0)
                embed(i + 1, 0)
                turn(i + 1, 1)
                collect(i, 1)
            embed(NG // 2 - 1, 1)
            collect(NG // 2 - 1, 0)
            collect(NG // 2 - 1, 1)

        @block.scalar
        def _(act):
            def copy_turned(i, u, first=False):
                g = i * 2 + u
                if not first:
                    act.wait_ge(emb_done, (g - 1) * GT)
                for q in range(2):
                    act.wait_ge(turned_e, g * 2 + q + 1)
                    act.copy(et[:, u, q, :], k.bank[:, q, :]).then_inc(e_copied, 1)

            def relu(i, u, first=False):
                g = i * 2 + u
                if not first:
                    act.wait_ge(summed, g - 1)
                for j in range(GT):
                    act.wait_ge(added_x, g * GT + 2 * GT + j + 1)
                    to = whole[:, u, WHOLE.index(j), :] if j in WHOLE else high[:, u, SPLIT.index(j), :]
                    act.activation(to, msg[:, j, :], ACT.Relu).then_inc(relu_done, 1)

            copy_turned(0, 0, True)
            copy_turned(0, 1, True)
            relu(0, 0, True)
            copy_turned(1, 0)
            relu(0, 1, True)
            copy_turned(1, 1)
            with act.Fori(1, NG // 2 - 1) as i:
                relu(i, 0)
                copy_turned(i + 1, 0)
                relu(i, 1)
                copy_turned(i + 1, 1)
            relu(NG // 2 - 1, 0)
            relu(NG // 2 - 1, 1)

        @block.vector
        def _(dve):
            def lower(g, u, j):
                if j in WHOLE:
                    return
                dve.wait_ge(relu_done, g * GT + j + 1)
                dve.scalar_tensor_tensor(low[:, u, SPLIT.index(j), :], msg[:, j, :], 0.0, high[:, u, SPLIT.index(j), :].bitcast(F32), ALU.max, ALU.subtract).then_inc(low_done, 1)

            def add_x(i, u, first=False):
                g = i * 2 + u
                dve.wait_ge(got_x[u], i * (16 * GT) + 16 * GT)
                for j in range(GT):
                    dve.wait_ge(emb_done, g * GT + j + 1)
                    if not first and j in WHOLE:
                        dve.wait_ge(relu_done, g * GT - GT + j + 1)
                    elif not first:
                        dve.wait_ge(low_done, g * len(SPLIT) - len(SPLIT) + SPLIT.index(j) + 1)
                    dve.tensor_tensor(msg[:, j, :], k.bank[:, 2 + j, :], xg[:, u, j, :], ALU.add).then_inc(added_x, 1)
                    if j >= 2:
                        lower(g, u, j - 2)
                    elif not first:
                        lower(g - 1, 1 - u, j + 2)

            def one_hot(i, u):
                for j in range(GT):
                    last = dve.tensor_scalar(hot[:, u, j, :], k.row128f[:], k.slot_dst[:, bass.ds((i * 2 + u) * GT + j, 1)], None, ALU.is_equal)
                last.then_inc(hot_ready, 1)

            def add_sum(i, u):
                g = i * 2 + u
                to = dve.value_load(k.blk[0:1, bass.ds(g, 1)], min_val=0, max_val=NB - 1) * D
                dve.wait_ge(summed, g + 1)
                dve.wait_ge(agg_added, g + 2)
                rows = agg[:, bass.ds(to, D)]
                dve.tensor_tensor(rows, k.bank[:, 6 + u, :], rows, ALU.add).then_inc(agg_added, 1)

            dve.sem_inc(added_x, 2 * GT)
            dve.memset(agg, 0.0).then_inc(agg_added, 2)
            dve.tensor_copy(ident_r[:], k.ident[:]).then_inc(w_split, 1)
            dve.wait_ge(w_loaded, 16)
            dve.tensor_copy(w_high[:], we[:]).then_inc(w_split, 1)
            dve.wait_ge(w_split, 2)
            dve.tensor_tensor(w_low[:], we[:], w_high[:].bitcast(F32), ALU.subtract).then_inc(w_split, 1)
            one_hot(0, 0)
            add_x(0, 0, True)
            one_hot(0, 1)
            add_x(0, 1)
            with dve.Fori(0, NG // 2 - 1) as i:
                add_sum(i, 0)
                one_hot(i + 1, 0)
                add_x(i + 1, 0)
                add_sum(i, 1)
                one_hot(i + 1, 1)
                add_x(i + 1, 1)
            lower(NG - 1, 1, GT - 2)
            lower(NG - 1, 1, GT - 1)
            add_sum(NG // 2 - 1, 0)
            add_sum(NG // 2 - 1, 1)




def widen(nc, k, a):
    S = nc.alloc_semaphore
    eps_loaded, bias_loaded, vec_loaded = S("eps_loaded"), S("bias31_loaded"), S("vec31_loaded")
    w_loaded, w_high, w_low = [S(f"w31_loaded{c}") for c in range(KC)], S("w31_high"), S("w31_low")
    h_ready, h_turned, h_high, h_low = S("h3_ready"), S("h3_turned"), S("h3_high"), S("h3_low")
    vec_turned, vec_copied, wide_done, wide_added = S("vec31_turned"), S("vec31_copied"), S("wide_done"), S("wide_added")
    var_ready, dev_ready, scaled, turned_z, gelu_high, gelu_low = (
        S("wide_var_ready"), S("wide_dev_ready"), S("wide_scaled"), S("wide_turned"), S("wide_gelu_high"), S("wide_gelu_low"))
    r = Region(nc, k.wide_end, ARENA_END)
    wide = r.take("wide", [P, NB, D2], F32)
    w = r.take("w31", [P, 2, KC, D2], F32R)
    bias = r.take("b31_row", [P, D2], F32)
    vec_rows, vec = r.take("vec31_rows", [4 * KC, P], F32), r.take("vec31", [P, 4 * KC], F32)
    one_eps = r.take("one_eps", [P, 1], F32)
    norm = Norm(nc, r, "norm31", NB)
    raw = Region(nc, k.wide_end, ARENA_END).take("w31_raw", [P, KC, D2], F32)
    gelu = Region(nc, k.x3_end, k.agg_end).take("gelu31", [P, 2, 512], F32)
    h = k.agg
    plan = [("product", b) for b in range(NB)]
    for n, (_, end) in enumerate(BATCHES):
        for half in range(2):
            at = min(end + 1 + half, NB) + 2 * KC * n + KC * half
            plan[at:at] = [("turn", n, c) for c in range(KC * half, KC * half + KC)]
    turns = [item[1:] for item in plan if item[0] == "turn"]
    with nc.Block() as block:
        @block.sync
        def _(sp):
            sp.dma_start(one_eps[:], row_of(a.L3_gnn_eps)).then_inc(eps_loaded, 16)
            for j, v in enumerate((a.L3_gnn_g1, a.L3_gnn_be1)):
                sp.dma_start(vec_rows[2 * KC * j:2 * KC * (j + 1), :], v.rearrange("(c p) -> c p", p=P)).then_inc(vec_loaded, 16)
            for c in range(KC):
                sp.dma_start(raw[:, c, :], a.L3_gnn_W1[c * P:(c + 1) * P, :]).then_inc(w_loaded[c], 16)
            sp.dma_start(bias[:], row_of(a.L3_gnn_b1)).then_inc(bias_loaded, 16)

        @block.gpsimd
        def _(pool):
            for c in range(KC):
                pool.wait_ge(w_high, c + 1)
                pool.tensor_tensor(w[:, 1, c, :], raw[:, c, :], w[:, 0, c, :].bitcast(F32), ALU.subtract).then_inc(w_low, 1)

        @block.tensor
        def _(pe):
            for b in range(NB):
                pe.wait_ge(h_ready, b + 1)
                if b >= 4:
                    pe.wait_ge(h_low, b - 3)
                for c in range(KC):
                    t = pe.transpose(k.bank[:, b % 4, c * P:(c + 1) * P], h[:, b, c * P:(c + 1) * P], k.ident[:])
                t.then_inc(h_turned, 1)
            pe.wait_ge(vec_loaded, 32)
            pe.transpose(k.bank[:, 7, 0:4 * KC], vec_rows[:], k.ident[0:4 * KC, 0:4 * KC]).then_inc(vec_turned, 1)
            pe.wait_ge(h_low, NB)
            pe.wait_ge(vec_copied, 1)

            def weights_arrive(c):
                pe.wait_ge(w_low, c + 1)

            n = 0
            for item in plan:
                if item[0] == "product":
                    b = item[1]
                    if b >= 2:
                        pe.wait_ge(wide_added, b - 1)
                    for o in range(2):
                        m = exact(pe, k.bank[:, 4 + 2 * (b % 2) + o, :], lambda q, c: k.wide_t[:, b, q, c, :],
                                  lambda q, c: w[:, q, c, o * D:(o + 1) * D], range(KC), weights_arrive if b == 0 else None)
                    m.then_inc(wide_done, 1)
                else:
                    first, end = BATCHES[item[1]]
                    pe.wait_ge(scaled, end)
                    if n >= 4:
                        pe.wait_ge(gelu_high, n - 3)
                    for b in range(first, end):
                        t = pe.transpose(k.bank[:, n % 4, (b - first) * P:(b - first + 1) * P], wide[:, b, item[2] * P:(item[2] + 1) * P], k.ident[:])
                    t.then_inc(turned_z, 1)
                    n += 1

        @block.scalar
        def _(act):
            for b in range(NB):
                if 4 <= b < 4 + KC:
                    act.wait_ge(w_loaded[b - 4], 16)
                    act.copy(w[:, 0, b - 4, :], raw[:, b - 4, :]).then_inc(w_high, 1)
                act.wait_ge(h_turned, b + 1)
                act.copy(k.wide_t[:, b, 0, 0:KC, :], k.bank[:, b % 4, :].rearrange("p (c n) -> p c n", c=KC)).then_inc(h_high, 1)
            for n, (batch, c) in enumerate(turns):
                first, end = BATCHES[batch]
                if c == 0:
                    act.wait_ge(var_ready, batch + 1)
                    act.sqrt(norm.dev[:, first:end], norm.var[:, first:end]).then_inc(dev_ready, 1)
                act.wait_ge(turned_z, n + 1)
                if n >= 2:
                    act.wait_ge(gelu_low, n - 1)
                wide_of = (end - first) * P
                act.activation(gelu[:, n % 2, 0:wide_of], k.bank[:, n % 4, 0:wide_of], ACT.Gelu, bias=vec[:, 2 * KC + c:2 * KC + c + 1], scale=vec[:, c:c + 1])
                act.activation(k.wide_t[:, first:end, 0, c, :], k.bank[:, n % 4, 0:wide_of].rearrange("p (b n) -> p b n", n=P), ACT.Gelu,
                               bias=vec[:, 2 * KC + c:2 * KC + c + 1], scale=vec[:, c:c + 1]).then_inc(gelu_high, 1)

        @block.vector
        def _(dve):
            me = Steps(nc, dve, "widen_dve")
            dve.wait_ge(eps_loaded, 16)
            me.then(dve.tensor_scalar(one_eps[:], one_eps[:], 1.0, None, ALU.add))
            for b in range(NB + 1):
                if b < NB:
                    dve.scalar_tensor_tensor(h[:, b, :], k.x3[:, b, :], one_eps[:], h[:, b, :], ALU.mult, ALU.add).then_inc(h_ready, 1)
                if b:
                    dve.wait_ge(h_high, b)
                    dve.tensor_tensor(k.wide_t[:, b - 1, 1, 0:KC, :], k.bank[:, (b - 1) % 4, :].rearrange("p (c n) -> p c n", c=KC),
                                      k.wide_t[:, b - 1, 0, 0:KC, :].bitcast(F32), ALU.subtract).then_inc(h_low, 1)
            dve.wait_ge(vec_turned, 1)
            dve.tensor_copy(vec[:], k.bank[:, 7, 0:4 * KC]).then_inc(vec_copied, 1)
            dve.wait_ge(bias_loaded, 16)

            def lower(n):
                batch, c = turns[n]
                first, end = BATCHES[batch]
                dve.wait_ge(gelu_high, n + 1)
                dve.tensor_tensor(k.wide_t[:, first:end, 1, c, :], gelu[:, n % 2, 0:(end - first) * P].rearrange("p (b n) -> p b n", n=P),
                                  k.wide_t[:, first:end, 0, c, :].bitcast(F32), ALU.subtract).then_inc(gelu_low, 1)

            def normalise(batch):
                first, end = BATCHES[batch]
                dve.wait_ge(dev_ready, batch + 1)
                norm.invert(dve, me, first, end)
                for j in range(first, end):
                    norm.apply(dve, j, wide[:, j, :]).then_inc(scaled, 1)

            n, batch = 0, 0
            for item in plan:
                if item[0] == "turn":
                    lower(n)
                    n += 1
                    if n == 2 * KC * batch and batch == len(BATCHES) - 1:
                        normalise(batch)
                    continue
                b = item[1]
                dve.wait_ge(wide_done, b + 1)
                dve.tensor_tensor(wide[:, b, :].rearrange("p (o n) -> p o n", o=2), k.bank[:, 4 + 2 * (b % 2):6 + 2 * (b % 2), :],
                                  bias[:].rearrange("p (o n) -> p o n", o=2), ALU.add).then_inc(wide_added, 1)
                dve.wait_ge(wide_added, b + 1)
                norm.stats(dve, me, b, wide[:, b, 0:D], wide[:, b, D:D2])
                first, end = BATCHES[batch]
                if b == end - 1:
                    norm.variance(dve, me, var_ready, first, end)
                    if batch < len(BATCHES) - 1:
                        normalise(batch)
                        batch += 1


def narrow(nc, k, a, second, out):
    S, which = nc.alloc_semaphore, "ab"[second]
    w_loaded, w_high, w_low = [S(f"w32_loaded{j}" + which) for j in range(KC)], S("w32_high" + which), S("w32_low" + which)
    rows_loaded, done, added = S("rows32_loaded" + which), S("narrow_done" + which), S("narrow_added" + which)
    var_ready, dev_ready, scaled, gelu_done = S("n_var_ready" + which), S("n_dev_ready" + which), S("n_scaled" + which), S("n_gelu" + which)
    result, stored, x3_added = S("n_result" + which), S("out_stored" + which), S("n_x3_added" + which)
    r = Region(nc, k.wide_end, ARENA_END)
    y = r.take("y32" + which, [P, NB, D], F32)
    w = r.take("w32" + which, [P, 2, 2 * KC, D], F32R)
    rows = [r.take(f"row32{which}{j}", [P, D], F32) for j in range(5)]
    norms = [Norm(nc, r, f"norm32{which}{j}", NB) for j in range(2)]
    batches = ((0, 2), (2, 4), (4, 6), (6, 8), (8, 9), (9, NB)) if second else ((0, 3), (3, 6), (6, 8), (8, 9), (9, NB))
    steps = [(0, 0)]
    for n in range(1, len(batches)):
        steps += [(0, n), (1, n - 1)]
    steps.append((1, len(batches) - 1))
    raw = Region(nc, k.wide_end, ARENA_END).take("w32_raw" + which, [P, 2 * KC, D], F32)
    if second:
        matrix, vectors = a.L3_gnn_M2, (a.L3_gnn_gB, a.L3_gnn_bB)
    else:
        matrix, vectors = a.L3_gnn_W2, (a.L3_gnn_b2, a.L3_gnn_g2, a.L3_gnn_be2, a.L3_gnn_gA, a.L3_gnn_bA)
    with nc.Block() as block:
        @block.sync
        def _(sp):
            for j in range(KC):
                sp.dma_start(raw[:, 2 * j:2 * j + 2, :], matrix[2 * j * P:2 * (j + 1) * P, :].rearrange("(c p) n -> p c n", p=P)).then_inc(w_loaded[j], 16)
            for row, v in zip(rows, vectors):
                sp.dma_start(row[:], row_of(v)).then_inc(rows_loaded, 16)
            if second:
                for b in range(NB):
                    sp.wait_ge(result, b + 1)
                    n = last_rows(b)
                    sp.dma_start(out[b * P:b * P + n, :], y[0:n, b, :]).then_inc(stored, 16)
                sp.wait_ge(stored, 16 * NB)

        @block.gpsimd
        def _(pool):
            if second:
                pool.wait_ge(rows_loaded, 16 * len(vectors))
            for b in range(NB):
                if second:
                    pool.tensor_tensor(k.x3[:, b, :], k.x3[:, b, :], rows[1][:], ALU.add).then_inc(x3_added, 1)
                else:
                    pool.wait_ge(gelu_done, b + 1)
                    pool.tensor_tensor(y[:, b, :], y[:, b, :], k.x3[:, b, :], ALU.add).then_inc(x3_added, 1)

        @block.tensor
        def _(pe):
            def weights_arrive(c):
                pe.wait_ge(w_low, c // 2 + 1)

            for b in range(NB):
                if b >= 8:
                    pe.wait_ge(added, b - 7)
                exact(pe, k.bank[:, b % 8, :], lambda q, c: k.wide_t[:, b, q, c, :], lambda q, c: w[:, q, c, :], range(2 * KC),
                      weights_arrive if b == 0 else None).then_inc(done, 1)

        @block.scalar
        def _(act):
            for j in range(KC):
                act.wait_ge(w_loaded[j], 16)
                act.copy(w[:, 0, 2 * j:2 * j + 2, :], raw[:, 2 * j:2 * j + 2, :]).then_inc(w_high, 1)
            for step, (j, n) in enumerate(steps):
                first, end = batches[n]
                act.wait_ge(var_ready, step + 1)
                act.sqrt(norms[j].dev[:, first:end], norms[j].var[:, first:end]).then_inc(dev_ready, 1)
                if j == 0 and not second:
                    for b in range(first, end):
                        act.wait_ge(scaled, b + 1)
                        act.activation(y[:, b, :], y[:, b, :], ACT.Gelu).then_inc(gelu_done, 1)

        @block.vector
        def _(dve):
            me = Steps(nc, dve, "narrow_dve" + which)
            for j in range(KC):
                dve.wait_ge(w_high, j + 1)
                dve.tensor_tensor(w[:, 1, 2 * j:2 * j + 2, :], raw[:, 2 * j:2 * j + 2, :], w[:, 0, 2 * j:2 * j + 2, :].bitcast(F32), ALU.subtract).then_inc(w_low, 1)
            dve.wait_ge(rows_loaded, 16 * len(vectors))
            gain = rows[0] if second else rows[1]

            def first_norm(first, end, step):
                for b in range(first, end):
                    dve.wait_ge(done, b + 1)
                    other = k.agg[:, b, :] if second else rows[0][:]
                    dve.tensor_tensor(y[:, b, :], k.bank[:, b % 8, :], other, ALU.add).then_inc(added, 1)
                    dve.wait_ge(added, b + 1)
                    norms[0].stats(dve, me, b, y[:, b, :])
                norms[0].variance(dve, me, var_ready, first, end)
                dve.wait_ge(dev_ready, step + 1)
                norms[0].invert(dve, me, first, end)
                for b in range(first, end):
                    if second:
                        dve.wait_ge(x3_added, b + 1)
                    shift = k.x3[:, b, :] if second else rows[2][:]
                    norms[0].affine(dve, me, b, y[:, b, :], gain[:], shift).then_inc(scaled, 1)

            def second_norm(first, end, step):
                for b in range(first, end):
                    if second:
                        dve.wait_ge(scaled, b + 1)
                    else:
                        dve.wait_ge(x3_added, b + 1)
                    norms[1].stats(dve, me, b, y[:, b, :])
                norms[1].variance(dve, me, var_ready, first, end)
                dve.wait_ge(dev_ready, step + 1)
                norms[1].invert(dve, me, first, end)
                for b in range(first, end):
                    if second:
                        norms[1].apply(dve, b, y[:, b, :]).then_inc(result, 1)
                    else:
                        me.then(dve.scalar_tensor_tensor(k.agg[:, b, :], y[:, b, :], norms[1].mean_var[:, b, 0:1], rows[3][:], ALU.subtract, ALU.mult))
                        dve.scalar_tensor_tensor(k.agg[:, b, :], k.agg[:, b, :], norms[1].dev[:, b:b + 1], rows[4][:], ALU.mult, ALU.add).then_inc(result, 1)

            for step, (j, n) in enumerate(steps):
                (first_norm, second_norm)[j](*batches[n], step)
            dve.wait_ge(result, NB)


def widen_again(nc, k, a):
    S = nc.alloc_semaphore
    w_loaded, w_high, w_low = [S(f"m1_loaded{c}") for c in range(KC)], S("m1_high"), S("m1_low")
    h_turned, h_high, h_low, done, gelu_high, gelu_low = S("ha_turned"), S("ha_high"), S("ha_low"), S("m_done"), S("m_gelu_high"), S("m_gelu_low")
    r = Region(nc, k.wide_end, ARENA_END)
    ht = r.take("ha_t", [P, NB, 2, KC, P], F32R)
    w = r.take("m1_w", [P, 2, KC, D2], F32R)
    gelu = r.take("m_gelu", [P, 2, 512], F32)
    raw_at = k.wide_end + 4 * 2 * KC * P * (NB - 4)
    raw = Region(nc, raw_at, ARENA_END).take("m1_raw", [P, KC, D2], F32)
    pieces = [(batch, o) for batch in range(len(BATCHES)) for o in range(2 * KC)]
    with nc.Block() as block:
        @block.sync
        def _(sp):
            for c in range(KC):
                sp.dma_start(raw[:, c, :], a.L3_gnn_M1[c * P:(c + 1) * P, :]).then_inc(w_loaded[c], 16)

        @block.tensor
        def _(pe):
            def turn(b):
                if b >= 2:
                    pe.wait_ge(h_low, b - 1)
                for c in range(KC):
                    t = pe.transpose(k.bank[:, b % 2, c * P:(c + 1) * P], k.agg[:, b, c * P:(c + 1) * P], k.ident[:])
                t.then_inc(h_turned, 1)

            for b in range(NB - 4):
                turn(b)

            def weights_arrive(c):
                pe.wait_ge(w_low, c + 1)

            for n, (batch, o) in enumerate(pieces):
                first, end = BATCHES[batch]
                if (batch, o) == (0, 1):
                    for b in range(NB - 4, NB):
                        turn(b)
                pe.wait_ge(h_low, end)
                if n >= 6:
                    pe.wait_ge(gelu_high, n - 5)
                exact(pe, k.bank[:, 2 + n % 6, 0:(end - first) * P], lambda q, c: w[:, q, c, o * P:(o + 1) * P],
                      lambda q, c: ht[:, first:end, q, c, :], range(KC), weights_arrive if n == 0 else None).then_inc(done, 1)

        @block.scalar
        def _(act):
            def high_part(b):
                act.wait_ge(h_turned, b + 1)
                act.copy(ht[:, b, 0, :, :], k.bank[:, b % 2, :].rearrange("p (c n) -> p c n", c=KC)).then_inc(h_high, 1)

            for b in range(NB - 4):
                high_part(b)
            for c in range(KC):
                act.wait_ge(w_loaded[c], 16)
                act.copy(w[:, 0, c, :], raw[:, c, :]).then_inc(w_high, 1)
            act.wait_ge(w_low, KC)
            for b in range(NB - 4, NB):
                high_part(b)
            for n, (batch, o) in enumerate(pieces):
                first, end = BATCHES[batch]
                act.wait_ge(done, n + 1)
                if n >= 2:
                    act.wait_ge(gelu_low, n - 1)
                from_bank = k.bank[:, 2 + n % 6, 0:(end - first) * P]
                act.activation(gelu[:, n % 2, 0:(end - first) * P], from_bank, ACT.Gelu)
                act.activation(k.wide_t[:, first:end, 0, o, :], from_bank.rearrange("p (b n) -> p b n", n=P), ACT.Gelu).then_inc(gelu_high, 1)

        @block.vector
        def _(dve):
            def low_part(b):
                dve.wait_ge(h_high, b + 1)
                dve.tensor_tensor(ht[:, b, 1, :, :], k.bank[:, b % 2, :].rearrange("p (c n) -> p c n", c=KC), ht[:, b, 0, :, :].bitcast(F32),
                                  ALU.subtract).then_inc(h_low, 1)

            for b in range(NB - 4):
                low_part(b)
            for c in range(KC):
                dve.wait_ge(w_high, c + 1)
                dve.tensor_tensor(w[:, 1, c, :], raw[:, c, :], w[:, 0, c, :].bitcast(F32), ALU.subtract).then_inc(w_low, 1)
            for b in range(NB - 4, NB):
                low_part(b)
            for n, (batch, o) in enumerate(pieces):
                first, end = BATCHES[batch]
                dve.wait_ge(gelu_high, n + 1)
                dve.tensor_tensor(k.wide_t[:, first:end, 1, o, :], gelu[:, n % 2, 0:(end - first) * P].rearrange("p (b n) -> p b n", n=P),
                                  k.wide_t[:, first:end, 0, o, :].bitcast(F32), ALU.subtract).then_inc(gelu_low, 1)
            dve.wait_ge(gelu_low, len(pieces))


class Names:
    pass


def program(nc, a, out):
    k = Names()
    k.slots_dram = nc.dram_tensor("slots_dram", (P * NT, REC), F32).ap()
    k.slots3_dram = nc.dram_tensor("slots3_dram", (P * NT3, REC), F32).ap()
    k.at_dram = nc.dram_tensor("at_dram", (NB, P, NB, P), F32).ap()
    k.table_dram = nc.dram_tensor("table_dram", (NP, D), F32).ap()
    k.qk_dram = nc.dram_tensor("qk_dram", (4, HP, P, NP), F32).ap()
    k.features_dram = nc.dram_tensor("features_dram", (LAYERS, NG // LAYERS * P, 2 * GT * ED), F32).ap()
    k.x1_dram = nc.dram_tensor("x1_dram", (NP, D), F32).ap()
    k.bank = nc.alloc_psum_tensor("bank", [P, 8, 512], F32)
    r = Region(nc, ARENA, ARENA_END)
    k.ident = r.take("ident", [P, P], F32)
    k.before = r.take("before", [P, P], F32)
    k.ones = r.take("ones", [P, P], F32)
    k.node_row = r.take("node_row", [P, NP], F16)
    k.row128 = r.take("row128", [P, P], F16)
    k.row128f = r.take("row128f", [P, P], F32)
    k.groups_row = r.take("groups_row", [P, NG3], F32)
    k.blk = r.take("blk", [1, NG], I32)
    k.slot_dst = r.take("slot_dst", [P, NT], F32)
    k.src_idx = r.take("src_idx", [P, NT], U32)
    k.id_idx = r.take("id_idx", [P, NT], U32)
    k.ident16 = r.take("ident16", [P, P], BF16)
    k.pad_rows = r.take("pad_rows", [P, 1], F32)
    k.counts = r.take("counts", [P, NB], F32)
    k.deg = r.take("deg", [P, NB], F32)
    k.shared_end = r.at
    k.alpha = r.take("alpha", [P, NB, D], F32)
    k.beta = r.take("beta", [P, NB, D], F32)
    k.rec, k.pos = r.take("rec", [P, EC, REC], F32), r.take("pos", [P, EC], U32)
    k.slot3_src, k.slot3_dst = r.take("slot3_src", [P, NT3], F32), r.take("slot3_dst", [P, NT3], F32)
    k.slot_w = r.take("slot_w", [P, 4, NT3], F32)
    k.place3, k.blk_f = r.take("place3", [1, NG3], I32), r.take("blk_f", [1, NG], F32)
    k.prefilled1 = nc.alloc_semaphore("slots1_prefilled")
    k.beta_end = r.at
    k.acc_c = r.take("acc_c", [P, NB, NP], F32)
    k.acc_a = r.take("acc_a", [P, NB, NP], F32)
    k.acc_end = r.at
    k.tail = ARENA_END - 2 * 2 * NB * NP
    r = Region(nc, k.tail, ARENA_END)
    k.ct = r.take("ct", [P, NB, NP], U16)
    k.mask = r.take("mask", [P, NB, NP], BF16)
    k.x1t = nc.alloc_sbuf_tensor_at("x1t", [P, KC, NP], F32, offset=k.tail - 4 * KC * NP)
    constants(nc, k)
    used = nc.snapshot_sems()
    sort_edges(nc, k, a)
    edge_matrices(nc, k)
    transpose_weights_of_edges(nc, k)
    layer0(nc, k)
    layer1(nc, k, a)
    nc.clear_and_free_semaphores(nc.allocated_since(used))
    nc.all_engine_barrier()
    r = Region(nc, k.shared_end, ARENA_END)
    k.x3 = r.take("x3", [P, NB, D], F32)
    k.x3_end = r.at
    layer2(nc, k, a)
    k.agg = r.take("agg", [P, NB, D], F32)
    k.agg_end = r.at
    edge_messages(nc, k, a)
    k.wide_t = r.take("wide_t", [P, NB, 2, 2 * KC, P], F32R)
    k.wide_end = r.at
    widen(nc, k, a)
    narrow(nc, k, a, False, None)
    widen_again(nc, k, a)
    narrow(nc, k, a, True, out)
    return k


_INS = ["x", "src", "dst", "edge_attr_128", "edge_weight", "L0_gnn_wc", "L0_gnn_wn", "L0_gnn_bias",
        "L1_gnn_Wq", "L1_gnn_bq", "L1_gnn_Wk", "L1_gnn_Wv", "L1_gnn_Wo", "L1_gnn_bo", "L1_gnn_W1", "L1_gnn_b1",
        "L1_gnn_W2", "L1_gnn_b2", "L1_gnn_g1", "L1_gnn_beta1", "L1_gnn_g2", "L1_gnn_beta2", "L1_gnn_ln_g", "L1_gnn_ln_b",
        "L2_gnn_W", "L2_gnn_b", "L3_gnn_W_edge", "L3_gnn_b_edge", "L3_gnn_eps", "L3_gnn_W1", "L3_gnn_b1", "L3_gnn_g1",
        "L3_gnn_be1", "L3_gnn_W2", "L3_gnn_b2", "L3_gnn_g2", "L3_gnn_be2", "L3_gnn_gA", "L3_gnn_bA", "L3_gnn_M1", "L3_gnn_M2",
        "L3_gnn_gB", "L3_gnn_bB"]


def kernel(**inputs):
    import numpy as np
    import concourse.bacc as bacc
    from concourse.bass_utils import run_bass_kernel_spmd

    nc = bacc.Bacc("TRN2", target_bir_lowering=False, num_devices=1)
    arrays, a = {}, Names()
    for name in _INS:
        array = np.ascontiguousarray(inputs[name])
        array = array.reshape(array.shape or (1,))
        arrays[f"in_{name}"] = array
        a.__dict__[name] = nc.dram_tensor(f"in_{name}", array.shape, mybir.dt.from_np(array.dtype), kind="ExternalInput").ap()
    out = nc.dram_tensor("out_0", (N, D), F32, kind="ExternalOutput").ap()
    program(nc, a, out)
    return run_bass_kernel_spmd(nc, [arrays], core_ids=[0]).results[0]["out_0"]
```
